# Optimizing a Trainium2 kernel written in Bass

```python
import numpy as np
import jax
import jax.numpy as jnp

def _softmax(x, axis=-1):
    return jax.nn.softmax(x, axis=axis)

def _gelu(x):
    return jax.nn.gelu(x, approximate=True)

def _silu(x):
    return jax.nn.silu(x)

def _sigmoid(x):
    return jax.nn.sigmoid(x)

def _layernorm(x, axis=-1, eps=1e-05):
    m = jnp.mean(x, axis=axis, keepdims=True)
    v = jnp.var(x, axis=axis, keepdims=True)
    return (x - m) / jnp.sqrt(v + eps)

def _scatter_add(tgt, idx, src, axis=0):
    return tgt.at[idx].add(src)

def _segment_sum(src, seg, n):
    return jax.ops.segment_sum(src, seg, n)
kernel_name = 'mk_audio_tower_d1_tok_audfeat768_r4_1c65d1'

def setup_inputs(seed: int=0):
    np.random.seed(seed)
    _w = jnp.asarray

    def _rec_inputs():
        import jax
        import jax.numpy as jnp
        _rk = jax.random.key(seed)
        x = -0.000183583 + 0.999963 * jax.random.normal(jax.random.fold_in(_rk, 1), (8, 750, 192), jnp.float32)
        return x
    x = _rec_inputs()

    def _L0_tok_setup():
        import jax, jax.numpy as jnp
        import numpy as np
        KEEP_RATIO = 0.7
        key = jax.random.key(seed)
        kx, kw = jax.random.split(key)
        B, N, D = (32, 1024, 192)
        x = jax.random.normal(kx, (B, N, D), dtype=jnp.float32)
        w = jax.random.normal(kw, (D, 1), dtype=jnp.float32) * (1.0 / np.sqrt(D))
        b = jnp.zeros((1,), dtype=jnp.float32)
        return {'x': x, 'w': w, 'b': b}
    _L0_tok_all = _L0_tok_setup()
    _L0_tok_in = {k: v for k, v in _L0_tok_all.items() if k in ('w', 'b')}
    del _L0_tok_all

    def _L0_attn_setup():
        import jax, jax.numpy as jnp
        import numpy as np
        NH = 12
        LEVEL = 4

        def _build_sets(T, Lmin):
            l_list, r_list = ([], [])
            L = Lmin
            while L <= T:
                for i in range(T // L):
                    l_list.append(i * L)
                    r_list.append((i + 1) * L - 1)
                L *= 2
            return (np.asarray(l_list, np.int32), np.asarray(r_list, np.int32))

        def _get_slice(x_cum, l_idx, r_idx):
            r = x_cum[:, :, r_idx, :]
            l = x_cum[:, :, np.maximum(np.asarray(l_idx) - 1, 0), :]
            mask = (np.asarray(l_idx) >= 1).astype(x_cum.dtype)[None, None, :, None]
            return r - l * mask

        def _get_slice_dyn(x_cum, l_idx, r_idx):
            r = x_cum[:, :, r_idx, :]
            l = x_cum[:, :, jnp.maximum(l_idx - 1, 0), :]
            mask = (l_idx >= 1).astype(x_cum.dtype)[None, None, :, None]
            return r - l * mask
        key = jax.random.key(seed)
        k0, k1, k2, k3 = jax.random.split(key, 4)
        B, T, C = (8, 512, 192)
        hs = C // NH
        s = 0.02
        return {'x': jax.random.normal(k0, (B, T, C), jnp.float32), 'Wqkv': jax.random.normal(k1, (3 * C, C), jnp.float32) * s, 'Wproj': jax.random.normal(k2, (C, C), jnp.float32) * s, 'Wv': jax.random.normal(k3, (hs, hs * hs), jnp.float32) * s, 'bv': jnp.zeros((hs,), jnp.float32)}
    _L0_attn_all = _L0_attn_setup()
    _L0_attn_in = {k: v for k, v in _L0_attn_all.items() if k in ('Wqkv', 'Wproj', 'Wv', 'bv')}
    del _L0_attn_all

    def _L0_ffn_setup():
        import jax, jax.numpy as jnp
        import numpy as np
        GT0 = [[0, 1, 0, 0, 1, 0], [0, 1, 0, 0, 0, 1], [0, 0, 1, 0, 1, 0], [0, 0, 1, 0, 0, 1], [0, 0, 0, 1, 1, 0], [0, 0, 0, 1, 0, 1]]
        NCLS = 6
        K = 1

        def _expert_pairs():
            pairs = []
            for i in range(NCLS):
                p = [(j - 1, k - 1) for j in range(1, 6) for k in range(1, 6) if j != k and GT0[i][j] == 1 and (GT0[i][k] == 1)]
                pairs.append(p)
            return pairs
        PAIRS = _expert_pairs()
        B, P, D, H = (64, 64, 192, 768)

        def _gelu(t):
            return jax.nn.gelu(t, approximate=False)
        key = jax.random.key(seed)
        ks = jax.random.split(key, 8)
        s = 0.02
        x = jax.random.normal(ks[0], (B, NCLS + P, D), dtype=jnp.float32)
        mids = jax.random.randint(ks[1], (B,), 0, 6)
        moe0_W1 = jax.random.normal(ks[2], (D, H), dtype=jnp.float32) * s
        moe0_b1 = jnp.zeros((H,), jnp.float32)
        moe0_W2 = jax.random.normal(ks[3], (H, D), dtype=jnp.float32) * s
        moe0_b2 = jnp.zeros((D,), jnp.float32)
        A1_W = jax.random.normal(ks[4], (5, D, H), dtype=jnp.float32) * s
        A1_b = jnp.zeros((5, H), jnp.float32)
        A2_W = jax.random.normal(ks[5], (5, H, D), dtype=jnp.float32) * s
        A2_b = jnp.zeros((5, D), jnp.float32)
        G_W = jax.random.normal(ks[6], (NCLS, D, 2), dtype=jnp.float32) * s
        return {'x': x, 'moe0_W1': moe0_W1, 'moe0_b1': moe0_b1, 'moe0_W2': moe0_W2, 'moe0_b2': moe0_b2, 'A1_W': A1_W, 'A1_b': A1_b, 'A2_W': A2_W, 'A2_b': A2_b, 'G_W': G_W, 'mids': mids}
    _L0_ffn_all = _L0_ffn_setup()
    _L0_ffn_in = {k: v for k, v in _L0_ffn_all.items() if k in ('moe0_W1', 'moe0_b1', 'moe0_W2', 'moe0_b2', 'A1_W', 'A1_b', 'A2_W', 'A2_b', 'G_W', 'mids')}
    del _L0_ffn_all
    return {'x': x, 'L0_tok_w': _L0_tok_in['w'], 'L0_tok_b': _L0_tok_in['b'], 'L0_attn_Wqkv': _L0_attn_in['Wqkv'], 'L0_attn_Wproj': _L0_attn_in['Wproj'], 'L0_attn_Wv': _L0_attn_in['Wv'], 'L0_attn_bv': _L0_attn_in['bv'], 'L0_ffn_moe0_W1': _L0_ffn_in['moe0_W1'], 'L0_ffn_moe0_b1': _L0_ffn_in['moe0_b1'], 'L0_ffn_moe0_W2': _L0_ffn_in['moe0_W2'], 'L0_ffn_moe0_b2': _L0_ffn_in['moe0_b2'], 'L0_ffn_A1_W': _L0_ffn_in['A1_W'], 'L0_ffn_A1_b': _L0_ffn_in['A1_b'], 'L0_ffn_A2_W': _L0_ffn_in['A2_W'], 'L0_ffn_A2_b': _L0_ffn_in['A2_b'], 'L0_ffn_G_W': _L0_ffn_in['G_W'], 'L0_ffn_mids': _L0_ffn_in['mids']}

def reference(x, L0_tok_w, L0_tok_b, L0_attn_Wqkv, L0_attn_Wproj, L0_attn_Wv, L0_attn_bv, L0_ffn_moe0_W1, L0_ffn_moe0_b1, L0_ffn_moe0_W2, L0_ffn_moe0_b2, L0_ffn_A1_W, L0_ffn_A1_b, L0_ffn_A2_W, L0_ffn_A2_b, L0_ffn_G_W, L0_ffn_mids):
    import jax
    import jax.numpy as jnp

    def _L0_tok_ref(x, w, b):
        import jax, jax.numpy as jnp
        import numpy as np
        KEEP_RATIO = 0.7
        scores = jnp.einsum('bnd,do->bn', x, w) + b[0]
        N = x.shape[1]
        k = int(round(N * KEEP_RATIO))
        _, idx = jax.lax.top_k(scores, k)
        return jnp.take_along_axis(x, idx[:, :, None], axis=1)

    def _L0_attn_ref(x, Wqkv, Wproj, Wv, bv):
        import jax, jax.numpy as jnp
        import numpy as np
        NH = 12
        LEVEL = 4

        def _build_sets(T, Lmin):
            l_list, r_list = ([], [])
            L = Lmin
            while L <= T:
                for i in range(T // L):
                    l_list.append(i * L)
                    r_list.append((i + 1) * L - 1)
                L *= 2
            return (np.asarray(l_list, np.int32), np.asarray(r_list, np.int32))

        def _get_slice(x_cum, l_idx, r_idx):
            r = x_cum[:, :, r_idx, :]
            l = x_cum[:, :, np.maximum(np.asarray(l_idx) - 1, 0), :]
            mask = (np.asarray(l_idx) >= 1).astype(x_cum.dtype)[None, None, :, None]
            return r - l * mask

        def _get_slice_dyn(x_cum, l_idx, r_idx):
            r = x_cum[:, :, r_idx, :]
            l = x_cum[:, :, jnp.maximum(l_idx - 1, 0), :]
            mask = (l_idx >= 1).astype(x_cum.dtype)[None, None, :, None]
            return r - l * mask
        B, T, C = x.shape
        nh = NH
        hs = C // nh
        Lmin = 2 ** LEVEL
        scale = 1.0 / jnp.sqrt(jnp.asarray(hs, x.dtype))
        qkv = x @ Wqkv.T
        q, k, v0 = jnp.split(qkv, 3, axis=-1)
        q = q.reshape(B, T, nh, hs).transpose(0, 2, 1, 3)
        k = k.reshape(B, T, nh, hs).transpose(0, 2, 1, 3)
        v0 = v0.reshape(B, T, nh, hs).transpose(0, 2, 1, 3)
        Wv3 = Wv.reshape(hs, hs, hs)
        v = jnp.einsum('bhti,bhtj,eij->bhte', k, v0, Wv3) + bv
        k_cum = jnp.cumsum(k, axis=2)
        v_cum = jnp.cumsum(v, axis=2)
        l_idx, r_idx = _build_sets(T, Lmin)
        K = _get_slice(k_cum, l_idx, r_idx)
        V = _get_slice(v_cum, l_idx, r_idx)
        t_idx = jnp.arange(T)
        mask = t_idx[:, None] >= jnp.asarray(r_idx)[None, :]
        logits = jnp.einsum('bhtd,bhsd->bhts', q, K) * scale
        logits = jnp.where(mask[None, None], logits, -jnp.inf)
        l_tail = t_idx // Lmin * Lmin
        K_tail = _get_slice_dyn(k_cum, l_tail, t_idx)
        V_tail = _get_slice_dyn(v_cum, l_tail, t_idx)
        tail_logits = jnp.sum(q * K_tail, axis=-1) * scale
        att = jax.nn.softmax(jnp.concatenate([logits, tail_logits[..., None]], axis=-1), axis=-1)
        out = jnp.einsum('bhts,bhsd->bhtd', att[..., :-1], V) + att[..., -1:] * V_tail
        out = out.transpose(0, 2, 1, 3).reshape(B, T, C)
        return out @ Wproj.T

    def _L0_ffn_ref(x, moe0_W1, moe0_b1, moe0_W2, moe0_b2, A1_W, A1_b, A2_W, A2_b, G_W, mids):
        import jax, jax.numpy as jnp
        import numpy as np
        GT0 = [[0, 1, 0, 0, 1, 0], [0, 1, 0, 0, 0, 1], [0, 0, 1, 0, 1, 0], [0, 0, 1, 0, 0, 1], [0, 0, 0, 1, 1, 0], [0, 0, 0, 1, 0, 1]]
        NCLS = 6
        K = 1

        def _expert_pairs():
            pairs = []
            for i in range(NCLS):
                p = [(j - 1, k - 1) for j in range(1, 6) for k in range(1, 6) if j != k and GT0[i][j] == 1 and (GT0[i][k] == 1)]
                pairs.append(p)
            return pairs
        PAIRS = _expert_pairs()
        B, P, D, H = (64, 64, 192, 768)

        def _gelu(t):
            return jax.nn.gelu(t, approximate=False)
        cls_tokens = x[:, :NCLS]
        patch_tokens = x[:, NCLS:]
        patch_out = _gelu(patch_tokens @ moe0_W1 + moe0_b1) @ moe0_W2 + moe0_b2
        cls_outs = []
        for i in range(NCLS):
            tok = cls_tokens[:, i]
            eouts = [_gelu(tok @ A1_W[a] + A1_b[a]) @ A2_W[c] + A2_b[c] for a, c in PAIRS[i]]
            out = jnp.stack(eouts, axis=-1)
            gate = jax.nn.softmax(tok @ G_W[i], axis=-1)
            thr = jnp.sort(gate, axis=-1)[..., -(K + 1)]
            mask = (gate > thr[..., None]).astype(gate.dtype)
            g = gate * mask
            g = g / jnp.clip(jnp.sum(g, axis=-1, keepdims=True), 1e-06)
            cls_outs.append(jnp.sum(out * g[:, None, :], axis=-1))
        cls_out = jnp.stack(cls_outs, axis=1)
        return jnp.concatenate([cls_out, patch_out], axis=1)
    h = _L0_tok_ref(x, L0_tok_w, L0_tok_b)
    h = h + _L0_attn_ref(_layernorm(h, axis=-1), L0_attn_Wqkv, L0_attn_Wproj, L0_attn_Wv, L0_attn_bv)
    h = h + _L0_ffn_ref(_layernorm(h, axis=-1), L0_ffn_moe0_W1, L0_ffn_moe0_b1, L0_ffn_moe0_W2, L0_ffn_moe0_b2, L0_ffn_A1_W, L0_ffn_A1_b, L0_ffn_A2_W, L0_ffn_A2_b, L0_ffn_G_W, L0_ffn_mids)
    return h

_drawn_inputs = setup_inputs


def setup_inputs(seed=0):
    import zlib

    import numpy as np

    out = dict(_drawn_inputs(seed))
    spreads = {'L0_attn_bv': (0.0, 0.1),
     'L0_ffn_moe0_b1': (0.0, 0.497),
     'L0_ffn_moe0_b2': (0.0, 0.1),
     'L0_ffn_A1_b': (0.0, 0.8),
     'L0_ffn_A2_b': (0.0, 0.8)}
    factors = {'L0_attn_Wv': 3.065, 'L0_ffn_A1_W': 8.0, 'L0_ffn_A2_W': 8.0, 'L0_ffn_G_W': 8.0}
    for name, (base, spread) in spreads.items():
        noise = np.random.default_rng([zlib.crc32(name.encode()), seed]).standard_normal(out[name].shape)
        drawn = base * np.exp(spread * noise) if base else spread * noise
        out[name] = jnp.asarray(drawn.astype(out[name].dtype))
    for name, factor in factors.items():
        out[name] = (out[name] * factor).astype(out[name].dtype)
    return out
```

```python
from contextlib import ExitStack

import concourse.bass as bass
import concourse.mybir as mybir

F32 = mybir.dt.float32
BF16 = mybir.dt.bfloat16
U32 = mybir.dt.uint32
U16 = mybir.dt.uint16
ALU = mybir.AluOpType
ACT = mybir.ActivationFunctionType
AX = mybir.AxisListType

NB, NTOK, D = 8, 750, 192
T = int(round(NTOK * 0.7))
NH, HS = 12, 16
BLK = 16
TP = -(-T // BLK) * BLK
NBLK = TP // BLK
CH = TP // 2
TT, NT = 105, 5
SC, NSC = 125, 6
FB = 96
HID = 768
NM = HID // 128
NCLS = 6
NSET = 63
EPS = 1e-5
SCALE = 0.25
NEG = -1e30
assert NT * TT == T and NSC * SC == NTOK

NTOKC, NQKV, NVAL, NATT, NFFN, NCC, NPOOL = 3, 1, 7, 6, 4, 7, 2
CHID, CDVE, CGELU = 11, 22, 6


def upto(b, per, k=None):
    v = b * per + (per if k is None else k)
    return max(v, 0) if isinstance(v, int) else v


def is_at(b, n):
    return isinstance(b, int) and b == n


def exists(b):
    return not isinstance(b, int) or 0 <= b < NB


def build(nc, x, tok_w, tok_b, wqkvT, wprojT, wvT, bv96, w1, b1c, w2, b2, a1, a1bc, a2, a2b, gw,
          c_ident, c_krep, c_vrep, c_kbd, c_onehot, c_parity, c_tail, c_lower, c_pick, c_cls, out):
    ctx = ExitStack()
    with ctx:
        def sb(name, shape, dt=F32):
            return ctx.enter_context(nc.sbuf_tensor(name, shape, dt))

        def sem(name):
            return ctx.enter_context(nc.semaphore(name))

        ident = sb("ident", [128, 128])
        krep = sb("krep", [FB, 2, 2, 128], BF16)
        vrep = sb("vrep", [FB, 2, 128], BF16)
        parity = sb("parity", [FB, 2])
        tailsel = sb("tailsel", [128, 32])
        lower = sb("lower", [SC, SC], BF16)
        pick = sb("pick", [48, NCLS, 2])
        clsrow = sb("clsrow", [5, 2, 48])
        neghalf = sb("neghalf", [TT, NT])
        wtok = sb("wtok", [SC, D])
        btok = sb("btok", [SC, 1])
        wqkv = sb("wqkv", [FB, 2, 3 * D])
        wproj = sb("wproj", [FB, 2, D])
        wbil = sb("wbil", [128, 2, 2, 32])
        bvcol = sb("bvcol", [FB, 1])
        w1s = sb("w1s", [FB, 2, HID])
        b1s = sb("b1s", [128, NM])
        w2s = sb("w2s", [128, NM, D])
        b2row = sb("b2row", [TT, D])
        a1bs = sb("a1bs", [128, 5, NM])
        a2bs = sb("a2bs", [5, D])
        gws = sb("gws", [FB, 2, NCLS, 2])

        xs = sb("xs", [SC, NSC, D])
        score_junk = sb("score_junk", [SC, NSC, D], BF16)
        score_raw = sb("score_raw", [SC, NSC])
        score_col = sb("score_col", [SC, NSC])
        score_row = sb("score_row", [SC, NTOK])
        cmp_junk = sb("cmp_junk", [SC, 2, NTOK], BF16)
        tie_junk = sb("tie_junk", [SC, 2, SC], BF16)
        counts = sb("counts", [SC, 3, NSC])
        rank_sum = sb("rank_sum", [SC, NSC])
        rank_base = sb("rank_base", [SC, 1])
        rank_idx = sb("rank_idx", [SC, NSC], U32)

        hA = sb("hA", [TT, NT, D])
        xn1 = sb("xn1", [TT, NT, D])
        xn1T = sb("xn1T", [FB, 2, TP])
        xn2T = sb("xn2T", [FB, 2, TP])
        stats = sb("stats", [TT, 2, NT, 6])
        meanvar = sb("meanvar", [TT, 2, NT, 2])
        vareps = sb("vareps", [TT, 2, NT])
        rstd = sb("rstd", [TT, 2, NT])
        nmean = sb("nmean", [TT, 2, NT])

        kvT = sb("kvT", [FB, 4, TP])
        qT = sb("qT", [FB, 2, TP])
        qkT = sb("qkT", [FB, 2, TP])
        region = sb("region", [128, 28 * TP])
        outer = region[:, 0:6 * TP].rearrange("p (g q t) -> p g q t", g=2, q=3)
        vrows = region[:, 6 * TP:12 * TP].rearrange("p (g q t) -> p g q t", g=2, q=3)
        stack = region[0:FB, 12 * TP:18 * TP].bitcast(BF16).rearrange("p (q t) -> p q t", q=12)
        parts = region[0:FB, 18 * TP:24 * TP].bitcast(BF16).rearrange("p (s k t) -> p s k t", s=3, k=4)
        rest = region[0:FB, 24 * TP:28 * TP].rearrange("p (k t) -> p k t", k=4)
        a1s = region[0:FB, 0:10 * HID].rearrange("p (a k n) -> p a k n", a=5, k=2)
        a2s = region[:, 10 * HID:10 * HID + 5 * NM * D].rearrange("p (a m n) -> p a m n", a=5, m=NM)
        vT = sb("vT", [FB, 2, TP])
        ksets = sb("ksets", [FB, 2, 64])
        vsets = sb("vsets", [FB, 2, 64])
        vexp = sb("vexp", [FB, 2, 2, 64])
        kbd = sb("kbd", [FB, 6, 128])
        vst = sb("vst", [128, 2, FB])
        X = sb("X", [FB, 6, TP])

        nmax = sb("nmax", [TT, 2, NH])
        smax = sb("smax", [TT, 2, NH])
        den = sb("den", [TT, 2, NH])
        rden = sb("rden", [TT, 2, NH])
        E = sb("E", [TT, 2, 6, 128])
        ET = sb("ET", [128, 6, TP])
        tailv = sb("tailv", [FB, 2, TP])
        outT = sb("outT", [FB, 2, TP])
        hR = sb("hR", [TT, NT, D])
        h1 = sb("h1", [TT, NT, D])
        h1b = sb("h1b", [TT, NT, D])
        xn2 = sb("xn2", [TT, NT, D])
        hid = ET
        osb = sb("osb", [TT, NT, D])

        cx = sb("cx", [FB, 2, NCLS, NB])
        cres = sb("cres", [48, D])
        chp = sb("chp", [128, 2, NM, 48])
        chz0 = sb("chz0", [128, 2, NM, 48])
        chz1 = sb("chz1", [128, 3, NM, 48])
        cg = sb("cg", [48, 12, 2])
        cgs = sb("cgs", [48, NCLS, 2])
        c0 = sb("c0", [48, D])
        c1 = sb("c1", [48, D])

        SA0 = ctx.enter_context(nc.psum_tensor("SA0", [128, 2, 512], F32))
        SA1 = ctx.enter_context(nc.psum_tensor("SA1", [128, 2, 512], F32))
        SB = ctx.enter_context(nc.psum_tensor("SB", [128, 2, 512], F32))
        SCC = ctx.enter_context(nc.psum_tensor("SCC", [128, 2, 512], F32))

        score_dram = nc.dram_tensor("score_dram", [NB, NTOK], F32, kind="Internal").ap()
        sorted_dram = nc.dram_tensor("sorted_dram", [NB * NTOK, D], F32, kind="Internal").ap()
        sorted_b = sorted_dram.rearrange("(b n) d -> b n d", b=NB)
        cls_dram = nc.dram_tensor("cls_dram", [NB, NCLS, D], F32, kind="Internal").ap()

        x_loaded = sem("x_loaded")
        score_stored = sem("score_stored")
        row_loaded = sem("row_loaded")
        scattered = sem("scattered")
        hA_loaded = sem("hA_loaded")
        hR_loaded = sem("hR_loaded")
        k_stacked = sem("k_stacked")
        v_stacked = sem("v_stacked")
        q_placed = sem("q_placed")
        qk_placed = sem("qk_placed")
        cls_stored = sem("cls_stored")
        out_stored = sem("out_stored")
        tok_const = sem("tok_const")
        qkv_const = sem("qkv_const")
        val_const = sem("val_const")
        att_const = sem("att_const")
        ffn_const = sem("ffn_const")
        cls_const = sem("cls_const")
        cls_io = sem("cls_io")
        xn1T_ready = sem("xn1T_ready")
        qkv_ready = sem("qkv_ready")
        logits_ready = sem("logits_ready")
        attT_ready = sem("attT_ready")
        pv_ready = sem("pv_ready")
        proj_ready = sem("proj_ready")
        vr_ready = sem("vr_ready")
        kr_ready = sem("kr_ready")
        contracted = sem("contracted")
        xn2T_ready = sem("xn2T_ready")
        ffn1_ready = sem("ffn1_ready")
        ffn2_ready = sem("ffn2_ready")
        vst_ready = sem("vst_ready")
        ln1_applied = sem("ln1_applied")
        xn1T_copied = sem("xn1T_copied")
        qkv_copied = sem("qkv_copied")
        part1_done = sem("part1_done")
        part2_done = sem("part2_done")
        exp_done = sem("exp_done")
        attT_copied = sem("attT_copied")
        vr_copied = sem("vr_copied")
        v_copied = sem("v_copied")
        ln2_applied = sem("ln2_applied")
        xn2T_copied = sem("xn2T_copied")
        cx_copied = sem("cx_copied")
        gelu_done = sem("gelu_done")
        vst_copied = sem("vst_copied")
        score_step = sem("score_step")
        score_done = sem("score_done")
        rank_step = sem("rank_step")
        rank_done = sem("rank_done")
        base_done = sem("base_done")
        ln_stats1 = sem("ln_stats1")
        ln_stats2 = sem("ln_stats2")
        nmean1_done = sem("nmean1_done")
        nmean2_done = sem("nmean2_done")
        max_step = sem("max_step")
        max_done = sem("max_done")
        rden_done = sem("rden_done")
        norm_done = sem("norm_done")
        tail_done = sem("tail_done")
        outT_done = sem("outT_done")
        residual_done = sem("residual_done")
        outer_done = sem("outer_done")
        qk_done = sem("qk_done")
        kbd_done = sem("kbd_done")
        vexp_done = sem("vexp_done")
        added = sem("added")
        pool_const = sem("pool_const")
        waits_passed = sem("waits_passed")
        rest1_done = sem("rest1_done")
        part3_done = sem("part3_done")
        kprefix = sem("kprefix")
        vprefix = sem("vprefix")
        kset_step = sem("kset_step")
        vset_step = sem("vset_step")
        rstd1_done = sem("rstd1_done")
        rstd2_done = sem("rstd2_done")
        h1b_done = sem("h1b_done")
        cgate_ready = sem("cgate_ready")
        chid_ready = sem("chid_ready")
        cout_ready = sem("cout_ready")
        cgs_done = sem("cgs_done")
        cdve = sem("cdve")
        cact = sem("cact")

        block = ctx.enter_context(nc.Block())

        def run(eng, iteration):
            for i in range(-3, 1):
                iteration(i)
            with eng.Fori(1, NB - 3) as i:
                iteration(i)
            for i in range(NB - 3, NB):
                iteration(i)

        def passed(eng):
            eng.sem_inc(waits_passed, 1)

        def both(ps, rows, n=CH):
            return ps[0:rows, :, 0:n]

        def halves(ap):
            return ap.rearrange("p (c t) -> p c t", c=2)

        @block.sync
        def _(eng):
            eng.dma_start(wtok[:], tok_w.rearrange("(o d) -> o d", o=1).to_broadcast([SC, D])).then_inc(tok_const, 16)
            eng.dma_start(btok[:], tok_b.rearrange("(o d) -> o d", o=1).to_broadcast([SC, 1])).then_inc(tok_const, 16)
            eng.dma_start(lower[:].bitcast(U16), c_lower).then_inc(tok_const, 16)

            def iteration(i):
                n, l, p = i + 3, i + 2, i + 1
                if exists(n):
                    eng.wait_ge(scattered, upto(n - 1, 16 * NSC))
                    eng.dma_start(xs[:], x[n].rearrange("(c p) d -> p c d", p=SC)).then_inc(x_loaded, 16)
                if exists(l):
                    eng.wait_ge(scattered, upto(l, 16 * NSC))
                    eng.wait_ge(ln1_applied, upto(l - 1, 1))
                    eng.wait_ge(ln_stats1, upto(l - 1, 3))
                    eng.dma_start(hA[:], sorted_b[l, 0:T].rearrange("(j p) d -> p j d", p=TT)).then_inc(hA_loaded, 16)
                if exists(i):
                    eng.wait_ge(residual_done, upto(i - 1, 2))
                    eng.dma_start(hR[:], sorted_b[i, 0:T].rearrange("(j p) d -> p j d", p=TT)).then_inc(hR_loaded, 16)
                if exists(n):
                    eng.wait_ge(score_done, upto(n, 1))
                    eng.dma_start(score_dram[n].rearrange("(c p) -> p c", p=SC), score_col[:],
                                                  allow_slow_non_contiguous=True).then_inc(score_stored, 16)

                def stack_up(kv, s):
                    for part in range(3):
                        for q in range(3):
                            eng.dma_start(stack[32 * part:32 * part + 32, 6 * kv + q:6 * kv + q + 4:3, :], parts[32 * q:32 * q + 32, part, 2 * kv:2 * kv + 2, :]).then_inc(s, 16)

                if exists(p):
                    eng.wait_ge(part3_done, upto(p, 2, 1))
                    eng.wait_ge(kr_ready, upto(p - 1, 24))
                    stack_up(0, k_stacked)
                if exists(n):
                    eng.wait_ge(score_stored, upto(n, 16))
                    eng.wait_ge(rank_step, upto(n - 1, NSC + 1))
                    eng.dma_start(score_row[:], score_dram[n].rearrange("(o m) -> o m", o=1).to_broadcast([SC, NTOK])).then_inc(row_loaded, 16)
                if exists(p):
                    eng.wait_ge(part3_done, upto(p, 2, 2))
                    eng.wait_ge(vr_ready, upto(p - 1, 12))
                    stack_up(1, v_stacked)
                    eng.wait_ge(qkv_copied, upto(p, 6))
                    eng.wait_ge(logits_ready, upto(p - 1, NT))
                    for q in range(3):
                        eng.dma_start(X[0:32, q:q + 4:3, :], qT[32 * q:32 * q + 32, :, :]).then_inc(q_placed, 16)
                if exists(i):
                    eng.wait_ge(residual_done, upto(i, 2))
                    eng.dma_start(cls_dram[i], h1[0:NCLS, 0, :]).then_inc(cls_stored, 16)
                if exists(p):
                    eng.wait_ge(qk_done, upto(p, 1))
                    for q in range(3):
                        eng.dma_start(X[32:64, q:q + 4:3, :], qkT[32 * q:32 * q + 32, :, :]).then_inc(qk_placed, 16)
                if exists(i):
                    eng.wait_ge(added, upto(i, 2))
                    ob = out[i].rearrange("(j p) d -> p j d", p=TT)
                    eng.dma_start(ob[:, 1:NT], osb[:, 1:NT]).then_inc(out_stored, 16)
                    eng.dma_start(ob[NCLS:TT, 0], osb[NCLS:TT, 0]).then_inc(out_stored, 16)

            run(eng, iteration)
            eng.wait_ge(cls_stored, upto(NB - 1, 16))
            for c in range(NCLS):
                eng.dma_start(cres[NB * c:NB * c + NB, :], cls_dram[:, c, :]).then_inc(cls_io, 16)
            eng.wait_ge(cdve, CDVE)
            for c in range(NCLS):
                eng.dma_start(out[:, c, :], c0[NB * c:NB * c + NB, :]).then_inc(cls_io, 16)
            eng.wait_ge(cls_io, 16 * 2 * NCLS)
            eng.wait_ge(out_stored, upto(NB - 1, 16 * 2))

        @block.tensor
        def _(eng):
            def mm(o, l, r, start=True, stop=True):
                return eng.matmul(o, l, r, start=start, stop=stop, skip_group_check=True)

            def logits(b, j, slot):
                if j == 0:
                    eng.wait_ge(q_placed, upto(b, 16 * 3))
                    eng.wait_ge(qk_placed, upto(b, 16 * 3))
                    eng.wait_ge(kbd_done, upto(b, 1))
                for h2 in range(6):
                    ins = mm(slot[0:TT, h2 // 3, (h2 % 3) * 128:(h2 % 3) * 128 + 128],
                             X[:, h2, TT * j:TT * j + TT], kbd[:, h2, :])
                ins.then_inc(logits_ready, 1)

            def project(b, k, slot):
                if k == 0:
                    eng.wait_ge(xn1T_copied, upto(b, 2))
                col = (D, D + FB, 2 * D, 2 * D + FB, 0, FB)[k]
                for c in range(2):
                    for kb in range(2):
                        ins = mm(slot[0:FB, c, 0:CH], wqkv[:, kb, col:col + FB],
                                 xn1T[:, kb, CH * c:CH * c + CH], kb == 0, kb == 1)
                ins.then_inc(qkv_ready, 1)

            def att_transpose(b, j, slot):
                eng.wait_ge(norm_done, upto(b, NT, j + 1))
                for h2 in range(6):
                    ins = eng.transpose(slot[:, h2 // 3, (h2 % 3) * TT:(h2 % 3) * TT + TT],
                                        E[:, j % 2, h2, :], ident[0:TT, 0:TT])
                ins.then_inc(attT_ready, 1)

            def iteration(i):
                p, l = i + 1, i + 2
                at, nx = exists(i), exists(p)
                if at:
                    eng.wait_ge(xn1T_copied, upto(p, 2)) if nx else None
                    eng.wait_ge(gelu_done, upto(i - 1, NM))
                    logits(i, 0, SB)
                    logits(i, 1, SCC)
                eng.wait_ge(added, upto(i - 1, 2))
                eng.wait_ge(outer_done, upto(i, 24))
                eng.wait_ge(vst_copied, upto(i, 1))
                if nx:
                    if is_at(p, 0):
                        eng.wait_ge(qkv_const, 16 * NQKV)
                    project(p, 0, SA0)
                    project(p, 1, SA1)
                    eng.wait_ge(qkv_copied, upto(p, 6, 1))
                    project(p, 2, SA0)
                    eng.wait_ge(qkv_copied, upto(p, 6, 2))
                    project(p, 3, SA1)
                if at:
                    eng.wait_ge(exp_done, upto(i, NT, 1))
                    logits(i, 2, SB)
                if nx:
                    eng.wait_ge(qkv_copied, upto(p, 6, 3))
                if at:
                    att_transpose(i, 0, SA0)
                if nx:
                    eng.wait_ge(qkv_copied, upto(p, 6, 4))
                    project(p, 4, SA1)
                    if at:
                        eng.wait_ge(attT_copied, upto(i, NT, 1))
                    project(p, 5, SA0)
                if at:
                    eng.wait_ge(exp_done, upto(i, NT, 2))
                    logits(i, 3, SCC)
                    if nx:
                        eng.wait_ge(qkv_copied, upto(p, 6, 5))
                    att_transpose(i, 1, SA1)
                    if nx:
                        eng.wait_ge(qkv_copied, upto(p, 6, 6))
                    eng.wait_ge(attT_copied, upto(i, NT, 1))
                    att_transpose(i, 2, SA0)
                    eng.wait_ge(exp_done, upto(i, NT, 3))
                    logits(i, 4, SB)
                    eng.wait_ge(attT_copied, upto(i, NT, 2))
                    att_transpose(i, 3, SA1)
                    eng.wait_ge(exp_done, upto(i, NT, 4))
                    att_transpose(i, 4, SCC)
                    for kb, num, tail in ((0, SA0, SA1), (1, SB, SCC)):
                        eng.wait_ge(attT_copied, upto(i, NT, 5))
                        eng.wait_ge(exp_done, upto(i, NT, 5))
                        for c in range(2):
                            for q in range(3):
                                mm(num[32 * q:32 * q + 32, c, 0:CH], vst[:, kb, 32 * q:32 * q + 32],
                                   ET[:, 3 * kb + q, CH * c:CH * c + CH])
                        for c in range(2):
                            for q in range(3):
                                ins = mm(tail[32 * q:32 * q + 32, c, 0:CH], tailsel[:],
                                         ET[:, 3 * kb + q, CH * c:CH * c + CH])
                        ins.then_inc(pv_ready, 1)
                    eng.wait_ge(outT_done, upto(i, 2))
                    for j in range(NT):
                        slot = SA0 if j < 4 else SA1
                        o = slot[0:TT, (j % 4) // 2, (j % 2) * D:(j % 2) * D + D]
                        for kb in range(2):
                            ins = mm(o, outT[:, kb, TT * j:TT * j + TT], wproj[:, kb, :], kb == 0, kb == 1)
                        if j >= 3:
                            ins.then_inc(proj_ready, 1)
                if nx:
                    if is_at(p, 0):
                        eng.wait_ge(val_const, 16 * NVAL)
                    eng.wait_ge(qkv_copied, upto(p, 6))
                    eng.wait_ge(residual_done, upto(i, 2))
                    eng.wait_ge(k_stacked, upto(p, 16 * 9))
                    eng.wait_ge(v_stacked, upto(p, 16 * 9))
                    nv = nk = 0

                    def contract(g):
                        kb, par, half = g // 4, g // 2 % 2, g % 2
                        eng.wait_ge(outer_done, upto(p, 24, 3 * g + 3))
                        if g == 4:
                            eng.wait_ge(v_copied, upto(p, 2, 1))
                        for c in range(2):
                            for q in range(3):
                                ins = mm(SCC[32 * q:32 * q + 32, c, 0:CH], wbil[:, half, par, :],
                                         outer[:, g % 2, q, CH * c:CH * c + CH],
                                         g % 4 == 0, g % 4 == 3)
                        ins.then_inc(contracted, 1)

                    for g in range(8):
                        kb, par, half = g // 4, g // 2 % 2, g % 2
                        for q in range(3):
                            if half == 0:
                                eng.wait_ge(vr_copied, upto(p, 12, nv))
                                for c in range(2):
                                    ins = mm(SB[:, c, 0:CH], vrep[:, par, :],
                                             stack[:, 6 + 3 * kb + q, CH * c:CH * c + CH])
                                ins.then_inc(vr_ready, 1)
                                nv += 1
                            slot = (SA0, SA1)[nk % 2]
                            if nk >= 2:
                                eng.wait_ge(outer_done, upto(p, 24, nk - 1))
                            for c in range(2):
                                ins = mm(slot[:, c, 0:CH], krep[:, par, half, :],
                                         stack[:, 3 * kb + q, CH * c:CH * c + CH])
                            ins.then_inc(kr_ready, 1)
                            nk += 1
                        if g >= 1:
                            contract(g - 1)
                    contract(7)
                if at:
                    eng.wait_ge(outer_done, upto(p, 24)) if nx else eng.wait_ge(residual_done, upto(i, 2))
                    eng.wait_ge(ln2_applied, upto(i, 1))
                    for kb, slot in ((0, SA0), (1, SA1)):
                        for j in range(NT):
                            ins = eng.transpose(slot[0:FB, j // 3, (j % 3) * TT:(j % 3) * TT + TT],
                                                xn2[:, j, FB * kb:FB * kb + FB], ident[0:TT, 0:TT])
                        ins.then_inc(xn2T_ready, 1)
                    eng.wait_ge(xn2T_copied, upto(i, 2))
                    if nx:
                        eng.wait_ge(vr_copied, upto(p, 12))
                        eng.wait_ge(v_copied, upto(p, 2))
                    eng.wait_ge(outT_done, upto(i, 2))
                    for m in range(NM):
                        slot = (SB, SCC, SA0, SA1)[m % 4]
                        if m >= 4:
                            eng.wait_ge(gelu_done, upto(i, NM, m - 3))
                        for c in range(2):
                            for kb in range(2):
                                ins = mm(slot[:, c, 0:CH], w1s[:, kb, 128 * m:128 * m + 128],
                                         xn2T[:, kb, CH * c:CH * c + CH], kb == 0, kb == 1)
                        ins.then_inc(ffn1_ready, 1)
                    eng.wait_ge(gelu_done, upto(i, NM))
                    for j in range(NT):
                        slot = SA0 if j < 4 else SA1
                        o = slot[0:TT, (j % 4) // 2, (j % 2) * D:(j % 2) * D + D]
                        for m in range(NM):
                            ins = mm(o, hid[:, m, TT * j:TT * j + TT], w2s[:, m, :], m == 0, m == NM - 1)
                        if j >= 3:
                            ins.then_inc(ffn2_ready, 1)
                if nx:
                    eng.wait_ge(outer_done, upto(p, 24))
                    eng.wait_ge(vexp_done, upto(p, 1))
                    for kb in range(2):
                        ins = eng.transpose(SA1[:, 1, FB * kb:FB * kb + FB],
                                            vexp[:, kb, :, :], ident[0:FB, 0:FB])
                    ins.then_inc(vst_ready, 1)
                if exists(l):
                    if is_at(l, 0):
                        eng.wait_ge(att_const, 16 * NATT)
                    eng.wait_ge(ln1_applied, upto(l, 1))
                    if nx:
                        eng.wait_ge(vr_copied, upto(p, 12))
                        eng.wait_ge(v_copied, upto(p, 2))
                    eng.wait_ge(gelu_done, upto(i, NM))
                    for kb, slot in ((0, SB), (1, SCC)):
                        for j in range(NT):
                            ins = eng.transpose(slot[0:FB, j // 3, (j % 3) * TT:(j % 3) * TT + TT],
                                                xn1[:, j, FB * kb:FB * kb + FB], ident[0:TT, 0:TT])
                        ins.then_inc(xn1T_ready, 1)
                if is_at(l, 0):
                    eng.wait_ge(ffn_const, 16 * NFFN)

            run(eng, iteration)

            eng.wait_ge(cls_const, 16 * NCC)
            eng.wait_ge(cx_copied, upto(NB - 1, 1))
            eng.wait_ge(gelu_done, upto(NB - 1, NM))
            cxv = [cx[:, kb] for kb in range(2)]
            for kb in range(2):
                ins = mm(SB[0:48, 0, 0:2 * NCLS], cxv[kb].rearrange("p c b -> p (c b)"), gws[:, kb, :, :], kb == 0, kb == 1)
            ins.then_inc(cgate_ready, 1)
            eng.wait_ge(added, upto(NB - 1, 2))
            for pair in range(2):
                hp = (SA0, SA1)[pair][:, 0, 0:NM * 48].rearrange("p (m c b) -> p m c b", m=NM, b=NB)
                for e in range(3 - pair):
                    a = e if pair == 0 else 3 + e
                    cs = slice(2 * e, 2 * e + 2) if pair == 0 else slice(e, NCLS, 2)
                    for m in range(NM):
                        for kb in range(2):
                            ins = mm(hp[:, m, cs, :], a1s[:, a, kb, 128 * m:128 * m + 128],
                                     cxv[kb][:, cs, :], kb == 0, kb == 1)
            ins.then_inc(chid_ready, 1)
            eng.wait_ge(cact, CGELU)
            for pair in range(2):
                o = SCC[0:48, pair, 0:D]
                mm(o, clsrow[:, pair, :], a2bs[:], True, False)
                for e in range(2 + pair):
                    a = 3 + e if pair == 0 else e
                    hz = (chz0, chz1)[pair]
                    for m in range(NM):
                        ins = mm(o, hz[:, e, m, :], a2s[:, a, m, :], False, e == 1 + pair and m == NM - 1)
            ins.then_inc(cout_ready, 1)

        @block.scalar
        def _(eng):
            def act(o, i_, f, **kw):
                return eng.activation(o, i_, f, **kw)

            eng.dma_start(ident[:], c_ident).then_inc(att_const, 16)
            eng.dma_start(parity[:], c_parity).then_inc(att_const, 16)
            eng.dma_start(tailsel[:], c_tail).then_inc(att_const, 16)
            eng.dma_start(X[64:96, :, :], c_onehot).then_inc(att_const, 16)
            eng.dma_start(kbd[32:96, :, :], c_kbd).then_inc(att_const, 16)
            eng.dma_start(wproj[:], wprojT.rearrange("(k p) n -> p k n", p=FB)).then_inc(att_const, 16)
            eng.dma_start(wqkv[:], wqkvT.rearrange("(k p) n -> p k n", p=FB)).then_inc(qkv_const, 16)
            eng.dma_start(krep[:].bitcast(U16), c_krep).then_inc(val_const, 16)
            eng.dma_start(vrep[:].bitcast(U16), c_vrep).then_inc(val_const, 16)
            eng.dma_start(bvcol[:], bv96).then_inc(val_const, 16)
            eng.wait_ge(pool_const, 1)
            for half in range(2):
                for par in range(2):
                    eng.dma_start(wbil[:, half, par, HS * par:HS * par + HS], wvT[128 * half:128 * half + 128, :]).then_inc(val_const, 16)
            eng.dma_start(w1s[:], w1.rearrange("(k p) n -> p k n", p=FB)).then_inc(ffn_const, 16)
            eng.dma_start(b1s[:], b1c).then_inc(ffn_const, 16)
            eng.dma_start(w2s[:], w2.rearrange("(m p) n -> p m n", p=128)).then_inc(ffn_const, 16)
            eng.dma_start(b2row[:], b2.rearrange("(o d) -> o d", o=1).to_broadcast([TT, D])).then_inc(ffn_const, 16)

            def transposed_copy(slot, dst, kb):
                act(dst[:, kb, 0:3 * TT], slot[0:FB, 0, 0:3 * TT], ACT.Copy)
                return act(dst[:, kb, 3 * TT:T], slot[0:FB, 1, 0:2 * TT], ACT.Copy)

            def exps(b, j):
                slot = (SB, SCC)[j % 2]
                eng.wait_ge(max_done, upto(b, NT, j + 1))
                if j >= 2:
                    eng.wait_ge(attT_ready, upto(b, NT, j - 1))
                else:
                    eng.wait_ge(attT_ready, upto(b - 1, NT))
                for h in range(NH):
                    o = (h % 2) * 64
                    ins = act(E[:, j % 2, h // 2, o:o + 64],
                              slot[0:TT, h // 6, (h % 6) * 64:(h % 6) * 64 + 64], ACT.Exp,
                              bias=nmax[:, j % 2, h:h + 1], scale=SCALE, accum_out=den[:, j % 2, h:h + 1])
                ins.then_inc(exp_done, 1)

            def copy_projection(b, k):
                slot = (SA0, SA1, SA0, SA1, SA1, SA0)[k]
                eng.wait_ge(qkv_ready, upto(b, 6, k + 1))
                if k == 0:
                    eng.wait_ge(kset_step, upto(b - 1, 6))
                    eng.wait_ge(part3_done, upto(b - 1, 2))
                    eng.wait_ge(qk_done, upto(b - 1, 1))
                if k == 4:
                    eng.wait_ge(q_placed, upto(b - 1, 16 * 3))
                dst = kvT[:, k, :] if k < 4 else qT[:, k - 4, :]
                act(halves(dst), both(slot, FB), ACT.Copy).then_inc(qkv_copied, 1)

            def part(b, kv, n):
                if n == 0:
                    eng.wait_ge(qkv_copied, upto(b, 6, 2 * kv + 2))
                    eng.wait_ge((v_stacked if kv else k_stacked), upto(b - 1, 16 * 9))
                    act(parts[:, 0, 2 * kv:2 * kv + 2, :], kvT[:, 2 * kv:2 * kv + 2, :], ACT.Copy).then_inc(part1_done, 1)
                else:
                    eng.wait_ge(rest1_done, upto(b, 2, kv + 1))
                    act(parts[:, 1, 2 * kv:2 * kv + 2, :], rest[:, 2 * kv:2 * kv + 2, :], ACT.Copy).then_inc(part2_done, 1)

            def copy_attT(b, j):
                slot = (SA0, SA1, SA0, SA1, SCC)[j]
                eng.wait_ge(attT_ready, upto(b, NT, j + 1))
                if j == 0:
                    eng.wait_ge(ffn2_ready, upto(b - 1, 2))
                act(
                    ET[:, :, TT * j:TT * j + TT].rearrange("p (k q) t -> p k q t", k=2),
                    slot[:, :, 0:3 * TT].rearrange("p k (q t) -> p k q t", q=3), ACT.Copy).then_inc(attT_copied, 1)

            def apply_norm(b, which, src, dst, sem):
                for j in range(NT):
                    ins = act(dst[:, j, :], src[:, j, :], ACT.Identity, scale=rstd[:, which, j:j + 1],
                              bias=nmean[:, which, j:j + 1])
                ins.then_inc(sem, 1)

            def iteration(i):
                p, l = i + 1, i + 2
                at, nx = exists(i), exists(p)
                if at:
                    exps(i, 0)
                if nx:
                    copy_projection(p, 0)
                    copy_projection(p, 1)
                    part(p, 0, 0)
                if at:
                    exps(i, 1)
                if nx:
                    copy_projection(p, 2)
                    copy_projection(p, 3)
                    part(p, 1, 0)
                if at:
                    copy_attT(i, 0)
                    exps(i, 2)
                if nx:
                    part(p, 0, 1)
                    copy_projection(p, 4)
                    copy_projection(p, 5)
                    part(p, 1, 1)
                if at:
                    exps(i, 3)
                    copy_attT(i, 1)
                    copy_attT(i, 2)
                    exps(i, 4)
                    copy_attT(i, 3)
                    copy_attT(i, 4)
                if is_at(i, NB - 1):
                    eng.wait_ge(contracted, upto(i, 8))
                    eng.dma_start(a1s[:], a1.rearrange("a (k p) n -> p a k n", p=FB)).then_inc(cls_const, 16)
                    eng.dma_start(a1bs[:], a1bc).then_inc(cls_const, 16)
                    eng.dma_start(a2s[:], a2.rearrange("a (m p) n -> p a m n", p=128)).then_inc(cls_const, 16)
                    eng.dma_start(a2bs[:], a2b).then_inc(cls_const, 16)
                    eng.dma_start(gws[:], gw).then_inc(cls_const, 16)
                    eng.dma_start(pick[:], c_pick).then_inc(cls_const, 16)
                    eng.dma_start(clsrow[:], c_cls).then_inc(cls_const, 16)

                def copy_values(kb):
                    eng.wait_ge(contracted, upto(p, 8, 4 * kb + 4))
                    if kb == 0:
                        eng.wait_ge(outT_done, upto(p - 1, 2))
                        eng.wait_ge(tail_done, upto(p - 1, 2))
                        eng.wait_ge(vset_step, upto(p - 1, 6))
                        if is_at(p, 0):
                            eng.wait_ge(val_const, 16 * NVAL)
                    act(halves(vT[:, kb, :]), both(SCC, FB), ACT.Identity, bias=bvcol[:, 0:1]).then_inc(v_copied, 1)

                nv = 0
                for g in range(8):
                    if nx and g % 2 == 0:
                        for q in range(3):
                            eng.wait_ge(vr_ready, upto(p, 12, nv + 1))
                            if g < 4:
                                eng.wait_ge(outer_done, upto(p - 1, 24, 6 * (g // 2) + 18))
                            else:
                                eng.wait_ge(outer_done, upto(p, 24, 6 * (g // 2) - 6))
                            act(halves(vrows[:, g // 2 % 2, q, :]), both(SB, 128), ACT.Copy).then_inc(vr_copied, 1)
                            nv += 1
                    if nx and g == 4:
                        copy_values(0)
                    if at and g == 5:
                        eng.wait_ge(nmean2_done, upto(i, 1))
                        eng.wait_ge(xn2T_ready, upto(i - 1, 2))
                        apply_norm(i, 1, h1, xn2, ln2_applied)
                if nx:
                    copy_values(1)
                if at:
                    for kb, slot in ((0, SA0), (1, SA1)):
                        eng.wait_ge(xn2T_ready, upto(i, 2, kb + 1))
                        if kb == 0:
                            eng.wait_ge(ffn1_ready, upto(i - 1, NM))
                            eng.wait_ge(cx_copied, upto(i - 1, 1))
                        transposed_copy(slot, xn2T, kb).then_inc(xn2T_copied, 1)
                    eng.wait_ge(xn2T_copied, upto(i, 2))
                    act(cx[:, :, :, i], xn2T[:, :, 0:NCLS], ACT.Copy).then_inc(cx_copied, 1)
                    for m in range(NM):
                        eng.wait_ge(ffn1_ready, upto(i, NM, m + 1))
                        if m == 0:
                            eng.wait_ge(pv_ready, upto(i, 2))
                        slot = (SB, SCC, SA0, SA1)[m % 4]
                        act(halves(hid[:, m, :]), both(slot, 128), ACT.Gelu, bias=b1s[:, m:m + 1]).then_inc(gelu_done, 1)
                if exists(l):
                    eng.wait_ge(nmean1_done, upto(l, 1))
                    eng.wait_ge(xn1T_ready, upto(l - 1, 2))
                    apply_norm(l, 0, hA, xn1, ln1_applied)
                if nx:
                    eng.wait_ge(vst_ready, upto(p, 1))
                    eng.wait_ge(pv_ready, upto(p - 1, 2))
                    act(vst[:], SA1[:, 1, 0:2 * FB].rearrange("p (k n) -> p k n", k=2), ACT.Copy).then_inc(vst_copied, 1)
                if exists(l):
                    for kb, slot in ((0, SB), (1, SCC)):
                        eng.wait_ge(xn1T_ready, upto(l, 2, kb + 1))
                        if kb == 0:
                            eng.wait_ge(qkv_ready, upto(l - 1, 6))
                        transposed_copy(slot, xn1T, kb).then_inc(xn1T_copied, 1)

            eng.wait_ge(ffn_const, 16 * NFFN)
            run(eng, iteration)

            eng.wait_ge(cdve, 2)
            act(cg[:, 1, :], cg[:, 0, :], ACT.Exp).then_inc(cact, 1)
            eng.wait_ge(cdve, CHID)
            for par in range(2):
                src = chp[:, 0].rearrange("p m (c b) -> p m c b", b=NB)[:, :, par:NCLS:2, :]
                dst = chz0[:, par].rearrange("p m (c b) -> p m c b", b=NB)[:, :, par:NCLS:2, :]
                act(dst, src, ACT.Gelu).then_inc(cact, 1)
            for e in range(3):
                src = chp[:, 1, :, 2 * NB * e:2 * NB * e + 2 * NB]
                act(chz1[:, e, :, 2 * NB * e:2 * NB * e + 2 * NB], src, ACT.Gelu).then_inc(cact, 1)

        @block.vector
        def _(eng):
            tt, ts, stt = eng.tensor_tensor, eng.tensor_scalar, eng.scalar_tensor_tensor
            eng.memset(counts[:], 0.0)
            eng.memset(rank_base[:], 0.0).then_inc(base_done, 1)

            def score(b):
                eng.wait_ge(x_loaded, upto(b, 16))
                if is_at(b, 0):
                    eng.wait_ge(tok_const, 16 * NTOKC)
                for c in range(NSC):
                    ins = eng.tensor_tensor_reduce(score_junk[:, c, :], xs[:, c, :], wtok[:], 1.0, 0.0,
                                                   ALU.mult, ALU.add, score_raw[:, c:c + 1])
                ins.then_inc(score_step, 1)
                eng.wait_ge(score_step, upto(b, 1))
                eng.wait_ge(score_stored, upto(b - 1, 16))
                eng.wait_ge(rank_step, upto(b - 1, NSC + 1))
                ts(score_col[:], score_raw[:], btok[:, 0:1], None, ALU.add).then_inc(score_done, 1)

            def rank(b):
                eng.wait_ge(row_loaded, upto(b, 16))
                eng.wait_ge(score_done, upto(b, 1))
                for c in range(NSC):
                    a = SC * c
                    s = score_col[:, c:c + 1]
                    if c >= 2:
                        eng.wait_ge(rank_step, upto(b, NSC + 1, c - 1))
                    if c >= 1:
                        ts(cmp_junk[:, c % 2, 0:a], score_row[:, 0:a], s, None, ALU.is_ge, ALU.add,
                           accum_out=counts[:, 0, c:c + 1])
                    ts(cmp_junk[:, c % 2, a:], score_row[:, a:], s, None, ALU.is_gt, ALU.add,
                       accum_out=counts[:, 1, c:c + 1])
                    ins = stt(tie_junk[:, c % 2, :], score_row[:, a:a + SC], s, lower[:],
                              ALU.is_equal, ALU.mult, accum_out=counts[:, 2, c:c + 1])
                    ins.then_inc(rank_step, 1)
                eng.wait_ge(rank_step, upto(b, NSC + 1, NSC))
                eng.tensor_reduce(rank_sum[:], counts[:].rearrange("p k c -> p c k"), AX.X, ALU.add).then_inc(rank_step, 1)
                eng.wait_ge(rank_step, upto(b, NSC + 1))
                eng.wait_ge(scattered, upto(b - 1, 16 * NSC))
                eng.wait_ge(base_done, upto(b, 1, 1))
                ts(rank_idx[:], rank_sum[:], rank_base[:, 0:1], None, ALU.add).then_inc(rank_done, 1)
                eng.wait_ge(rank_done, upto(b, 1))
                ts(rank_base[:], rank_base[:], float(NTOK), None, ALU.add).then_inc(base_done, 1)

            def norm_stats(b, which, src, step):
                for j in range(NT):
                    ins = eng.bn_stats(stats[:, which, j, :], src[:, j, :])
                ins.then_inc(step, 1)
                eng.wait_ge(step, upto(b, 3, 1))
                passed(eng)
                for j in range(NT):
                    ins = eng.bn_aggr(meanvar[:, which, j, :], stats[:, which, j, :])
                ins.then_inc(step, 1)
                eng.wait_ge(step, upto(b, 3, 2))
                eng.wait_ge((ln1_applied, ln2_applied)[which], upto(b - 1, 1))
                ts(vareps[:, which, :], meanvar[:, which, :, 1], EPS, None, ALU.add).then_inc(step, 1)

            def norm_mean(b, which, rstd_done, sem):
                eng.wait_ge(rstd_done, upto(b, 1))
                stt(nmean[:, which, :], meanvar[:, which, :, 0], -1.0, rstd[:, which, :],
                           ALU.mult, ALU.mult).then_inc(sem, 1)

            def maxima(b, j):
                slot = (SB, SCC)[j % 2]
                eng.wait_ge(logits_ready, upto(b, NT, j + 1))
                if j >= 2:
                    eng.wait_ge(exp_done, upto(b, NT, j - 1))
                else:
                    eng.wait_ge(exp_done, upto(b - 1, NT))
                eng.tensor_reduce(smax[:, j % 2, :].rearrange("p (k h) -> p k h", k=2),
                                              slot[0:TT, :, 0:384].rearrange("p k (h s) -> p k h s", s=64),
                                              AX.X, ALU.max).then_inc(max_step, 1)
                eng.wait_ge(max_step, upto(b, NT, j + 1))
                ts(nmax[:, j % 2, :], smax[:, j % 2, :], -SCALE, None, ALU.mult).then_inc(max_done, 1)

            def normalise(b, j):
                eng.wait_ge(exp_done, upto(b, NT, j + 1))
                eng.reciprocal(rden[:, j % 2, :], den[:, j % 2, :]).then_inc(rden_done, 1)
                eng.wait_ge(rden_done, upto(b, NT, j + 1))
                e = E[:, j % 2].rearrange("p q (r s) -> p (q r) s", r=2)
                tt(e, e, rden[:, j % 2, :].unsqueeze(2).to_broadcast([TT, NH, 64]), ALU.mult).then_inc(norm_done, 1)

            def iteration(i):
                n, l, p = i + 3, i + 2, i + 1
                at, nx = exists(i), exists(p)
                if at:
                    maxima(i, 0)
                    maxima(i, 1)
                    normalise(i, 0)
                    maxima(i, 2)
                    normalise(i, 1)
                if exists(n):
                    score(n)
                if at:
                    maxima(i, 3)
                    normalise(i, 2)
                    maxima(i, 4)
                    normalise(i, 3)
                    normalise(i, 4)
                    for kb, num, tail in ((0, SA0, SA1), (1, SB, SCC)):
                        eng.wait_ge(pv_ready, upto(i, 2, kb + 1))
                        tt(halves(tailv[:, kb, :]), both(tail, FB), halves(vT[:, kb, :]), ALU.mult).then_inc(tail_done, 1)
                        eng.wait_ge(tail_done, upto(i, 2, kb + 1))
                        eng.wait_ge(proj_ready, upto(i - 1, 2))
                        tt(halves(outT[:, kb, :]), both(num, FB), halves(tailv[:, kb, :]), ALU.add).then_inc(outT_done, 1)
                    eng.wait_ge(proj_ready, upto(i, 2, 1))
                    eng.wait_ge(hR_loaded, upto(i, 16))
                    eng.wait_ge(h1b_done, upto(i - 1, 1))
                    eng.wait_ge(ln2_applied, upto(i - 1, 1))
                    eng.wait_ge(cls_stored, upto(i - 1, 16))
                    tt(h1[:, 0:4, :].rearrange("p (k j) d -> p k (j d)", k=2), SA0[0:TT, :, 0:2 * D],
                                        hR[:, 0:4, :].rearrange("p (k j) d -> p k (j d)", k=2), ALU.add).then_inc(residual_done, 1)
                    eng.wait_ge(proj_ready, upto(i, 2, 2))
                    tt(h1[:, 4, :], SA1[0:TT, 0, 0:D], hR[:, 4, :], ALU.add).then_inc(residual_done, 1)
                    eng.wait_ge(residual_done, upto(i, 2))
                    norm_stats(i, 1, h1, ln_stats2)
                for g in range(8):
                    if nx:
                        if g >= 2:
                            eng.wait_ge(contracted, upto(p, 8, g - 1))
                        for q in range(3):
                            eng.wait_ge(kr_ready, upto(p, 24, 3 * g + q + 1))
                            eng.wait_ge(vr_copied, upto(p, 12, 3 * (g // 2) + q + 1))
                            slot = (SA0, SA1)[(3 * g + q) % 2]
                            tt(halves(outer[:, g % 2, q, :]), both(slot, 128),
                                             halves(vrows[:, g // 2 % 2, q, :]), ALU.mult).then_inc(outer_done, 1)
                    if at and g == 1:
                        norm_mean(i, 1, rstd2_done, nmean2_done)
                if nx:
                    eng.wait_ge(kprefix, upto(p, 4))
                    eng.wait_ge(qkv_copied, upto(p, 6))
                    eng.wait_ge(qk_placed, upto(p - 1, 16 * 3))
                    tt(qkT[:], qT[:], kvT[:, 0:2, :], ALU.mult).then_inc(qk_done, 1)
                    eng.wait_ge(kset_step, upto(p, 6))
                    eng.wait_ge(logits_ready, upto(p - 1, NT))
                    if is_at(p, 0):
                        eng.wait_ge(att_const, 16 * NATT)
                    for q in range(3):
                        rows = slice(32 * q, 32 * q + 32)
                        for par in range(2):
                            ins = ts(kbd[0:32, q:q + 4:3, 64 * par:64 * par + NSET], ksets[rows, :, 0:NSET],
                                     parity[rows, par:par + 1], None, ALU.mult)
                    ins.then_inc(kbd_done, 1)
                if exists(n):
                    rank(n)
                if exists(l):
                    eng.wait_ge(hA_loaded, upto(l, 16))
                    norm_stats(l, 0, hA, ln_stats1)
                if nx:
                    eng.wait_ge(vset_step, upto(p, 6))
                    eng.wait_ge(vst_ready, upto(p - 1, 1))
                    for par in range(2):
                        ins = ts(vexp[:, :, par, 0:NSET], vsets[:, :, 0:NSET], parity[:, par:par + 1], None, ALU.mult)
                    ins.then_inc(vexp_done, 1)
                if exists(l):
                    norm_mean(l, 0, rstd1_done, nmean1_done)
                if at:
                    eng.wait_ge(h1b_done, upto(i, 1))
                    eng.wait_ge(out_stored, upto(i - 1, 16 * 2))
                    eng.wait_ge(ffn2_ready, upto(i, 2, 1))
                    tt(osb[:, 0:4, :].rearrange("p (k j) d -> p k (j d)", k=2), SA0[0:TT, :, 0:2 * D],
                                h1b[:, 0:4, :].rearrange("p (k j) d -> p k (j d)", k=2), ALU.add).then_inc(added, 1)
                    eng.wait_ge(ffn2_ready, upto(i, 2, 2))
                    tt(osb[:, 4, :], SA1[0:TT, 0, 0:D], h1b[:, 4, :], ALU.add).then_inc(added, 1)

            eng.wait_ge(pool_const, NPOOL)
            run(eng, iteration)

            count = [0]

            def step(ins):
                ins.then_inc(cdve, 1)
                count[0] += 1
                eng.wait_ge(cdve, count[0])

            eng.wait_ge(cgate_ready, 1)
            eng.wait_ge(cls_const, 16 * NCC)
            gl = cg[:, 2, :]
            ins = tt(cgs[:], SB[0:48, 0, 0:2 * NCLS].rearrange("p (c o) -> p c o", o=2), pick[:], ALU.mult)
            ins.then_inc(cgs_done, 1)
            eng.wait_ge(cgs_done, 1)
            eng.tensor_reduce(gl, cgs[:].rearrange("p c o -> p o c"), AX.X, ALU.add).then_inc(cgs_done, 1)
            eng.wait_ge(cgs_done, 2)
            step(eng.tensor_reduce(cg[:, 3, 0:1], gl, AX.X, ALU.max))
            step(ts(cg[:, 0, :], gl, cg[:, 3, 0:1], None, ALU.subtract))
            eng.wait_ge(chid_ready, 1)
            for pair in range(2):
                hp = (SA0, SA1)[pair][:, 0, 0:NM * 48].rearrange("p (m t) -> p m t", m=NM)
                if pair == 0:
                    for e in range(3):
                        cols = slice(2 * NB * e, 2 * NB * e + 2 * NB)
                        step(tt(chp[:, 0, :, cols], hp[:, :, cols],
                                a1bs[:, e, :].unsqueeze(2).to_broadcast([128, NM, 2 * NB]), ALU.add))
                else:
                    for e in range(2):
                        for k in range(3):
                            cols = slice(NB * (e + 2 * k), NB * (e + 2 * k) + NB)
                            step(tt(chp[:, 1, :, cols], hp[:, :, cols],
                                    a1bs[:, 3 + e, :].unsqueeze(2).to_broadcast([128, NM, NB]), ALU.add))
            assert count[0] == CHID
            eng.wait_ge(cact, 1)
            e = cg[:, 1, :]
            step(eng.tensor_reduce(cg[:, 4, 0:1], e, AX.X, ALU.add))
            step(eng.reciprocal(cg[:, 4, 1:2], cg[:, 4, 0:1]))
            step(ts(cg[:, 5, :], e, cg[:, 4, 1:2], None, ALU.mult))
            step(eng.tensor_reduce(cg[:, 6, 0:1], cg[:, 5, :], AX.X, ALU.min))
            step(stt(cg[:, 7, :], cg[:, 5, :], cg[:, 6, 0:1], cg[:, 5, :], ALU.is_gt, ALU.mult))
            step(eng.tensor_reduce(cg[:, 8, 0:1], cg[:, 7, :], AX.X, ALU.add))
            step(ts(cg[:, 8, 1:2], cg[:, 8, 0:1], 1e-6, None, ALU.max))
            step(eng.reciprocal(cg[:, 9, 0:1], cg[:, 8, 1:2]))
            step(ts(cg[:, 10, :], cg[:, 7, :], cg[:, 9, 0:1], None, ALU.mult))
            eng.wait_ge(cout_ready, 1)
            eng.wait_ge(cls_io, 16 * NCLS)
            step(stt(c1[:], SCC[0:48, 0, 0:D], cg[:, 10, 0:1], cres[:], ALU.mult, ALU.add))
            step(stt(c0[:], SCC[0:48, 1, 0:D], cg[:, 10, 1:2], c1[:], ALU.mult, ALU.add))
            assert count[0] == CDVE

        @block.gpsimd
        def _(eng):
            eng.memset(wbil[:], 0.0).then_inc(pool_const, 1)
            eng.memset(neghalf[:], -0.5)
            for t_ in (xn1T, xn2T, ET):
                eng.memset(t_[:, :, T:TP], 0.0)
            eng.memset(vexp[:], 0.0)
            eng.memset(kbd[0:32, :, :], 0.0)
            eng.memset(chz0[:], 0.0)
            eng.memset(chz1[:], 0.0).then_inc(pool_const, 1)

            def running_sums(b, buf, step):
                w = 1
                k = 0
                while w < BLK:
                    v = buf.rearrange("p k (n t) -> p (k n) t", t=2 * w)
                    if k:
                        eng.wait_ge(step, upto(b, 4, k))
                    last = v[:, :, w - 1:w].to_broadcast([FB, 2 * TP // (2 * w), w]) if w > 1 else v[:, :, 0:1]
                    eng.tensor_tensor(v[:, :, w:2 * w], v[:, :, w:2 * w], last, ALU.add).then_inc(step, 1)
                    w, k = 2 * w, k + 1

            def set_sums(b, buf, sets, step):
                full = buf.rearrange("p k (n t) -> p k n t", t=BLK)
                passed(eng)
                eng.tensor_copy(sets[:, :, 0:32], full[:, :, 0:32, BLK - 1]).then_inc(step, 1)
                at, n = 0, 32
                for k in range(1, 6):
                    eng.wait_ge(step, upto(b, 6, k))
                    eng.tensor_tensor(sets[:, :, at + n:at + n + n // 2], sets[:, :, at:at + n:2],
                                              sets[:, :, at + 1:at + n:2], ALU.add).then_inc(step, 1)
                    at, n = at + n, n // 2

            def inv_root(b, which, stats_done, sem):
                eng.wait_ge(stats_done, upto(b, 3))
                eng.wait_ge((nmean1_done, nmean2_done)[which], upto(b - 1, 1))
                eng.wait_ge((ln1_applied, ln2_applied)[which], upto(b - 1, 1))
                eng.tensor_tensor(rstd[:, which, :], vareps[:, which, :], neghalf[:], ALU.pow).then_inc(sem, 1)

            def iteration(i):
                n, l, p = i + 3, i + 2, i + 1
                at, nx = exists(i), exists(p)
                if nx:
                    for kv in range(2):
                        blocks = slice(2 * kv, 2 * kv + 2)
                        eng.wait_ge(part1_done, upto(p, 2, kv + 1))
                        eng.tensor_tensor(rest[:, blocks, :], kvT[:, blocks, :],
                                                        parts[:, 0, blocks, :], ALU.subtract).then_inc(rest1_done, 1)
                    for kv in range(2):
                        blocks = slice(2 * kv, 2 * kv + 2)
                        eng.wait_ge(part2_done, upto(p, 2, kv + 1))
                        eng.tensor_tensor(parts[:, 2, blocks, :], rest[:, blocks, :],
                                                        parts[:, 1, blocks, :], ALU.subtract).then_inc(part3_done, 1)
                    running_sums(p, kvT[:, 0:2, :], kprefix)
                    eng.wait_ge(kprefix, upto(p, 4))
                    eng.wait_ge(kbd_done, upto(p - 1, 1))
                    set_sums(p, kvT[:, 0:2, :], ksets, kset_step)
                if at:
                    inv_root(i, 1, ln_stats2, rstd2_done)
                    eng.wait_ge(residual_done, upto(i, 2))
                    eng.wait_ge(added, upto(i - 1, 2))
                    eng.tensor_tensor(h1b[:], h1[:], b2row[:].unsqueeze(1).to_broadcast([TT, NT, D]), ALU.add).then_inc(h1b_done, 1)
                if nx:
                    eng.wait_ge(v_copied, upto(p, 2))
                    running_sums(p, vT[:], vprefix)
                    eng.wait_ge(vprefix, upto(p, 4))
                    eng.wait_ge(vexp_done, upto(p - 1, 1))
                    set_sums(p, vT[:], vsets, vset_step)
                if exists(l):
                    inv_root(l, 0, ln_stats1, rstd1_done)
                if exists(n):
                    eng.wait_ge(rank_done, upto(n, 1))
                    passed(eng)
                    for c in range(NSC):
                        eng.indirect_dma_start(
                            sorted_dram, bass.IndirectOffsetOnAxis(ap=rank_idx[:, c:c + 1], axis=0),
                            xs[:, c, :], None).then_inc(scattered, 16)

            eng.wait_ge(ffn_const, 16 * NFFN)
            run(eng, iteration)


def constants():
    import numpy as np
    one = 0x3F80
    r = np.arange(128)
    krep = np.zeros((FB, 2, 2, 128), np.uint16)
    vrep = np.zeros((FB, 2, 128), np.uint16)
    for part in range(3):
        for par in range(2):
            for e in range(HS):
                row = 32 * part + 16 * par + e
                vrep[row, par, r % 16 == e] = one
                for half in range(2):
                    krep[row, par, half, 8 * half + r // 16 == e] = one
    kbd = np.zeros((64, 6, 2, 64), np.float32)
    for par in range(2):
        kbd[16 * par:16 * par + 16, :, par, NSET] = 1
    ends, length = [], 1
    while length <= 32:
        ends += [(k + 1) * length for k in range(32 // length)]
        length *= 2
    assert len(ends) == NSET
    for b in range(32):
        kbd[32 + b, :, :, :NSET] = np.where(np.array(ends) > b, NEG, 0)
    onehot = np.zeros((32, 6, TP), np.float32)
    for t in range(T):
        if (t + 1) // BLK < 32:
            onehot[(t + 1) // BLK, :, t] = 1
    parity = np.zeros((FB, 2), np.float32)
    for row in range(FB):
        parity[row, row // 16 % 2] = 1
    tail = np.zeros((128, 32), np.float32)
    for par in range(2):
        tail[64 * par + NSET, 16 * par:16 * par + 16] = 1
    lower = (np.arange(SC)[None, :] < np.arange(SC)[:, None]).astype(np.uint16) * np.uint16(one)
    pick = np.zeros((48, NCLS, 2), np.float32)
    cls = np.zeros((5, 2, 48), np.float32)
    for row in range(48):
        c = row // NB
        pick[row, c] = 1
        cls[3 + c % 2, 0, row] = 1
        cls[c // 2, 1, row] = 1
    return {"c_ident": np.eye(128, dtype=np.float32), "c_krep": krep, "c_vrep": vrep,
            "c_kbd": kbd.reshape(64, 6, 128), "c_onehot": onehot, "c_parity": parity,
            "c_tail": tail, "c_lower": lower, "c_pick": pick, "c_cls": cls}


def layout(inp):
    import numpy as np
    f = {k: np.asarray(v) for k, v in inp.items()}
    ct = np.ascontiguousarray
    return {
        "x": f["x"], "tok_w": ct(f["L0_tok_w"].reshape(D)), "tok_b": f["L0_tok_b"],
        "wqkvT": ct(f["L0_attn_Wqkv"].T), "wprojT": ct(f["L0_attn_Wproj"].T),
        "wvT": ct(f["L0_attn_Wv"].T), "bv96": ct(np.tile(f["L0_attn_bv"], FB // HS).reshape(FB, 1)),
        "w1": f["L0_ffn_moe0_W1"], "b1c": ct(f["L0_ffn_moe0_b1"].reshape(NM, 128).T),
        "w2": f["L0_ffn_moe0_W2"], "b2": f["L0_ffn_moe0_b2"],
        "a1": f["L0_ffn_A1_W"], "a1bc": ct(f["L0_ffn_A1_b"].reshape(5, NM, 128).transpose(2, 0, 1)),
        "a2": f["L0_ffn_A2_W"], "a2b": f["L0_ffn_A2_b"], "gw": ct(f["L0_ffn_G_W"].reshape(NCLS, 2, FB, 2).transpose(2, 1, 0, 3)),
        **constants(),
    }


def kernel(**inputs):
    import concourse.bacc as bacc
    from concourse.bass_utils import run_bass_kernel_spmd

    nc = bacc.Bacc("TRN2", target_bir_lowering=False, num_devices=1)
    arrays = layout(inputs)
    aps = [nc.dram_tensor(name, list(a.shape), mybir.dt.from_np(a.dtype), kind="ExternalInput").ap()
           for name, a in arrays.items()]
    out = nc.dram_tensor("out", [NB, T, D], F32, kind="ExternalOutput").ap()
    build(nc, *aps, out)
    r = run_bass_kernel_spmd(nc, [arrays], core_ids=[0])
    return r.results[0]["out"]
```

```python
from contextlib import ExitStack

import concourse.bass as bass
import concourse.mybir as mybir

F32 = mybir.dt.float32
BF16 = mybir.dt.bfloat16
U32 = mybir.dt.uint32
U16 = mybir.dt.uint16
ALU = mybir.AluOpType
ACT = mybir.ActivationFunctionType
AX = mybir.AxisListType

NB, NTOK, D = 8, 750, 192
T = int(round(NTOK * 0.7))
NH, HS = 12, 16
BLK = 16
TP = -(-T // BLK) * BLK
NBLK = TP // BLK
CH = TP // 2
TT, NT = 105, 5
SC, NSC = 125, 6
FB = 96
HID = 768
NM = HID // 128
NCLS = 6
NSET = 63
EPS = 1e-5
SCALE = 0.25
NEG = -1e30
assert NT * TT == T and NSC * SC == NTOK

NTOKC, NQKV, NVAL, NATT, NFFN, NCC, NPOOL = 3, 1, 7, 6, 4, 7, 2
CHID, CDVE, CGELU = 11, 22, 6

NU = 16
NKR, NVR = 3 * NU, 3 * NU // 2
NF1 = 2 * NM
NXT = 4
FILL = {5: (0, 1), 6: (2, 3), 7: (4,), 8: (5,), 9: (6,), 10: (7,), 11: (8,), 12: (9,), 13: (10,), 14: (11,), 15: (12,)}
NFILL = NXT + NF1


def unit(u):
    return u // 8, u // 4 % 2, u // 2 % 2, u % 2


def copies_after(u):
    nxt = 3 * (u // 2 + 1)
    return [k for k in ((nxt, nxt + 1), (nxt + 2,))[u % 2] if k < NVR]


def fill_after(u):
    return FILL.get(u, ())


def left_fill():
    return range(sum(len(f) for f in FILL.values()), NFILL)


def upto(b, per, k=None):
    v = b * per + (per if k is None else k)
    return max(v, 0) if isinstance(v, int) else v


def is_at(b, n):
    return isinstance(b, int) and b == n


def exists(b):
    return not isinstance(b, int) or 0 <= b < NB


def build(nc, x, tok_w, tok_b, wqkvT, wprojT, wvT, bv96, w1, b1c, w2, b2, a1, a1bc, a2, a2b, gw,
          c_ident, c_krep, c_vrep, c_kbd, c_onehot, c_parity, c_tail, c_lower, c_pick, c_cls, out):
    ctx = ExitStack()
    with ctx:
        def sb(name, shape, dt=F32):
            return ctx.enter_context(nc.sbuf_tensor(name, shape, dt))

        def sem(name):
            return ctx.enter_context(nc.semaphore(name))

        ident = sb("ident", [128, 128])
        krep = sb("krep", [FB, 2, 2, 128], BF16)
        vrep = sb("vrep", [FB, 2, 128], BF16)
        parity = sb("parity", [FB, 2])
        tailsel = sb("tailsel", [128, 32])
        lower = sb("lower", [SC, SC], BF16)
        pick = sb("pick", [48, NCLS, 2])
        clsrow = sb("clsrow", [5, 2, 48])
        neghalf = sb("neghalf", [TT, NT])
        wtok = sb("wtok", [SC, D])
        btok = sb("btok", [SC, 1])
        wqkv = sb("wqkv", [FB, 2, 3 * D])
        wproj = sb("wproj", [FB, 2, D])
        wbil = sb("wbil", [128, 2, 2, 32])
        bvcol = sb("bvcol", [FB, 1])
        w1s = sb("w1s", [FB, 2, HID])
        b1s = sb("b1s", [128, NM])
        w2s = sb("w2s", [128, NM, D])
        b2row = sb("b2row", [TT, D])
        a1bs = sb("a1bs", [128, 5, NM])
        a2bs = sb("a2bs", [5, D])
        gws = sb("gws", [FB, 2, NCLS, 2])

        xs = sb("xs", [SC, NSC, D])
        score_junk = sb("score_junk", [SC, NSC, D], BF16)
        score_raw = sb("score_raw", [SC, NSC])
        score_col = sb("score_col", [SC, NSC])
        score_row = sb("score_row", [SC, NTOK])
        cmp_junk = sb("cmp_junk", [SC, 2, NTOK], BF16)
        tie_junk = sb("tie_junk", [SC, 2, SC], BF16)
        counts = sb("counts", [SC, 3, NSC])
        rank_sum = sb("rank_sum", [SC, NSC])
        rank_base = sb("rank_base", [SC, 1])
        rank_idx = sb("rank_idx", [SC, NSC], U32)

        hA = sb("hA", [TT, NT, D])
        xn1 = sb("xn1", [TT, NT, D])
        xn1T = sb("xn1T", [FB, 2, TP])
        xn2T = sb("xn2T", [FB, 2, TP])
        stats = sb("stats", [TT, 2, NT, 6])
        meanvar = sb("meanvar", [TT, 2, NT, 2])
        vareps = sb("vareps", [TT, 2, NT])
        rstd = sb("rstd", [TT, 2, NT])
        nmean = sb("nmean", [TT, 2, NT])

        kvT = sb("kvT", [FB, 4, TP])
        qT = sb("qT", [FB, 2, TP])
        qkT = sb("qkT", [FB, 2, TP])
        region = sb("region", [128, 28 * TP])
        outer = region[:, 0:6 * TP].rearrange("p (g q t) -> p g q t", g=4, q=3)
        vrows = region[:, 6 * TP:12 * TP].rearrange("p (g q t) -> p g q t", g=4, q=3)
        stack = region[0:FB, 12 * TP:18 * TP].bitcast(BF16).rearrange("p (q t) -> p q t", q=12)
        parts = region[0:FB, 18 * TP:24 * TP].bitcast(BF16).rearrange("p (s k t) -> p s k t", s=3, k=4)
        rest = region[0:FB, 24 * TP:28 * TP].rearrange("p (k t) -> p k t", k=4)
        a1s = region[0:FB, 0:10 * HID].rearrange("p (a k n) -> p a k n", a=5, k=2)
        a2s = region[:, 10 * HID:10 * HID + 5 * NM * D].rearrange("p (a m n) -> p a m n", a=5, m=NM)
        vT = sb("vT", [FB, 2, TP])
        ksets = sb("ksets", [FB, 2, 64])
        vsets = sb("vsets", [FB, 2, 64])
        vexp = sb("vexp", [FB, 2, 2, 64])
        kbd = sb("kbd", [FB, 6, 128])
        vst = sb("vst", [128, 2, FB])
        X = sb("X", [FB, 6, TP])

        smax = sb("smax", [TT, 2, NH])
        den = sb("den", [TT, 2, NH])
        rden = sb("rden", [TT, 2, NH])
        E = sb("E", [TT, 3, 6, 128])
        ET = sb("ET", [128, 6, TP])
        tailv = sb("tailv", [FB, 2, TP])
        outT = sb("outT", [FB, 2, TP])
        hR = sb("hR", [TT, NT, D])
        h1 = sb("h1", [TT, NT, D])
        h1b = sb("h1b", [TT, NT, D])
        xn2 = sb("xn2", [TT, NT, D])
        hid = ET
        osb = sb("osb", [TT, NT, D])

        cx = sb("cx", [FB, 2, NCLS, NB])
        cres = sb("cres", [48, D])
        chp = sb("chp", [128, 2, NM, 48])
        chz0 = sb("chz0", [128, 2, NM, 48])
        chz1 = sb("chz1", [128, 3, NM, 48])
        cg = sb("cg", [48, 12, 2])
        cgs = sb("cgs", [48, NCLS, 2])
        c0 = sb("c0", [48, D])

        SA0 = ctx.enter_context(nc.psum_tensor("SA0", [128, 2, 512], F32))
        SA1 = ctx.enter_context(nc.psum_tensor("SA1", [128, 2, 512], F32))
        SB = ctx.enter_context(nc.psum_tensor("SB", [128, 2, 512], F32))
        SCC = ctx.enter_context(nc.psum_tensor("SCC", [128, 2, 512], F32))

        KR = (SA0[:, 0, 0:CH], SA0[:, 1, 0:CH], SA1[:, 0, 0:CH])
        VR = SA1[:, 1, 0:CH]
        ACC = (SCC[0:FB, 0, 0:CH], SCC[0:FB, 1, 0:CH])
        F = (SB[:, 0, :], SB[:, 1, :])

        score_dram = nc.dram_tensor("score_dram", [NB, NTOK], F32, kind="Internal").ap()
        sorted_dram = nc.dram_tensor("sorted_dram", [NB * NTOK, D], F32, kind="Internal").ap()
        sorted_b = sorted_dram.rearrange("(b n) d -> b n d", b=NB)
        cls_dram = nc.dram_tensor("cls_dram", [NB, NCLS, D], F32, kind="Internal").ap()

        x_loaded = sem("x_loaded")
        score_stored = sem("score_stored")
        row_loaded = sem("row_loaded")
        scattered = sem("scattered")
        hA_loaded = sem("hA_loaded")
        hR_loaded = sem("hR_loaded")
        k_stacked = sem("k_stacked")
        v_stacked = sem("v_stacked")
        q_placed = sem("q_placed")
        qk_placed = sem("qk_placed")
        cls_stored = sem("cls_stored")
        out_stored = sem("out_stored")
        tok_const = sem("tok_const")
        qkv_const = sem("qkv_const")
        val_const = sem("val_const")
        att_const = sem("att_const")
        ffn_const = sem("ffn_const")
        cls_const = sem("cls_const")
        cls_io = sem("cls_io")
        xn1T_ready = sem("xn1T_ready")
        qkv_ready = sem("qkv_ready")
        logits_ready = sem("logits_ready")
        attT_ready = sem("attT_ready")
        pv_ready = sem("pv_ready")
        proj_ready = sem("proj_ready")
        vr_ready = sem("vr_ready")
        kr_ready = sem("kr_ready")
        contracted = sem("contracted")
        xn2T_ready = sem("xn2T_ready")
        ffn1_ready = sem("ffn1_ready")
        ffn2_ready = sem("ffn2_ready")
        vst_ready = sem("vst_ready")
        ln1_applied = sem("ln1_applied")
        xn1T_copied = sem("xn1T_copied")
        qkv_copied = sem("qkv_copied")
        part1_done = sem("part1_done")
        part2_done = sem("part2_done")
        exp_done = sem("exp_done")
        attT_copied = sem("attT_copied")
        vr_copied = sem("vr_copied")
        v_copied = sem("v_copied")
        ln2_applied = sem("ln2_applied")
        xn2T_copied = sem("xn2T_copied")
        cx_copied = sem("cx_copied")
        gelu_done = sem("gelu_done")
        vst_copied = sem("vst_copied")
        score_step = sem("score_step")
        score_done = sem("score_done")
        rank_step = sem("rank_step")
        rank_done = sem("rank_done")
        base_done = sem("base_done")
        ln_stats1 = sem("ln_stats1")
        ln_stats2 = sem("ln_stats2")
        nmean1_done = sem("nmean1_done")
        nmean2_done = sem("nmean2_done")
        max_step = sem("max_step")
        centred = sem("centred")
        sum_done = sem("sum_done")
        rden_done = sem("rden_done")
        norm_done = sem("norm_done")
        tail_done = sem("tail_done")
        outT_done = sem("outT_done")
        residual_done = sem("residual_done")
        outer_done = sem("outer_done")
        qk_done = sem("qk_done")
        kbd_done = sem("kbd_done")
        vexp_done = sem("vexp_done")
        added = sem("added")
        pool_const = sem("pool_const")
        waits_passed = sem("waits_passed")
        rest1_done = sem("rest1_done")
        part3_done = sem("part3_done")
        kprefix = sem("kprefix")
        vprefix = sem("vprefix")
        kset_step = sem("kset_step")
        vset_step = sem("vset_step")
        rstd1_done = sem("rstd1_done")
        rstd2_done = sem("rstd2_done")
        h1b_done = sem("h1b_done")
        cgate_ready = sem("cgate_ready")
        chid_ready = sem("chid_ready")
        cout_ready = sem("cout_ready")
        cgs_done = sem("cgs_done")
        cdve = sem("cdve")
        cact = sem("cact")

        block = ctx.enter_context(nc.Block())

        def run(eng, iteration):
            for i in range(-3, 1):
                iteration(i)
            with eng.Fori(1, NB - 3) as i:
                iteration(i)
            for i in range(NB - 3, NB):
                iteration(i)

        def passed(eng):
            eng.sem_inc(waits_passed, 1)

        def both(ps, rows, n=CH):
            return ps[0:rows, :, 0:n]

        def halves(ap):
            return ap.rearrange("p (c t) -> p c t", c=2)

        @block.sync
        def _(eng):
            eng.dma_start(wtok[:], tok_w.rearrange("(o d) -> o d", o=1).to_broadcast([SC, D])).then_inc(tok_const, 16)
            eng.dma_start(btok[:], tok_b.rearrange("(o d) -> o d", o=1).to_broadcast([SC, 1])).then_inc(tok_const, 16)
            eng.dma_start(lower[:].bitcast(U16), c_lower).then_inc(tok_const, 16)

            def iteration(i):
                n, l, p = i + 3, i + 2, i + 1
                if exists(n):
                    eng.wait_ge(scattered, upto(n - 1, 16 * NSC))
                    eng.dma_start(xs[:], x[n].rearrange("(c p) d -> p c d", p=SC)).then_inc(x_loaded, 16)
                if exists(l):
                    eng.wait_ge(scattered, upto(l, 16 * NSC))
                    eng.wait_ge(ln1_applied, upto(l - 1, NT))
                    eng.wait_ge(ln_stats1, upto(l - 1, 3))
                    eng.dma_start(hA[:], sorted_b[l, 0:T].rearrange("(j p) d -> p j d", p=TT)).then_inc(hA_loaded, 16)
                if exists(i):
                    eng.wait_ge(residual_done, upto(i - 1, 2))
                    eng.dma_start(hR[:], sorted_b[i, 0:T].rearrange("(j p) d -> p j d", p=TT)).then_inc(hR_loaded, 16)

                def stack_up(kv, s):
                    for part in range(3):
                        for q in range(3):
                            eng.dma_start(stack[32 * part:32 * part + 32, 6 * kv + q:6 * kv + q + 4:3, :], parts[32 * q:32 * q + 32, part, 2 * kv:2 * kv + 2, :]).then_inc(s, 16)

                if exists(p):
                    eng.wait_ge(part3_done, upto(p, 2, 1))
                    eng.wait_ge(kr_ready, upto(p - 1, NKR))
                    stack_up(0, k_stacked)
                if exists(p):
                    eng.wait_ge(part3_done, upto(p, 2, 2))
                    eng.wait_ge(vr_ready, upto(p - 1, NVR))
                    stack_up(1, v_stacked)
                    eng.wait_ge(qkv_copied, upto(p, 6))
                    eng.wait_ge(logits_ready, upto(p - 1, NT))
                    for q in range(3):
                        eng.dma_start(X[0:32, q:q + 4:3, :], qT[32 * q:32 * q + 32, :, :]).then_inc(q_placed, 16)
                if exists(i):
                    eng.wait_ge(residual_done, upto(i, 2))
                    eng.dma_start(cls_dram[i], h1[0:NCLS, 0, :]).then_inc(cls_stored, 16)
                if exists(n):
                    eng.wait_ge(score_done, upto(n, 1))
                    eng.dma_start(score_dram[n].rearrange("(c p) -> p c", p=SC), score_col[:],
                                                  allow_slow_non_contiguous=True).then_inc(score_stored, 16)
                if exists(n):
                    eng.wait_ge(score_stored, upto(n, 16))
                    eng.wait_ge(rank_step, upto(n - 1, NSC + 1))
                    eng.dma_start(score_row[:], score_dram[n].rearrange("(o m) -> o m", o=1).to_broadcast([SC, NTOK])).then_inc(row_loaded, 16)
                if exists(p):
                    eng.wait_ge(qk_done, upto(p, 1))
                    for q in range(3):
                        eng.dma_start(X[32:64, q:q + 4:3, :], qkT[32 * q:32 * q + 32, :, :]).then_inc(qk_placed, 16)
                if exists(i):
                    eng.wait_ge(added, upto(i, 2))
                    ob = out[i].rearrange("(j p) d -> p j d", p=TT)
                    eng.dma_start(ob[:, 1:NT], osb[:, 1:NT]).then_inc(out_stored, 16)
                    eng.dma_start(ob[NCLS:TT, 0], osb[NCLS:TT, 0]).then_inc(out_stored, 16)

            run(eng, iteration)
            eng.wait_ge(cls_stored, upto(NB - 1, 16))
            for c in range(NCLS):
                eng.dma_start(cres[NB * c:NB * c + NB, :], cls_dram[:, c, :]).then_inc(cls_io, 16)
            eng.wait_ge(cdve, CDVE)
            for c in range(NCLS):
                eng.dma_start(out[:, c, :], c0[NB * c:NB * c + NB, :]).then_inc(cls_io, 16)
            eng.wait_ge(cls_io, 16 * 2 * NCLS)
            eng.wait_ge(out_stored, upto(NB - 1, 16 * 2))

        @block.tensor
        def _(eng):
            def mm(o, l, r, start=True, stop=True):
                return eng.matmul(o, l, r, start=start, stop=stop, skip_group_check=True)

            def logits(b, j, slot):
                if j == 0:
                    eng.wait_ge(q_placed, upto(b, 16 * 3))
                    eng.wait_ge(qk_placed, upto(b, 16 * 3))
                    eng.wait_ge(kbd_done, upto(b, 1))
                for h2 in range(6):
                    ins = mm(slot[0:TT, h2 // 3, (h2 % 3) * 128:(h2 % 3) * 128 + 128],
                             X[:, h2, TT * j:TT * j + TT], kbd[:, h2, :])
                ins.then_inc(logits_ready, 1)

            def project(b, k, slot):
                if k == 0:
                    eng.wait_ge(xn1T_copied, upto(b, NXT))
                col = (D, D + FB, 2 * D, 2 * D + FB, 0, FB)[k]
                for c in range(2):
                    for kb in range(2):
                        ins = mm(slot[0:FB, c, 0:CH], wqkv[:, kb, col:col + FB],
                                 xn1T[:, kb, CH * c:CH * c + CH], kb == 0, kb == 1)
                ins.then_inc(qkv_ready, 1)

            def att_transpose(b, j, slot):
                eng.wait_ge(norm_done, upto(b, NT, j + 1))
                for h2 in range(6):
                    ins = eng.transpose(slot[:, h2 // 3, (h2 % 3) * TT:(h2 % 3) * TT + TT],
                                        E[:, j % 3, h2, :], ident[0:TT, 0:TT])
                ins.then_inc(attT_ready, 1)

            def iteration(i):
                p, l = i + 1, i + 2
                at, nx = exists(i), exists(p)
                if at:
                    if nx:
                        eng.wait_ge(xn1T_copied, upto(p, NXT))
                    eng.wait_ge(gelu_done, upto(i - 1, NF1))
                    logits(i, 0, SB)
                    logits(i, 1, SCC)
                eng.wait_ge(added, upto(i - 1, 2))
                eng.wait_ge(outer_done, upto(i, NKR))
                eng.wait_ge(vst_copied, upto(i, 1))
                if nx:
                    if is_at(p, 0):
                        eng.wait_ge(qkv_const, 16 * NQKV)
                    project(p, 0, SA0)
                    project(p, 1, SA1)
                if at:
                    eng.wait_ge(centred, upto(i, NT, 1))
                    logits(i, 2, SB)
                if nx:
                    eng.wait_ge(qkv_copied, upto(p, 6, 1))
                    project(p, 2, SA0)
                    eng.wait_ge(qkv_copied, upto(p, 6, 2))
                if at:
                    att_transpose(i, 0, SA1)
                    eng.wait_ge(centred, upto(i, NT, 2))
                    logits(i, 3, SCC)
                if nx:
                    eng.wait_ge(qkv_copied, upto(p, 6, 3))
                    project(p, 3, SA0)
                if at:
                    eng.wait_ge(attT_copied, upto(i, NT, 1))
                    att_transpose(i, 1, SA1)
                    eng.wait_ge(centred, upto(i, NT, 3))
                    logits(i, 4, SB)
                if nx:
                    eng.wait_ge(qkv_copied, upto(p, 6, 4))
                    project(p, 4, SA0)
                if at:
                    eng.wait_ge(attT_copied, upto(i, NT, 2))
                    att_transpose(i, 2, SA1)
                if nx:
                    eng.wait_ge(qkv_copied, upto(p, 6, 5))
                    project(p, 5, SA0)
                if at:
                    eng.wait_ge(attT_copied, upto(i, NT, 3))
                    att_transpose(i, 3, SA1)
                if nx:
                    eng.wait_ge(qkv_copied, upto(p, 6, 6))
                if at:
                    att_transpose(i, 4, SA0)
                    for kb, num, tail in ((0, SA0, SA1), (1, SB, SCC)):
                        eng.wait_ge(attT_copied, upto(i, NT, 5))
                        eng.wait_ge(centred, upto(i, NT, 5))
                        for c in range(2):
                            for q in range(3):
                                mm(num[32 * q:32 * q + 32, c, 0:CH], vst[:, kb, 32 * q:32 * q + 32],
                                   ET[:, 3 * kb + q, CH * c:CH * c + CH])
                        for c in range(2):
                            for q in range(3):
                                ins = mm(tail[32 * q:32 * q + 32, c, 0:CH], tailsel[:],
                                         ET[:, 3 * kb + q, CH * c:CH * c + CH])
                        ins.then_inc(pv_ready, 1)

                def copy_v0(k):
                    c, kb, par, _ = unit(2 * (k // 3))
                    eng.wait_ge(vr_copied, upto(p, NVR, k))
                    mm(VR, vrep[:, par, :], stack[:, 6 + 3 * kb + k % 3, CH * c:CH * c + CH]).then_inc(vr_ready, 1)

                def copy_k(u):
                    c, kb, par, half = unit(u)
                    for q in range(3):
                        if 3 * u + q >= 3:
                            eng.wait_ge(outer_done, upto(p, NKR, 3 * u + q - 2))
                        mm(KR[q], krep[:, par, half, :], stack[:, 3 * kb + q, CH * c:CH * c + CH]).then_inc(kr_ready, 1)

                def contract(u):
                    c, kb, par, half = unit(u)
                    eng.wait_ge(outer_done, upto(p, NKR, 3 * u + 3))
                    if u == 4 and at:
                        eng.wait_ge(residual_done, upto(i, 2))
                    if u == 8 or u == 12:
                        eng.wait_ge(v_copied, upto(p, 4, u // 4 - 1))
                    for q in range(3):
                        ins = mm(ACC[u // 4 % 2][32 * q:32 * q + 32, :], wbil[:, half, par, :],
                                 outer[:, u % 4, q, :], u % 4 == 0, u % 4 == 3)
                    ins.then_inc(contracted, 1)

                def fill(f):
                    if f < NXT:
                        g, kb = f // 2, f % 2
                        if f == 0:
                            eng.wait_ge(residual_done, upto(i, 2))
                        if f >= 2:
                            eng.wait_ge(xn2T_copied, upto(i, NXT, f - 1))
                        eng.wait_ge(ln2_applied, upto(i, NT, (3, 5)[g]))
                        for j in range(3 * g, (3, 5)[g]):
                            ins = eng.transpose(F[f % 2][0:FB, (j % 3) * TT:(j % 3) * TT + TT],
                                                xn2[:, j, FB * kb:FB * kb + FB], ident[0:TT, 0:TT])
                        ins.then_inc(xn2T_ready, 1)
                    else:
                        c, m = (f - NXT) // NM, (f - NXT) % NM
                        eng.wait_ge(xn2T_copied, upto(i, NXT))
                        if f >= NXT + 2:
                            eng.wait_ge(gelu_done, upto(i, NF1, f - NXT - 1))
                        for kb in range(2):
                            ins = mm(F[f % 2][:, 0:CH], w1s[:, kb, 128 * m:128 * m + 128],
                                     xn2T[:, kb, CH * c:CH * c + CH], kb == 0, kb == 1)
                        ins.then_inc(ffn1_ready, 1)

                def out_project():
                    eng.wait_ge(outT_done, upto(i, 2))
                    for j in range(NT):
                        o = SB[0:TT, j // 2, (j % 2) * D:(j % 2) * D + D] if j < 4 else SCC[0:TT, 1, 0:D]
                        for kb in range(2):
                            ins = mm(o, outT[:, kb, TT * j:TT * j + TT], wproj[:, kb, :], kb == 0, kb == 1)
                        if j >= 3:
                            ins.then_inc(proj_ready, 1)

                if nx:
                    if is_at(p, 0):
                        eng.wait_ge(val_const, 16 * NVAL)
                    eng.wait_ge(qkv_copied, upto(p, 6))
                    if at:
                        eng.wait_ge(outT_done, upto(i, 2, 1))
                    eng.wait_ge(k_stacked, upto(p, 16 * 9))
                    eng.wait_ge(v_stacked, upto(p, 16 * 9))
                    for k in range(3):
                        copy_v0(k)
                    copy_k(0)
                if at:
                    out_project()
                if nx:
                    for u in range(NU):
                        if u >= 1:
                            copy_k(u)
                        for k in copies_after(u)[:1]:
                            copy_v0(k)
                        if u >= 1:
                            contract(u - 1)
                        if at:
                            for f in fill_after(u):
                                fill(f)
                        for k in copies_after(u)[1:]:
                            copy_v0(k)
                    contract(NU - 1)
                if at:
                    for f in left_fill() if nx else range(NFILL):
                        fill(f)
                if exists(l):
                    if is_at(l, 0):
                        eng.wait_ge(att_const, 16 * NATT)
                    if nx:
                        eng.wait_ge(v_copied, upto(p, 4))
                    if at:
                        eng.wait_ge(residual_done, upto(i, 2))
                    for s in range(NXT):
                        kb, g = s // 2, s % 2
                        if s >= 2:
                            eng.wait_ge(xn1T_copied, upto(l, NXT, s - 1))
                        eng.wait_ge(ln1_applied, upto(l, NT))
                        for j in range(3 * g, (3, 5)[g]):
                            ins = eng.transpose(SCC[0:FB, g, (j % 3) * TT:(j % 3) * TT + TT],
                                                xn1[:, j, FB * kb:FB * kb + FB], ident[0:TT, 0:TT])
                        ins.then_inc(xn1T_ready, 1)
                if at:
                    if nx:
                        eng.wait_ge(outer_done, upto(p, NKR))
                    for j in range(NT):
                        o = SA0[0:TT, j // 2, (j % 2) * D:(j % 2) * D + D] if j < 4 else SA1[0:TT, 0, 0:D]
                        eng.wait_ge(gelu_done, upto(i, NF1, NM if j < 2 else NF1))
                        for m in range(NM):
                            ins = mm(o, hid[:, m, TT * j:TT * j + TT], w2s[:, m, :], m == 0, m == NM - 1)
                        if j >= 3:
                            ins.then_inc(ffn2_ready, 1)
                if nx:
                    eng.wait_ge(vr_copied, upto(p, NVR))
                    eng.wait_ge(vexp_done, upto(p, 1))
                    for kb in range(2):
                        ins = eng.transpose(SA1[:, 1, FB * kb:FB * kb + FB],
                                            vexp[:, kb, :, :], ident[0:FB, 0:FB])
                    ins.then_inc(vst_ready, 1)
                if is_at(l, 0):
                    eng.wait_ge(ffn_const, 16 * NFFN)

            run(eng, iteration)

            eng.wait_ge(cls_const, 16 * NCC)
            eng.wait_ge(cx_copied, upto(NB - 1, 1))
            eng.wait_ge(gelu_done, upto(NB - 1, NF1))
            cxv = [cx[:, kb] for kb in range(2)]
            for kb in range(2):
                ins = mm(SB[0:48, 0, 0:2 * NCLS], cxv[kb].rearrange("p c b -> p (c b)"), gws[:, kb, :, :], kb == 0, kb == 1)
            ins.then_inc(cgate_ready, 1)
            eng.wait_ge(added, upto(NB - 1, 2))
            for pair in range(2):
                hp = (SA0, SA1)[pair][:, 0, 0:NM * 48].rearrange("p (m c b) -> p m c b", m=NM, b=NB)
                for e in range(3 - pair):
                    a = e if pair == 0 else 3 + e
                    cs = slice(2 * e, 2 * e + 2) if pair == 0 else slice(e, NCLS, 2)
                    for m in range(NM):
                        for kb in range(2):
                            ins = mm(hp[:, m, cs, :], a1s[:, a, kb, 128 * m:128 * m + 128],
                                     cxv[kb][:, cs, :], kb == 0, kb == 1)
            ins.then_inc(chid_ready, 1)
            eng.wait_ge(cact, CGELU)
            for pair in range(2):
                o = SCC[0:48, pair, 0:D]
                mm(o, clsrow[:, pair, :], a2bs[:], True, False)
                for e in range(2 + pair):
                    a = 3 + e if pair == 0 else e
                    hz = (chz0, chz1)[pair]
                    for m in range(NM):
                        ins = mm(o, hz[:, e, m, :], a2s[:, a, m, :], False, e == 1 + pair and m == NM - 1)
            ins.then_inc(cout_ready, 1)

        @block.scalar
        def _(eng):
            def act(o, i_, f, **kw):
                return eng.activation(o, i_, f, **kw)

            eng.dma_start(ident[:], c_ident).then_inc(att_const, 16)
            eng.dma_start(parity[:], c_parity).then_inc(att_const, 16)
            eng.dma_start(tailsel[:], c_tail).then_inc(att_const, 16)
            eng.dma_start(X[64:96, :, :], c_onehot).then_inc(att_const, 16)
            eng.dma_start(kbd[32:96, :, :], c_kbd).then_inc(att_const, 16)
            eng.dma_start(wproj[:], wprojT.rearrange("(k p) n -> p k n", p=FB)).then_inc(att_const, 16)
            eng.dma_start(wqkv[:], wqkvT.rearrange("(k p) n -> p k n", p=FB)).then_inc(qkv_const, 16)
            eng.dma_start(krep[:].bitcast(U16), c_krep).then_inc(val_const, 16)
            eng.dma_start(vrep[:].bitcast(U16), c_vrep).then_inc(val_const, 16)
            eng.dma_start(bvcol[:], bv96).then_inc(val_const, 16)
            eng.wait_ge(pool_const, 1)
            for half in range(2):
                for par in range(2):
                    eng.dma_start(wbil[:, half, par, HS * par:HS * par + HS], wvT[128 * half:128 * half + 128, :]).then_inc(val_const, 16)
            eng.dma_start(w1s[:], w1.rearrange("(k p) n -> p k n", p=FB)).then_inc(ffn_const, 16)
            eng.dma_start(b1s[:], b1c).then_inc(ffn_const, 16)
            eng.dma_start(w2s[:], w2.rearrange("(m p) n -> p m n", p=128)).then_inc(ffn_const, 16)
            eng.dma_start(b2row[:], b2.rearrange("(o d) -> o d", o=1).to_broadcast([TT, D])).then_inc(ffn_const, 16)

            def transposed_copy(bank, dst, kb, g):
                a, z = ((0, 3), (3, 5))[g]
                return act(dst[:, kb, a * TT:z * TT], bank[0:FB, 0:(z - a) * TT], ACT.Copy)

            def exps(b, j):
                eng.wait_ge(centred, upto(b, NT, j + 1))
                act(E[:, j % 3], E[:, j % 3], ACT.Exp, scale=SCALE).then_inc(exp_done, 1)

            def copy_projection(b, k):
                slot = (SA0, SA1, SA0, SA0, SA0, SA0)[k]
                eng.wait_ge(qkv_ready, upto(b, 6, k + 1))
                if k == 0:
                    eng.wait_ge(kset_step, upto(b - 1, 6))
                    eng.wait_ge(part3_done, upto(b - 1, 2))
                    eng.wait_ge(qk_done, upto(b - 1, 1))
                if k == 4:
                    eng.wait_ge(q_placed, upto(b - 1, 16 * 3))
                dst = kvT[:, k, :] if k < 4 else qT[:, k - 4, :]
                act(halves(dst), both(slot, FB), ACT.Copy).then_inc(qkv_copied, 1)

            def part(b, kv, n):
                if n == 0:
                    eng.wait_ge(qkv_copied, upto(b, 6, 2 * kv + 2))
                    eng.wait_ge((v_stacked if kv else k_stacked), upto(b - 1, 16 * 9))
                    act(parts[:, 0, 2 * kv:2 * kv + 2, :], kvT[:, 2 * kv:2 * kv + 2, :], ACT.Copy).then_inc(part1_done, 1)
                else:
                    eng.wait_ge(rest1_done, upto(b, 2, kv + 1))
                    act(parts[:, 1, 2 * kv:2 * kv + 2, :], rest[:, 2 * kv:2 * kv + 2, :], ACT.Copy).then_inc(part2_done, 1)

            def copy_attT(b, j):
                slot = (SA1, SA1, SA1, SA1, SA0)[j]
                eng.wait_ge(attT_ready, upto(b, NT, j + 1))
                if j == 0:
                    eng.wait_ge(ffn2_ready, upto(b - 1, 2))
                act(
                    ET[:, :, TT * j:TT * j + TT].rearrange("p (k q) t -> p k q t", k=2),
                    slot[:, :, 0:3 * TT].rearrange("p k (q t) -> p k q t", q=3), ACT.Copy).then_inc(attT_copied, 1)

            def apply_norm(which, src, dst, sem, tiles):
                for j in tiles:
                    act(dst[:, j, :], src[:, j, :], ACT.Identity, scale=rstd[:, which, j:j + 1],
                        bias=nmean[:, which, j:j + 1]).then_inc(sem, 1)

            def iteration(i):
                p, l = i + 1, i + 2
                at, nx = exists(i), exists(p)
                if at:
                    exps(i, 0)
                if nx:
                    copy_projection(p, 0)
                if at:
                    exps(i, 1)
                if nx:
                    copy_projection(p, 1)
                    part(p, 0, 0)
                if at:
                    exps(i, 2)
                if nx:
                    copy_projection(p, 2)
                if at:
                    copy_attT(i, 0)
                if nx:
                    part(p, 0, 1)
                    copy_projection(p, 3)
                    part(p, 1, 0)
                if at:
                    exps(i, 3)
                    copy_attT(i, 1)
                if nx:
                    copy_projection(p, 4)
                    part(p, 1, 1)
                if at:
                    exps(i, 4)
                    copy_attT(i, 2)
                if nx:
                    copy_projection(p, 5)
                if at:
                    copy_attT(i, 3)
                    copy_attT(i, 4)
                if is_at(i, NB - 1):
                    eng.wait_ge(contracted, upto(i, NU))
                    eng.dma_start(a1s[:], a1.rearrange("a (k p) n -> p a k n", p=FB)).then_inc(cls_const, 16)
                    eng.dma_start(a1bs[:], a1bc).then_inc(cls_const, 16)
                    eng.dma_start(a2s[:], a2.rearrange("a (m p) n -> p a m n", p=128)).then_inc(cls_const, 16)
                    eng.dma_start(a2bs[:], a2b).then_inc(cls_const, 16)
                    eng.dma_start(gws[:], gw).then_inc(cls_const, 16)
                    eng.dma_start(pick[:], c_pick).then_inc(cls_const, 16)
                    eng.dma_start(clsrow[:], c_cls).then_inc(cls_const, 16)

                def copy_v0(k):
                    pair = k // 3
                    eng.wait_ge(vr_ready, upto(p, NVR, k + 1))
                    if pair < 4:
                        eng.wait_ge(outer_done, upto(p - 1, NKR, 6 * (pair + 5)))
                    else:
                        eng.wait_ge(outer_done, upto(p, NKR, 6 * (pair - 3)))
                    act(vrows[:, pair % 4, k % 3, :], VR, ACT.Copy).then_inc(vr_copied, 1)

                def copy_values(s):
                    c, kb = s // 2, s % 2
                    eng.wait_ge(contracted, upto(p, NU, 4 * s + 4))
                    if s == 0:
                        eng.wait_ge(outT_done, upto(p - 1, 2))
                        eng.wait_ge(tail_done, upto(p - 1, 2))
                        eng.wait_ge(vset_step, upto(p - 1, 6))
                        if is_at(p, 0):
                            eng.wait_ge(val_const, 16 * NVAL)
                    act(vT[:, kb, CH * c:CH * c + CH], ACC[s % 2], ACT.Identity, bias=bvcol[:, 0:1]).then_inc(v_copied, 1)

                def fill(f):
                    if f < NXT:
                        eng.wait_ge(xn2T_ready, upto(i, NXT, f + 1))
                        if f == 0:
                            eng.wait_ge(ffn1_ready, upto(i - 1, NF1))
                            eng.wait_ge(cx_copied, upto(i - 1, 1))
                        transposed_copy(F[f % 2], xn2T, f % 2, f // 2).then_inc(xn2T_copied, 1)
                        if f == NXT - 1:
                            eng.wait_ge(xn2T_copied, upto(i, NXT))
                            act(cx[:, :, :, i], xn2T[:, :, 0:NCLS], ACT.Copy).then_inc(cx_copied, 1)
                    else:
                        c, m = (f - NXT) // NM, (f - NXT) % NM
                        eng.wait_ge(ffn1_ready, upto(i, NF1, f - NXT + 1))
                        if f == NXT:
                            eng.wait_ge(pv_ready, upto(i, 2))
                        act(hid[:, m, CH * c:CH * c + CH], F[f % 2][:, 0:CH], ACT.Gelu,
                            bias=b1s[:, m:m + 1]).then_inc(gelu_done, 1)

                def norm2(tiles):
                    if tiles[0] == 0:
                        eng.wait_ge(nmean2_done, upto(i, 1))
                        eng.wait_ge(xn2T_ready, upto(i - 1, NXT))
                    apply_norm(1, h1, xn2, ln2_applied, tiles)

                if nx:
                    for k in range(3):
                        copy_v0(k)
                    for u in range(NU):
                        for k in copies_after(u):
                            copy_v0(k)
                        if u >= 4 and u % 4 == 0:
                            copy_values(u // 4 - 1)
                        if at:
                            if u == 3:
                                norm2((0, 1, 2))
                            if u == 4:
                                norm2((3, 4))
                            for f in fill_after(u):
                                fill(f)
                    copy_values(3)
                elif at:
                    norm2(range(NT))
                if exists(l):
                    eng.wait_ge(nmean1_done, upto(l, 1))
                    eng.wait_ge(xn1T_ready, upto(l - 1, NXT))
                    apply_norm(0, hA, xn1, ln1_applied, range(NT))
                if at:
                    for f in left_fill() if nx else range(NFILL):
                        fill(f)
                if exists(l):
                    for s in range(NXT):
                        eng.wait_ge(xn1T_ready, upto(l, NXT, s + 1))
                        if s == 0:
                            eng.wait_ge(qkv_ready, upto(l - 1, 6))
                        transposed_copy(SCC[:, s % 2, :], xn1T, s // 2, s % 2).then_inc(xn1T_copied, 1)
                if nx:
                    eng.wait_ge(vst_ready, upto(p, 1))
                    eng.wait_ge(pv_ready, upto(p - 1, 2))
                    act(vst[:], SA1[:, 1, 0:2 * FB].rearrange("p (k n) -> p k n", k=2), ACT.Copy).then_inc(vst_copied, 1)

            eng.wait_ge(ffn_const, 16 * NFFN)
            run(eng, iteration)

            eng.wait_ge(cdve, 2)
            act(cg[:, 1, :], cg[:, 0, :], ACT.Exp).then_inc(cact, 1)
            eng.wait_ge(cdve, CHID)
            for par in range(2):
                src = chp[:, 0].rearrange("p m (c b) -> p m c b", b=NB)[:, :, par:NCLS:2, :]
                dst = chz0[:, par].rearrange("p m (c b) -> p m c b", b=NB)[:, :, par:NCLS:2, :]
                act(dst, src, ACT.Gelu).then_inc(cact, 1)
            for e in range(3):
                src = chp[:, 1, :, 2 * NB * e:2 * NB * e + 2 * NB]
                act(chz1[:, e, :, 2 * NB * e:2 * NB * e + 2 * NB], src, ACT.Gelu).then_inc(cact, 1)

        @block.vector
        def _(eng):
            tt, ts, stt = eng.tensor_tensor, eng.tensor_scalar, eng.scalar_tensor_tensor
            eng.memset(counts[:], 0.0)
            eng.memset(rank_base[:], 0.0).then_inc(base_done, 1)

            def score(b):
                eng.wait_ge(x_loaded, upto(b, 16))
                if is_at(b, 0):
                    eng.wait_ge(tok_const, 16 * NTOKC)
                for c in range(NSC):
                    ins = eng.tensor_tensor_reduce(score_junk[:, c, :], xs[:, c, :], wtok[:], 1.0, 0.0,
                                                   ALU.mult, ALU.add, score_raw[:, c:c + 1])
                ins.then_inc(score_step, 1)
                eng.wait_ge(score_step, upto(b, 1))
                eng.wait_ge(score_stored, upto(b - 1, 16))
                eng.wait_ge(rank_step, upto(b - 1, NSC + 1))
                ts(score_col[:], score_raw[:], btok[:, 0:1], None, ALU.add).then_inc(score_done, 1)

            def rank(b):
                eng.wait_ge(row_loaded, upto(b, 16))
                eng.wait_ge(score_done, upto(b, 1))
                for c in range(NSC):
                    a = SC * c
                    s = score_col[:, c:c + 1]
                    if c >= 2:
                        eng.wait_ge(rank_step, upto(b, NSC + 1, c - 1))
                    if c >= 1:
                        ts(cmp_junk[:, c % 2, 0:a], score_row[:, 0:a], s, None, ALU.is_ge, ALU.add,
                           accum_out=counts[:, 0, c:c + 1])
                    ts(cmp_junk[:, c % 2, a:], score_row[:, a:], s, None, ALU.is_gt, ALU.add,
                       accum_out=counts[:, 1, c:c + 1])
                    ins = stt(tie_junk[:, c % 2, :], score_row[:, a:a + SC], s, lower[:],
                              ALU.is_equal, ALU.mult, accum_out=counts[:, 2, c:c + 1])
                    ins.then_inc(rank_step, 1)
                eng.wait_ge(rank_step, upto(b, NSC + 1, NSC))
                eng.tensor_reduce(rank_sum[:], counts[:].rearrange("p k c -> p c k"), AX.X, ALU.add).then_inc(rank_step, 1)
                eng.wait_ge(rank_step, upto(b, NSC + 1))
                eng.wait_ge(scattered, upto(b - 1, 16 * NSC))
                eng.wait_ge(base_done, upto(b, 1, 1))
                ts(rank_idx[:], rank_sum[:], rank_base[:, 0:1], None, ALU.add).then_inc(rank_done, 1)
                eng.wait_ge(rank_done, upto(b, 1))
                ts(rank_base[:], rank_base[:], float(NTOK), None, ALU.add).then_inc(base_done, 1)

            def norm_stats(b, which, src, step):
                for j in range(NT):
                    ins = eng.bn_stats(stats[:, which, j, :], src[:, j, :])
                ins.then_inc(step, 1)
                eng.wait_ge(step, upto(b, 3, 1))
                passed(eng)
                for j in range(NT):
                    ins = eng.bn_aggr(meanvar[:, which, j, :], stats[:, which, j, :])
                ins.then_inc(step, 1)
                eng.wait_ge(step, upto(b, 3, 2))
                eng.wait_ge((ln1_applied, ln2_applied)[which], upto(b - 1, NT))
                ts(vareps[:, which, :], meanvar[:, which, :, 1], EPS, None, ALU.add).then_inc(step, 1)

            def norm_mean(b, which, rstd_done, sem):
                eng.wait_ge(rstd_done, upto(b, 1))
                stt(nmean[:, which, :], meanvar[:, which, :, 0], -1.0, rstd[:, which, :],
                           ALU.mult, ALU.mult).then_inc(sem, 1)

            def centre(b, j):
                slot = (SB, SCC)[j % 2]
                psum = slot[0:TT, :, 0:384].rearrange("p k (h s) -> p k h s", s=64)
                smax_j = smax[:, j % 2, :].rearrange("p (k h) -> p k h", k=2)
                eng.wait_ge(logits_ready, upto(b, NT, j + 1))
                eng.wait_ge(centred, upto(b, NT, j - 1))
                eng.tensor_reduce(smax_j, psum, AX.X, ALU.max).then_inc(max_step, 1)
                eng.wait_ge(max_step, upto(b, NT, j + 1))
                if j >= 3:
                    eng.wait_ge(attT_ready, upto(b, NT, j - 2))
                else:
                    eng.wait_ge(attT_ready, upto(b - 1, NT))
                tt(E[:, j % 3].rearrange("p (k q) (r s) -> p k (q r) s", k=2, r=2), psum,
                   smax_j.unsqueeze(3).to_broadcast([TT, 2, 6, 64]), ALU.subtract).then_inc(centred, 1)

            def normalise(b, j):
                e = E[:, j % 3].rearrange("p q (r s) -> p (q r) s", r=2)
                eng.wait_ge(exp_done, upto(b, NT, j + 1))
                eng.wait_ge(rden_done, upto(b, NT, j - 1))
                eng.tensor_reduce(den[:, j % 2, :], e, AX.X, ALU.add).then_inc(sum_done, 1)
                eng.wait_ge(sum_done, upto(b, NT, j + 1))
                eng.wait_ge(norm_done, upto(b, NT, j - 1))
                eng.reciprocal(rden[:, j % 2, :], den[:, j % 2, :]).then_inc(rden_done, 1)
                eng.wait_ge(rden_done, upto(b, NT, j + 1))
                tt(e, e, rden[:, j % 2, :].unsqueeze(2).to_broadcast([TT, NH, 64]), ALU.mult).then_inc(norm_done, 1)

            def iteration(i):
                n, l, p = i + 3, i + 2, i + 1
                at, nx = exists(i), exists(p)
                if at:
                    centre(i, 0)
                    centre(i, 1)
                    normalise(i, 0)
                    centre(i, 2)
                    normalise(i, 1)
                    centre(i, 3)
                    normalise(i, 2)
                    centre(i, 4)
                    normalise(i, 3)
                    normalise(i, 4)
                if at:
                    for kb, num, tail in ((0, SA0, SA1), (1, SB, SCC)):
                        eng.wait_ge(pv_ready, upto(i, 2, kb + 1))
                        tt(halves(tailv[:, kb, :]), both(tail, FB), halves(vT[:, kb, :]), ALU.mult).then_inc(tail_done, 1)
                        eng.wait_ge(tail_done, upto(i, 2, kb + 1))
                        eng.wait_ge(proj_ready, upto(i - 1, 2))
                        tt(halves(outT[:, kb, :]), both(num, FB), halves(tailv[:, kb, :]), ALU.add).then_inc(outT_done, 1)

                def products(u):
                    for q in range(3):
                        eng.wait_ge(kr_ready, upto(p, NKR, 3 * u + q + 1))
                        eng.wait_ge(vr_copied, upto(p, NVR, 3 * (u // 2) + q + 1))
                        if q == 0:
                            eng.wait_ge(contracted, upto(p, NU, u - 3) if u >= 4 else upto(p - 1, NU, u + 13))
                        tt(outer[:, u % 4, q, :], KR[q], vrows[:, u // 2 % 4, q, :], ALU.mult).then_inc(outer_done, 1)

                if nx:
                    products(0)
                if at:
                    eng.wait_ge(proj_ready, upto(i, 2, 1))
                    eng.wait_ge(hR_loaded, upto(i, 16))
                    eng.wait_ge(h1b_done, upto(i - 1, 1))
                    eng.wait_ge(ln2_applied, upto(i - 1, NT))
                    eng.wait_ge(cls_stored, upto(i - 1, 16))
                    tt(h1[:, 0:4, :].rearrange("p (k j) d -> p k (j d)", k=2), SB[0:TT, :, 0:2 * D],
                       hR[:, 0:4, :].rearrange("p (k j) d -> p k (j d)", k=2), ALU.add).then_inc(residual_done, 1)
                    eng.wait_ge(proj_ready, upto(i, 2, 2))
                    tt(h1[:, 4, :], SCC[0:TT, 1, 0:D], hR[:, 4, :], ALU.add).then_inc(residual_done, 1)
                if nx:
                    products(1)
                if at:
                    eng.wait_ge(residual_done, upto(i, 2))
                    norm_stats(i, 1, h1, ln_stats2)
                if nx:
                    products(2)
                if at:
                    norm_mean(i, 1, rstd2_done, nmean2_done)
                if exists(n) and not nx:
                    score(n)
                if exists(l) and not nx:
                    eng.wait_ge(hA_loaded, upto(l, 16))
                    norm_stats(l, 0, hA, ln_stats1)
                    norm_mean(l, 0, rstd1_done, nmean1_done)
                if nx:
                    for u in range(3, NU):
                        products(u)
                        if exists(n) and u == 5:
                            score(n)
                        if exists(l) and u == 8:
                            eng.wait_ge(hA_loaded, upto(l, 16))
                            norm_stats(l, 0, hA, ln_stats1)
                        if exists(l) and u == 10:
                            norm_mean(l, 0, rstd1_done, nmean1_done)
                if nx:
                    eng.wait_ge(kprefix, upto(p, 4))
                    eng.wait_ge(qkv_copied, upto(p, 6))
                    eng.wait_ge(qk_placed, upto(p - 1, 16 * 3))
                    tt(qkT[:], qT[:], kvT[:, 0:2, :], ALU.mult).then_inc(qk_done, 1)
                    eng.wait_ge(kset_step, upto(p, 6))
                    eng.wait_ge(logits_ready, upto(p - 1, NT))
                    if is_at(p, 0):
                        eng.wait_ge(att_const, 16 * NATT)
                    for q in range(3):
                        rows = slice(32 * q, 32 * q + 32)
                        for par in range(2):
                            ins = ts(kbd[0:32, q:q + 4:3, 64 * par:64 * par + NSET], ksets[rows, :, 0:NSET],
                                     parity[rows, par:par + 1], None, ALU.mult)
                    ins.then_inc(kbd_done, 1)
                if exists(n):
                    rank(n)
                if nx:
                    eng.wait_ge(vset_step, upto(p, 6))
                    eng.wait_ge(vst_ready, upto(p - 1, 1))
                    for par in range(2):
                        ins = ts(vexp[:, :, par, 0:NSET], vsets[:, :, 0:NSET], parity[:, par:par + 1], None, ALU.mult)
                    ins.then_inc(vexp_done, 1)
                if at:
                    eng.wait_ge(h1b_done, upto(i, 1))
                    eng.wait_ge(out_stored, upto(i - 1, 16 * 2))
                    eng.wait_ge(ffn2_ready, upto(i, 2, 1))
                    tt(osb[:, 0:4, :].rearrange("p (k j) d -> p k (j d)", k=2), SA0[0:TT, :, 0:2 * D],
                                h1b[:, 0:4, :].rearrange("p (k j) d -> p k (j d)", k=2), ALU.add).then_inc(added, 1)
                    eng.wait_ge(ffn2_ready, upto(i, 2, 2))
                    tt(osb[:, 4, :], SA1[0:TT, 0, 0:D], h1b[:, 4, :], ALU.add).then_inc(added, 1)

            eng.wait_ge(pool_const, NPOOL)
            run(eng, iteration)

            count = [0]

            def step(ins):
                ins.then_inc(cdve, 1)
                count[0] += 1
                eng.wait_ge(cdve, count[0])

            eng.wait_ge(cgate_ready, 1)
            eng.wait_ge(cls_const, 16 * NCC)
            gl = cg[:, 2, :]
            ins = tt(cgs[:], SB[0:48, 0, 0:2 * NCLS].rearrange("p (c o) -> p c o", o=2), pick[:], ALU.mult)
            ins.then_inc(cgs_done, 1)
            eng.wait_ge(cgs_done, 1)
            eng.tensor_reduce(gl, cgs[:].rearrange("p c o -> p o c"), AX.X, ALU.add).then_inc(cgs_done, 1)
            eng.wait_ge(cgs_done, 2)
            step(eng.tensor_reduce(cg[:, 3, 0:1], gl, AX.X, ALU.max))
            step(ts(cg[:, 0, :], gl, cg[:, 3, 0:1], None, ALU.subtract))
            eng.wait_ge(chid_ready, 1)
            for pair in range(2):
                hp = (SA0, SA1)[pair][:, 0, 0:NM * 48].rearrange("p (m t) -> p m t", m=NM)
                if pair == 0:
                    for e in range(3):
                        cols = slice(2 * NB * e, 2 * NB * e + 2 * NB)
                        step(tt(chp[:, 0, :, cols], hp[:, :, cols],
                                a1bs[:, e, :].unsqueeze(2).to_broadcast([128, NM, 2 * NB]), ALU.add))
                else:
                    for e in range(2):
                        for k in range(3):
                            cols = slice(NB * (e + 2 * k), NB * (e + 2 * k) + NB)
                            step(tt(chp[:, 1, :, cols], hp[:, :, cols],
                                    a1bs[:, 3 + e, :].unsqueeze(2).to_broadcast([128, NM, NB]), ALU.add))
            assert count[0] == CHID
            eng.wait_ge(cact, 1)
            e = cg[:, 1, :]
            step(eng.tensor_reduce(cg[:, 4, 0:1], e, AX.X, ALU.add))
            step(eng.reciprocal(cg[:, 4, 1:2], cg[:, 4, 0:1]))
            step(ts(cg[:, 5, :], e, cg[:, 4, 1:2], None, ALU.mult))
            step(eng.tensor_reduce(cg[:, 6, 0:1], cg[:, 5, :], AX.X, ALU.min))
            step(stt(cg[:, 7, :], cg[:, 5, :], cg[:, 6, 0:1], cg[:, 5, :], ALU.is_gt, ALU.mult))
            step(eng.tensor_reduce(cg[:, 8, 0:1], cg[:, 7, :], AX.X, ALU.add))
            step(ts(cg[:, 8, 1:2], cg[:, 8, 0:1], 1e-6, None, ALU.max))
            step(eng.reciprocal(cg[:, 9, 0:1], cg[:, 8, 1:2]))
            step(ts(cg[:, 10, :], cg[:, 7, :], cg[:, 9, 0:1], None, ALU.mult))
            eng.wait_ge(cout_ready, 1)
            eng.wait_ge(cls_io, 16 * NCLS)
            step(stt(cres[:], SCC[0:48, 0, 0:D], cg[:, 10, 0:1], cres[:], ALU.mult, ALU.add))
            step(stt(c0[:], SCC[0:48, 1, 0:D], cg[:, 10, 1:2], cres[:], ALU.mult, ALU.add))
            assert count[0] == CDVE

        @block.gpsimd
        def _(eng):
            eng.memset(wbil[:], 0.0).then_inc(pool_const, 1)
            eng.memset(neghalf[:], -0.5)
            for t_ in (xn1T, xn2T, ET):
                eng.memset(t_[:, :, T:TP], 0.0)
            eng.memset(vexp[:], 0.0)
            eng.memset(kbd[0:32, :, :], 0.0)
            eng.memset(chz0[:], 0.0)
            eng.memset(chz1[:], 0.0).then_inc(pool_const, 1)

            def running_sums(b, buf, step):
                w = 1
                k = 0
                while w < BLK:
                    v = buf.rearrange("p k (n t) -> p (k n) t", t=2 * w)
                    if k:
                        eng.wait_ge(step, upto(b, 4, k))
                    last = v[:, :, w - 1:w].to_broadcast([FB, 2 * TP // (2 * w), w]) if w > 1 else v[:, :, 0:1]
                    eng.tensor_tensor(v[:, :, w:2 * w], v[:, :, w:2 * w], last, ALU.add).then_inc(step, 1)
                    w, k = 2 * w, k + 1

            def set_sums(b, buf, sets, step):
                full = buf.rearrange("p k (n t) -> p k n t", t=BLK)
                passed(eng)
                eng.tensor_copy(sets[:, :, 0:32], full[:, :, 0:32, BLK - 1]).then_inc(step, 1)
                at, n = 0, 32
                for k in range(1, 6):
                    eng.wait_ge(step, upto(b, 6, k))
                    eng.tensor_tensor(sets[:, :, at + n:at + n + n // 2], sets[:, :, at:at + n:2],
                                              sets[:, :, at + 1:at + n:2], ALU.add).then_inc(step, 1)
                    at, n = at + n, n // 2

            def inv_root(b, which, stats_done, sem):
                eng.wait_ge(stats_done, upto(b, 3))
                eng.wait_ge((nmean1_done, nmean2_done)[which], upto(b - 1, 1))
                eng.wait_ge((ln1_applied, ln2_applied)[which], upto(b - 1, NT))
                eng.tensor_tensor(rstd[:, which, :], vareps[:, which, :], neghalf[:], ALU.pow).then_inc(sem, 1)

            def iteration(i):
                n, l, p = i + 3, i + 2, i + 1
                at, nx = exists(i), exists(p)
                if nx:
                    for kv in range(2):
                        blocks = slice(2 * kv, 2 * kv + 2)
                        eng.wait_ge(part1_done, upto(p, 2, kv + 1))
                        eng.tensor_tensor(rest[:, blocks, :], kvT[:, blocks, :],
                                                        parts[:, 0, blocks, :], ALU.subtract).then_inc(rest1_done, 1)
                        eng.wait_ge(part2_done, upto(p, 2, kv + 1))
                        eng.tensor_tensor(parts[:, 2, blocks, :], rest[:, blocks, :],
                                                        parts[:, 1, blocks, :], ALU.subtract).then_inc(part3_done, 1)
                    running_sums(p, kvT[:, 0:2, :], kprefix)
                    eng.wait_ge(kprefix, upto(p, 4))
                    eng.wait_ge(kbd_done, upto(p - 1, 1))
                    set_sums(p, kvT[:, 0:2, :], ksets, kset_step)
                if at:
                    inv_root(i, 1, ln_stats2, rstd2_done)
                    eng.wait_ge(residual_done, upto(i, 2))
                    eng.wait_ge(added, upto(i - 1, 2))
                    eng.tensor_tensor(h1b[:], h1[:], b2row[:].unsqueeze(1).to_broadcast([TT, NT, D]), ALU.add).then_inc(h1b_done, 1)
                if exists(l):
                    inv_root(l, 0, ln_stats1, rstd1_done)
                if nx:
                    eng.wait_ge(v_copied, upto(p, 4))
                    running_sums(p, vT[:], vprefix)
                    eng.wait_ge(vprefix, upto(p, 4))
                    eng.wait_ge(vexp_done, upto(p - 1, 1))
                    set_sums(p, vT[:], vsets, vset_step)
                if exists(n):
                    eng.wait_ge(rank_done, upto(n, 1))
                    passed(eng)
                    for c in range(NSC):
                        eng.indirect_dma_start(
                            sorted_dram, bass.IndirectOffsetOnAxis(ap=rank_idx[:, c:c + 1], axis=0),
                            xs[:, c, :], None).then_inc(scattered, 16)

            eng.wait_ge(ffn_const, 16 * NFFN)
            run(eng, iteration)


def constants():
    import numpy as np
    one = 0x3F80
    r = np.arange(128)
    krep = np.zeros((FB, 2, 2, 128), np.uint16)
    vrep = np.zeros((FB, 2, 128), np.uint16)
    for part in range(3):
        for par in range(2):
            for e in range(HS):
                row = 32 * part + 16 * par + e
                vrep[row, par, r % 16 == e] = one
                for half in range(2):
                    krep[row, par, half, 8 * half + r // 16 == e] = one
    kbd = np.zeros((64, 6, 2, 64), np.float32)
    for par in range(2):
        kbd[16 * par:16 * par + 16, :, par, NSET] = 1
    ends, length = [], 1
    while length <= 32:
        ends += [(k + 1) * length for k in range(32 // length)]
        length *= 2
    assert len(ends) == NSET
    for b in range(32):
        kbd[32 + b, :, :, :NSET] = np.where(np.array(ends) > b, NEG, 0)
    onehot = np.zeros((32, 6, TP), np.float32)
    for t in range(T):
        if (t + 1) // BLK < 32:
            onehot[(t + 1) // BLK, :, t] = 1
    parity = np.zeros((FB, 2), np.float32)
    for row in range(FB):
        parity[row, row // 16 % 2] = 1
    tail = np.zeros((128, 32), np.float32)
    for par in range(2):
        tail[64 * par + NSET, 16 * par:16 * par + 16] = 1
    lower = (np.arange(SC)[None, :] < np.arange(SC)[:, None]).astype(np.uint16) * np.uint16(one)
    pick = np.zeros((48, NCLS, 2), np.float32)
    cls = np.zeros((5, 2, 48), np.float32)
    for row in range(48):
        c = row // NB
        pick[row, c] = 1
        cls[3 + c % 2, 0, row] = 1
        cls[c // 2, 1, row] = 1
    return {"c_ident": np.eye(128, dtype=np.float32), "c_krep": krep, "c_vrep": vrep,
            "c_kbd": kbd.reshape(64, 6, 128), "c_onehot": onehot, "c_parity": parity,
            "c_tail": tail, "c_lower": lower, "c_pick": pick, "c_cls": cls}


def layout(inp):
    import numpy as np
    f = {k: np.asarray(v) for k, v in inp.items()}
    ct = np.ascontiguousarray
    return {
        "x": f["x"], "tok_w": ct(f["L0_tok_w"].reshape(D)), "tok_b": f["L0_tok_b"],
        "wqkvT": ct(f["L0_attn_Wqkv"].T), "wprojT": ct(f["L0_attn_Wproj"].T),
        "wvT": ct(f["L0_attn_Wv"].T), "bv96": ct(np.tile(f["L0_attn_bv"], FB // HS).reshape(FB, 1)),
        "w1": f["L0_ffn_moe0_W1"], "b1c": ct(f["L0_ffn_moe0_b1"].reshape(NM, 128).T),
        "w2": f["L0_ffn_moe0_W2"], "b2": f["L0_ffn_moe0_b2"],
        "a1": f["L0_ffn_A1_W"], "a1bc": ct(f["L0_ffn_A1_b"].reshape(5, NM, 128).transpose(2, 0, 1)),
        "a2": f["L0_ffn_A2_W"], "a2b": f["L0_ffn_A2_b"], "gw": ct(f["L0_ffn_G_W"].reshape(NCLS, 2, FB, 2).transpose(2, 1, 0, 3)),
        **constants(),
    }


def kernel(**inputs):
    import concourse.bacc as bacc
    from concourse.bass_utils import run_bass_kernel_spmd

    nc = bacc.Bacc("TRN2", target_bir_lowering=False, num_devices=1)
    arrays = layout(inputs)
    aps = [nc.dram_tensor(name, list(a.shape), mybir.dt.from_np(a.dtype), kind="ExternalInput").ap()
           for name, a in arrays.items()]
    out = nc.dram_tensor("out", [NB, T, D], F32, kind="ExternalOutput").ap()
    build(nc, *aps, out)
    r = run_bass_kernel_spmd(nc, [arrays], core_ids=[0])
    return r.results[0]["out"]
```

```python
from contextlib import ExitStack

import concourse.bass as bass
import concourse.mybir as mybir

F32 = mybir.dt.float32
BF16 = mybir.dt.bfloat16
U32 = mybir.dt.uint32
U16 = mybir.dt.uint16
ALU = mybir.AluOpType
ACT = mybir.ActivationFunctionType
AX = mybir.AxisListType

NB, NTOK, D = 8, 750, 192
T = int(round(NTOK * 0.7))
NH, HS = 12, 16
BLK = 16
TP = -(-T // BLK) * BLK
CH = TP // 2
TT, NT = 105, 5
SC, NSC = 125, 6
FB = 96
HID = 768
NM = HID // 128
NCLS = 6
NSET = 63
EPS = 1e-5
SCALE = 0.25
NEG = -1e30
assert NT * TT == T and NSC * SC == NTOK

NTOKC, NQKV, NVAL, NATT, NFFN, NCC, NPOOL = 3, 1, 7, 6, 4, 7, 2
CHID, CDVE, CGELU = 7, 19, 6

NU = 16
NKR, NVR = 3 * NU, 3 * NU // 2
NF1 = 2 * NM
CROW = (0, 2 * NB, 2 * NB, 0, 2 * NB)
COFF = (0, 0, 2 * NB, 0, NB)
NQ = 7
NXT = 4
FILL = {5: (0, 1), 6: (2, 3), 7: (4,), 8: (5,), 9: (6,), 10: (7,), 11: (8,), 12: (9,), 13: (10,), 14: (11,), 15: (12,)}
NFILL = NXT + NF1
RANKED, RANKED2 = 2, 5


def unit(u):
    return u // 8, u // 4 % 2, u // 2 % 2, u % 2


def copies_after(u):
    nxt = 3 * (u // 2 + 1)
    return [k for k in ((nxt, nxt + 1), (nxt + 2,))[u % 2] if k < NVR]


def fill_after(u):
    return FILL.get(u, ())


def left_fill():
    return range(sum(len(f) for f in FILL.values()), NFILL)


def upto(b, per, k=None):
    v = b * per + (per if k is None else k)
    return max(v, 0) if isinstance(v, int) else v


def is_at(b, n):
    return isinstance(b, int) and b == n


def exists(b):
    return not isinstance(b, int) or 0 <= b < NB


def build(nc, x, tok_w, tok_b, wqkvT, wprojT, wvT, bv96, w1, b1c, w2, b2, a1, a1bc, a2, a2b, gw,
          c_ident, c_krep, c_vrep, c_kbd, c_onehot, c_parity, c_tail, c_lower, c_pick, c_cls, out):
    ctx = ExitStack()
    with ctx:
        def sb(name, shape, dt=F32):
            return ctx.enter_context(nc.sbuf_tensor(name, shape, dt))

        def sem(name):
            return ctx.enter_context(nc.semaphore(name))

        ident = sb("ident", [128, 128])
        krep = sb("krep", [FB, 2, 2, 128], BF16)
        vrep = sb("vrep", [FB, 2, 128], BF16)
        parity = sb("parity", [FB, 2])
        tailsel = sb("tailsel", [128, 32])
        lower = sb("lower", [SC, SC], BF16)
        pick = sb("pick", [48, NCLS, 2])
        clsrow = sb("clsrow", [5, 2, 48])
        neghalf = sb("neghalf", [TT, NT])
        wtok = sb("wtok", [SC, D])
        btok = sb("btok", [SC, 1])
        wqkv = sb("wqkv", [FB, 2, 3 * D])
        wproj = sb("wproj", [FB, 2, D])
        wbil = sb("wbil", [128, 2, 2, 32])
        bvcol = sb("bvcol", [FB, 1])
        w1s = sb("w1s", [FB, 2, HID])
        b1s = sb("b1s", [128, NM])
        w2s = sb("w2s", [128, NM, D])
        b2row = sb("b2row", [TT, D])
        a1bs = sb("a1bs", [128, 5, NM])
        a2bs = sb("a2bs", [5, D])
        gws = sb("gws", [FB, 2, NCLS, 2])

        xs = sb("xs", [SC, NSC, D])
        score_junk = sb("score_junk", [SC, NSC, D], BF16)
        score_raw = sb("score_raw", [SC, NSC])
        score_col = sb("score_col", [SC, NSC])
        score_row = sb("score_row", [SC, NTOK])
        cmp_junk = sb("cmp_junk", [SC, 2, NTOK], BF16)
        tie_junk = sb("tie_junk", [SC, 2, SC], BF16)
        counts = sb("counts", [SC, 3, NSC])
        rank_sum = sb("rank_sum", [SC, NSC])
        rank_base = sb("rank_base", [SC, 1])
        rank_idx = sb("rank_idx", [SC, NSC], U32)

        hA = sb("hA", [TT, NT, D])
        xn1 = sb("xn1", [TT, NT, D])
        xn1T = sb("xn1T", [FB, 2, TP])
        xn2T = sb("xn2T", [FB, 2, TP])
        stats = sb("stats", [TT, 2, NT, 6])
        meanvar = sb("meanvar", [TT, 2, NT, 2])
        vareps = sb("vareps", [TT, 2, NT])
        rstd = sb("rstd", [TT, 2, NT])
        nmean = sb("nmean", [TT, 2, NT])

        kvT = sb("kvT", [FB, 4, TP])
        qT = sb("qT", [FB, 2, TP])
        qkT = sb("qkT", [FB, 2, TP])
        region = sb("region", [128, max(25 * TP, 10 * HID + 5 * NM * D)])
        outer = region[:, 0:6 * TP].rearrange("p (g q t) -> p g q t", g=4, q=3)
        vrows = region[:, 6 * TP:9 * TP].rearrange("p (g q t) -> p g q t", g=2, q=3)
        stack = region[0:FB, 9 * TP:15 * TP].bitcast(BF16).rearrange("p (q t) -> p q t", q=12)
        parts = region[0:FB, 15 * TP:21 * TP].bitcast(BF16).rearrange("p (s k t) -> p s k t", s=3, k=4)
        rest = region[0:FB, 21 * TP:25 * TP].rearrange("p (k t) -> p k t", k=4)
        a1s = region[0:FB, 0:10 * HID].rearrange("p (a k n) -> p a k n", a=5, k=2)
        a2s = region[:, 10 * HID:10 * HID + 5 * NM * D].rearrange("p (a m n) -> p a m n", a=5, m=NM)
        vT = sb("vT", [FB, 2, TP])
        ksets = sb("ksets", [FB, 2, 64])
        vsets = sb("vsets", [FB, 2, 64])
        vexp = sb("vexp", [FB, 2, 2, 64])
        kbd = sb("kbd", [FB, 6, 128])
        vst = sb("vst", [128, 2, FB])
        X = sb("X", [FB, 6, TP])

        smax = sb("smax", [TT, 2, NH])
        den = sb("den", [TT, 2, NH])
        rden = sb("rden", [TT, 2, NH])
        E = sb("E", [TT, 4, 6, 128])
        ET = sb("ET", [128, 6, TP])
        tailv = sb("tailv", [FB, 2, TP])
        outT = sb("outT", [FB, 2, TP])
        hR = sb("hR", [TT, NT, D])
        h1 = sb("h1", [TT, NT, D])
        h1b = sb("h1b", [TT, NT, D])
        xn2 = sb("xn2", [TT, NT, D])
        hid = ET
        osb = sb("osb", [TT, NT, D])

        cx = sb("cx", [FB, 2, NCLS, NB])
        cxp = sb("cxp", [FB, 2, 2, NCLS // 2, NB])
        crow = ET[:, 0:2, 0:HID // 2]
        crow4 = ET[0:64, 2, 0:HID // 2]
        cres = sb("cres", [48, D])
        chp = sb("chp", [128, 2, NM, 48])
        chz0 = sb("chz0", [128, 2, NM, 48])
        chz1 = sb("chz1", [128, 3, NM, 48])
        cg = sb("cg", [48, 12, 2])
        cgs = sb("cgs", [48, NCLS, 2])
        c0 = sb("c0", [48, D])

        SA0 = ctx.enter_context(nc.psum_tensor("SA0", [128, 2, 512], F32))
        SA1 = ctx.enter_context(nc.psum_tensor("SA1", [128, 2, 512], F32))
        SB = ctx.enter_context(nc.psum_tensor("SB", [128, 2, 512], F32))
        SCC = ctx.enter_context(nc.psum_tensor("SCC", [128, 2, 512], F32))

        KR = (SA0[:, 0, 0:CH], SA0[:, 1, 0:CH], SA1[:, 0, 0:CH])
        VR = SA1[:, 1, 0:CH]
        ACC = (SCC[0:FB, 0, 0:CH], SCC[0:FB, 1, 0:CH])
        F = (SB[:, 0, :], SB[:, 1, :])

        score_dram = nc.dram_tensor("score_dram", [NB, NTOK], F32, kind="Internal").ap()
        sorted_dram = nc.dram_tensor("sorted_dram", [NB * NTOK, D], F32, kind="Internal").ap()
        sorted_b = sorted_dram.rearrange("(b n) d -> b n d", b=NB)
        cls_dram = nc.dram_tensor("cls_dram", [NB, NCLS, D], F32, kind="Internal").ap()

        x_loaded = sem("x_loaded")
        score_stored = sem("score_stored")
        row_loaded = sem("row_loaded")
        scattered = sem("scattered")
        hA_loaded = sem("hA_loaded")
        hR_loaded = sem("hR_loaded")
        k_stacked = sem("k_stacked")
        v_stacked = sem("v_stacked")
        q_placed = sem("q_placed")
        qk_placed = sem("qk_placed")
        cls_stored = sem("cls_stored")
        out_stored = sem("out_stored")
        tok_const = sem("tok_const")
        qkv_const = sem("qkv_const")
        val_const = sem("val_const")
        att_const = sem("att_const")
        ffn_const = sem("ffn_const")
        cls_const = sem("cls_const")
        cls_io = sem("cls_io")
        xn1T_ready = sem("xn1T_ready")
        qkv_ready = sem("qkv_ready")
        logits_ready = sem("logits_ready")
        attT_ready = sem("attT_ready")
        pv_ready = sem("pv_ready")
        proj_ready = sem("proj_ready")
        vr_ready = sem("vr_ready")
        kr_ready = sem("kr_ready")
        contracted = sem("contracted")
        xn2T_ready = sem("xn2T_ready")
        ffn1_ready = sem("ffn1_ready")
        ffn2_ready = sem("ffn2_ready")
        vst_ready = sem("vst_ready")
        ln1_applied = sem("ln1_applied")
        xn1T_copied = sem("xn1T_copied")
        qkv_copied = sem("qkv_copied")
        part1_done = sem("part1_done")
        part2_done = sem("part2_done")
        exp_done = sem("exp_done")
        attT_copied = sem("attT_copied")
        vr_copied = sem("vr_copied")
        v_copied = sem("v_copied")
        ln2_applied = sem("ln2_applied")
        xn2T_copied = sem("xn2T_copied")
        cx_copied = sem("cx_copied")
        gelu_done = sem("gelu_done")
        vst_copied = sem("vst_copied")
        rest2_done = sem("rest2_done")
        part3_done = sem("part3_done")
        score_step = sem("score_step")
        score_done = sem("score_done")
        rank_step = sem("rank_step")
        rank_done = sem("rank_done")
        base_done = sem("base_done")
        ln_stats1 = sem("ln_stats1")
        ln_stats2 = sem("ln_stats2")
        nmean1_done = sem("nmean1_done")
        nmean2_done = sem("nmean2_done")
        max_step = sem("max_step")
        centred = sem("centred")
        sum_done = sem("sum_done")
        rden_done = sem("rden_done")
        norm_done = sem("norm_done")
        tail_done = sem("tail_done")
        outT_done = sem("outT_done")
        residual_done = sem("residual_done")
        outer_done = sem("outer_done")
        qk_done = sem("qk_done")
        kbd_done = sem("kbd_done")
        vexp_done = sem("vexp_done")
        added = sem("added")
        pool_const = sem("pool_const")
        waits_passed = sem("waits_passed")
        rest1_done = sem("rest1_done")
        kprefix = sem("kprefix")
        vprefix = sem("vprefix")
        kset_step = sem("kset_step")
        vset_step = sem("vset_step")
        rstd1_done = sem("rstd1_done")
        rstd2_done = sem("rstd2_done")
        h1b_done = sem("h1b_done")
        cgate_ready = sem("cgate_ready")
        cxp_done = sem("cxp_done")
        crow_act = sem("crow_act")
        crow_dve = sem("crow_dve")
        chidT_ready = sem("chidT_ready")
        chid_ready = sem("chid_ready")
        cout_ready = sem("cout_ready")
        cgs_done = sem("cgs_done")
        cdve = sem("cdve")
        cact = sem("cact")

        block = ctx.enter_context(nc.Block())

        def run(eng, iteration):
            for i in range(-3, 1):
                iteration(i)
            with eng.Fori(1, NB - 3) as i:
                iteration(i)
            for i in range(NB - 3, NB):
                iteration(i)

        def passed(eng):
            eng.sem_inc(waits_passed, 1)

        def both(ps, rows, n=CH):
            return ps[0:rows, :, 0:n]

        def halves(ap):
            return ap.rearrange("p (c t) -> p c t", c=2)

        @block.sync
        def _(eng):
            eng.dma_start(xs[:], x[0].rearrange("(c p) d -> p c d", p=SC)).then_inc(x_loaded, 16)
            eng.dma_start(wtok[:], tok_w.rearrange("(o d) -> o d", o=1).to_broadcast([SC, D])).then_inc(tok_const, 16)
            eng.dma_start(btok[:], tok_b.rearrange("(o d) -> o d", o=1).to_broadcast([SC, 1])).then_inc(tok_const, 16)
            eng.dma_start(lower[:].bitcast(U16), c_lower).then_inc(tok_const, 16)

            def iteration(i):
                n, l, p = i + 3, i + 2, i + 1
                if exists(i):
                    eng.wait_ge(residual_done, upto(i - 1, 2))
                    eng.dma_start(hR[:], sorted_b[i, 0:T].rearrange("(j p) d -> p j d", p=TT)).then_inc(hR_loaded, 16)

                def stack_up(kv, s):
                    eng.wait_ge(part3_done, upto(p, 2, 2 - kv))
                    for q in range(3):
                        eng.dma_start(stack[:, 6 * kv + 2 * q:6 * kv + 2 * q + 2, :],
                                      parts[32 * q:32 * q + 32, :, 2 * kv:2 * kv + 2, :]).then_inc(s, 16)

                if exists(p):
                    eng.wait_ge(kr_ready, upto(p - 1, NKR))
                    eng.wait_ge(vr_ready, upto(p - 1, NVR))
                    stack_up(1, v_stacked)
                    stack_up(0, k_stacked)
                if exists(l):
                    eng.wait_ge(scattered, upto(l, 16 * NSC))
                    eng.wait_ge(ln1_applied, upto(l - 1, NT))
                    eng.wait_ge(ln_stats1, upto(l - 1, 3))
                    eng.dma_start(hA[:], sorted_b[l, 0:T].rearrange("(j p) d -> p j d", p=TT)).then_inc(hA_loaded, 16)
                if exists(n) and not is_at(n, 0):
                    eng.wait_ge(scattered, upto(n - 1, 16 * NSC))
                    eng.dma_start(xs[:], x[n].rearrange("(c p) d -> p c d", p=SC)).then_inc(x_loaded, 16)
                if exists(p):
                    eng.wait_ge(qkv_copied, upto(p, NQ))
                    eng.wait_ge(logits_ready, upto(p - 1, NT))
                    for q in range(3):
                        eng.dma_start(X[0:32, q:q + 4:3, :], qT[32 * q:32 * q + 32, :, :]).then_inc(q_placed, 16)
                if exists(i):
                    eng.wait_ge(residual_done, upto(i, 2))
                    eng.dma_start(cls_dram[i], h1[0:NCLS, 0, :]).then_inc(cls_stored, 16)
                if exists(n):
                    eng.wait_ge(score_done, upto(n, 1))
                    eng.dma_start(score_dram[n].rearrange("(c p) -> p c", p=SC), score_col[:],
                                                  allow_slow_non_contiguous=True).then_inc(score_stored, 16)
                if exists(n):
                    eng.wait_ge(score_stored, upto(n, 16))
                    eng.wait_ge(rank_step, upto(n - 1, NSC + 1))
                    eng.dma_start(score_row[:], score_dram[n].rearrange("(o m) -> o m", o=1).to_broadcast([SC, NTOK])).then_inc(row_loaded, 16)
                if exists(p):
                    eng.wait_ge(qk_done, upto(p, 1))
                    for q in range(3):
                        eng.dma_start(X[32:64, q:q + 4:3, :], qkT[32 * q:32 * q + 32, :, :]).then_inc(qk_placed, 16)
                if exists(i):
                    eng.wait_ge(added, upto(i, 2))
                    ob = out[i].rearrange("(j p) d -> p j d", p=TT)
                    eng.dma_start(ob[:, 1:NT], osb[:, 1:NT]).then_inc(out_stored, 16)
                    eng.dma_start(ob[NCLS:TT, 0], osb[NCLS:TT, 0]).then_inc(out_stored, 16)

            run(eng, iteration)
            eng.wait_ge(cls_stored, upto(NB - 1, 16))
            eng.dma_start(cres[:], cls_dram.rearrange("b c d -> c b d")).then_inc(cls_io, 16)
            eng.wait_ge(cdve, CDVE)
            eng.dma_start(out[:, 0:NCLS, :].rearrange("b c d -> c b d"), c0[:]).then_inc(cls_io, 16)
            eng.wait_ge(cls_io, 16 * 2)
            eng.wait_ge(out_stored, upto(NB - 1, 16 * 2))

        @block.tensor
        def _(eng):
            def mm(o, l, r, start=True, stop=True):
                return eng.matmul(o, l, r, start=start, stop=stop, skip_group_check=True)

            def logits(b, j, slot):
                if j == 0:
                    eng.wait_ge(q_placed, upto(b, 16 * 3))
                    eng.wait_ge(qk_placed, upto(b, 16 * 3))
                    eng.wait_ge(kbd_done, upto(b, 1))
                for h2 in range(6):
                    ins = mm(slot[0:TT, h2 // 3, (h2 % 3) * 128:(h2 % 3) * 128 + 128],
                             X[:, h2, TT * j:TT * j + TT], kbd[:, h2, :])
                ins.then_inc(logits_ready, 1)

            def project(b, k, slot):
                if k == 0:
                    eng.wait_ge(xn1T_copied, upto(b, NXT))
                col = (D, D + FB, 2 * D, 2 * D + FB, 0)[k]
                for c in range(2):
                    for kb in range(2):
                        ins = mm(slot[0:FB, c, 0:CH], wqkv[:, kb, col:col + FB],
                                 xn1T[:, kb, CH * c:CH * c + CH], kb == 0, kb == 1)
                ins.then_inc(qkv_ready, 1)

            def att_transpose(b, j, slot):
                eng.wait_ge(norm_done, upto(b, NT, j + 1))
                for h2 in range(6):
                    ins = eng.transpose(slot[:, h2 // 3, (h2 % 3) * TT:(h2 % 3) * TT + TT],
                                        E[:, j % 4, h2, :], ident[0:TT, 0:TT])
                ins.then_inc(attT_ready, 1)

            def iteration(i):
                p, l = i + 1, i + 2
                at, nx = exists(i), exists(p)
                eng.wait_ge(outer_done, upto(i, NKR))
                eng.wait_ge(added, upto(i - 1, 2, 1))
                if nx and is_at(p, 0):
                    eng.wait_ge(qkv_const, 16 * NQKV)
                if at:
                    att_transpose(i, 0, SA0)
                eng.wait_ge(added, upto(i - 1, 2))
                eng.wait_ge(vst_copied, upto(i, 1))
                if at:
                    att_transpose(i, 1, SA1)
                    eng.wait_ge(centred, upto(i, NT, 3))
                    logits(i, 4, SB)
                if nx:
                    if at:
                        eng.wait_ge(attT_copied, upto(i, NT, 1))
                    project(p, 0, SA0)
                    if at:
                        eng.wait_ge(attT_copied, upto(i, NT, 2))
                    project(p, 1, SA1)
                    eng.wait_ge(qkv_copied, upto(p, NQ, 1))
                    project(p, 2, SA0)
                    eng.wait_ge(qkv_copied, upto(p, NQ, 2))
                    project(p, 3, SA1)
                if nx and not at:
                    project(p, 4, SCC)
                if at:
                    for j in range(2, NT):
                        if j == 4 and nx:
                            eng.wait_ge(centred, upto(i, NT, 4))
                            project(p, 4, SCC)
                        if nx and j < 4:
                            eng.wait_ge(qkv_copied, upto(p, NQ, j + 1))
                        eng.wait_ge(attT_copied, upto(i, NT, j - 1))
                        att_transpose(i, j, (SA0, SA1)[j % 2])
                if at:
                    for kb, num, tail in ((1, SB, SCC), (0, SA0, SA1)):
                        if kb == 1:
                            eng.wait_ge(centred, upto(i, NT, 5))
                            if nx:
                                eng.wait_ge(qkv_copied, upto(p, NQ, 5))
                        for c in range(2):
                            eng.wait_ge(attT_copied, upto(i, NT, (3, 5)[c] if kb == 1 else 5))
                            for q in range(3):
                                ins = mm(tail[32 * q:32 * q + 32, c, 0:CH], tailsel[:],
                                         ET[:, 3 * kb + q, CH * c:CH * c + CH])
                            if c == 1:
                                ins.then_inc(pv_ready, 1)
                            for q in range(3):
                                ins = mm(num[32 * q:32 * q + 32, c, 0:CH], vst[:, kb, 32 * q:32 * q + 32],
                                         ET[:, 3 * kb + q, CH * c:CH * c + CH])
                        ins.then_inc(pv_ready, 1)

                def copy_v0(k):
                    c, kb, par, _ = unit(2 * (k // 3))
                    eng.wait_ge(vr_copied, upto(p, NVR, k))
                    mm(VR, vrep[:, par, :], stack[:, 6 + 2 * (k % 3) + kb, CH * c:CH * c + CH]).then_inc(vr_ready, 1)

                def copy_k(u):
                    if u == 0:
                        eng.wait_ge(k_stacked, upto(p, 16 * 3))
                    c, kb, par, half = unit(u)
                    for q in range(3):
                        if u and q != 1:
                            eng.wait_ge(outer_done, upto(p, NKR, 3 * u + (q - 2 if q else -1)))
                        mm(KR[q], krep[:, par, half, :], stack[:, 2 * q + kb, CH * c:CH * c + CH]).then_inc(kr_ready, 1)

                def contract(u):
                    c, kb, par, half = unit(u)
                    eng.wait_ge(outer_done, upto(p, NKR, 3 * u + 3))
                    if u == 0:
                        eng.wait_ge(qkv_copied, upto(p, NQ, 6))
                    if u == 4 and at:
                        eng.wait_ge(residual_done, upto(i, 2))
                    if u == 8 or u == 12:
                        eng.wait_ge(v_copied, upto(p, 4, u // 4 - 1))
                    for q in range(3):
                        ins = mm(ACC[u // 4 % 2][32 * q:32 * q + 32, :], wbil[:, half, par, :],
                                 outer[:, u % 4, q, :], u % 4 == 0, u % 4 == 3)
                    ins.then_inc(contracted, 1)

                def project_half(c):
                    if at and c == 1:
                        eng.wait_ge(residual_done, upto(i, 2))
                    for kb in range(2):
                        ins = mm((SCC, SB)[c][0:FB, c, 0:CH], wqkv[:, kb, FB:2 * FB], xn1T[:, kb, CH * c:CH * c + CH], kb == 0, kb == 1)
                    ins.then_inc(qkv_ready, 1)

                def fill(f):
                    if f < NXT:
                        g, kb = f // 2, f % 2
                        if f == 0:
                            eng.wait_ge(residual_done, upto(i, 2))
                            if nx:
                                eng.wait_ge(qkv_copied, upto(p, NQ))
                        if f >= 2:
                            eng.wait_ge(xn2T_copied, upto(i, NXT, f - 1))
                        eng.wait_ge(ln2_applied, upto(i, NT, (3, 5)[g]))
                        for j in range(3 * g, (3, 5)[g]):
                            ins = eng.transpose(F[f % 2][0:FB, (j % 3) * TT:(j % 3) * TT + TT],
                                                xn2[:, j, FB * kb:FB * kb + FB], ident[0:TT, 0:TT])
                        ins.then_inc(xn2T_ready, 1)
                    else:
                        c, m = (f - NXT) // NM, (f - NXT) % NM
                        eng.wait_ge(xn2T_copied, upto(i, NXT))
                        if f >= NXT + 2:
                            eng.wait_ge(gelu_done, upto(i, NF1, f - NXT - 1))
                        for kb in range(2):
                            ins = mm(F[f % 2][:, 0:CH], w1s[:, kb, 128 * m:128 * m + 128],
                                     xn2T[:, kb, CH * c:CH * c + CH], kb == 0, kb == 1)
                        ins.then_inc(ffn1_ready, 1)

                def out_project(j):
                    if j == 0:
                        eng.wait_ge(outT_done, upto(i, 2))
                    if j == 4 and nx:
                        eng.wait_ge(qkv_copied, upto(p, NQ, 6))
                    o = SB[0:TT, j // 2, (j % 2) * D:(j % 2) * D + D] if j < 4 else SCC[0:TT, 1, 0:D]
                    for kb in range(2):
                        ins = mm(o, outT[:, kb, TT * j:TT * j + TT], wproj[:, kb, :], kb == 0, kb == 1)
                    if j >= 3:
                        ins.then_inc(proj_ready, 1)

                if nx:
                    if is_at(p, 0):
                        eng.wait_ge(val_const, 16 * NVAL)
                    eng.wait_ge(qkv_copied, upto(p, NQ, 5))
                    if at:
                        eng.wait_ge(tail_done, upto(i, 2, 1))
                    project_half(0)
                    if at:
                        eng.wait_ge(tail_done, upto(i, 2))
                    eng.wait_ge(v_stacked, upto(p, 16 * 3))
                    copy_v0(0)
                if nx and not at:
                    copy_v0(1)
                    copy_v0(2)
                    copy_k(0)
                    copy_v0(3)
                    copy_k(1)
                    copy_v0(4)
                if nx and at:
                    out_project(0)
                    copy_v0(1)
                    out_project(1)
                    copy_v0(2)
                    copy_k(0)
                    out_project(2)
                    copy_v0(3)
                    out_project(3)
                    copy_k(1)
                    out_project(4)
                    copy_v0(4)
                elif at:
                    for j in range(NT):
                        out_project(j)
                if nx:
                    contract(0)
                    copy_v0(5)
                    for u in range(2, NU):
                        copy_k(u)
                        if u % 2 == 0 and 3 * (u // 2 + 1) < NVR:
                            copy_v0(3 * (u // 2 + 1))
                        contract(u - 1)
                        if u % 2 == 1 and 3 * (u // 2 + 1) < NVR:
                            copy_v0(3 * (u // 2 + 1) + 2)
                        if u == 4:
                            project_half(1)
                        if at:
                            for f in fill_after(u):
                                fill(f)
                        if u % 2 == 0 and 3 * (u // 2 + 1) < NVR:
                            copy_v0(3 * (u // 2 + 1) + 1)
                    contract(NU - 1)
                if at:
                    for f in left_fill() if nx else range(NFILL):
                        fill(f)
                if nx and not exists(l):
                    eng.wait_ge(v_copied, upto(p, 4))
                if exists(l):
                    if is_at(l, 0):
                        eng.wait_ge(att_const, 16 * NATT)
                    if nx:
                        eng.wait_ge(v_copied, upto(p, 4))
                    if at:
                        eng.wait_ge(residual_done, upto(i, 2))
                        eng.wait_ge(outer_done, upto(p, NKR))
                        eng.wait_ge(vr_copied, upto(p, NVR))
                    for s in range(NXT):
                        kb, g = s // 2, s % 2
                        eng.wait_ge(ln1_applied, upto(l, NT))
                        for j in range(3 * g, (3, 5)[g]):
                            ins = eng.transpose((SCC, SA1)[kb][0:FB, g, (j % 3) * TT:(j % 3) * TT + TT],
                                                xn1[:, j, FB * kb:FB * kb + FB], ident[0:TT, 0:TT])
                        ins.then_inc(xn1T_ready, 1)
                if nx:
                    eng.wait_ge(gelu_done, upto(i, NF1))
                    logits(p, 0, SB)
                    if exists(l):
                        eng.wait_ge(xn1T_copied, upto(l, NXT, 2))
                    logits(p, 1, SCC)
                if at:
                    if nx:
                        eng.wait_ge(outer_done, upto(p, NKR))
                    for j in range(NT):
                        o = SA0[0:TT, j // 2, (j % 2) * D:(j % 2) * D + D] if j < 4 else SA1[0:TT, 0, 0:D]
                        eng.wait_ge(gelu_done, upto(i, NF1, NM if j < 2 else NF1))
                        if j == 4 and exists(l):
                            eng.wait_ge(xn1T_copied, upto(l, NXT))
                        for m in range(NM):
                            ins = mm(o, hid[:, m, TT * j:TT * j + TT], w2s[:, m, :], m == 0, m == NM - 1)
                        if j >= 3:
                            ins.then_inc(ffn2_ready, 1)
                        if nx and j in (2, 3):
                            eng.wait_ge(centred, upto(p, NT, j - 1))
                            logits(p, j, (SB, SCC)[j - 2])
                elif nx:
                    for j in (2, 3):
                        eng.wait_ge(centred, upto(p, NT, j - 1))
                        logits(p, j, (SB, SCC)[j - 2])
                if nx:
                    eng.wait_ge(vr_copied, upto(p, NVR))
                    if exists(l):
                        eng.wait_ge(xn1T_copied, upto(l, NXT))
                    eng.wait_ge(vexp_done, upto(p, 1))
                    for kb in range(2):
                        ins = eng.transpose(SA1[:, 1, FB * kb:FB * kb + FB],
                                            vexp[:, kb, :, :], ident[0:FB, 0:FB])
                    ins.then_inc(vst_ready, 1)
                if is_at(l, 0):
                    eng.wait_ge(ffn_const, 16 * NFFN)

            run(eng, iteration)

            eng.wait_ge(cls_const, 16 * NCC)
            eng.wait_ge(cx_copied, upto(NB - 1, 1))
            eng.wait_ge(gelu_done, upto(NB - 1, NF1))
            eng.wait_ge(residual_done, upto(NB - 1, 2))
            cxv = [cx[:, kb].rearrange("p c b -> p (c b)") for kb in range(2)]
            cxpv = [cxp[:, kb].rearrange("p o c b -> p (o c b)") for kb in range(2)]
            for kb in range(2):
                ins = mm(SCC[0:48, 1, 0:2 * NCLS], cxv[kb], gws[:, kb, :, :], kb == 0, kb == 1)
            ins.then_inc(cgate_ready, 1)
            eng.wait_ge(added, upto(NB - 1, 2))
            eng.wait_ge(cxp_done, 2)
            for half in range(2):
                cols = slice(HID // 2 * half, HID // 2 * half + HID // 2)
                for kb in range(2):
                    for a in range(4):
                        rows = (cxv if a < 3 else cxpv)[kb][:, CROW[a]:CROW[a] + 32]
                        ins = mm(SA0[32 * a:32 * a + 32, half, 0:HID // 2], rows, a1s[:, a, kb, cols], kb == 0, kb == 1)
                ins.then_inc(chid_ready, 1)
            for kb in range(2):
                for half in range(2):
                    cols = slice(HID // 2 * half, HID // 2 * half + HID // 2)
                    ins = mm(SA1[32 * half:32 * half + 32, half, 0:HID // 2], cxpv[kb][:, CROW[4]:CROW[4] + 32],
                             a1s[:, 4, kb, cols], kb == 0, kb == 1)
            ins.then_inc(chid_ready, 1)
            for m in range(NM):
                if m == 0:
                    eng.wait_ge(crow_act, 1)
                if m == 3:
                    eng.wait_ge(crow_dve, 1)
                ins = eng.transpose(SB[:, m // 3, (m % 3) * 128:(m % 3) * 128 + 128],
                                    crow[:, m // 3, (m % 3) * 128:(m % 3) * 128 + 128], ident[:])
            ins.then_inc(chidT_ready, 1)
            eng.wait_ge(crow_act, 3)
            for m in range(3):
                ins = eng.transpose(SCC[:, 0, m * 64:m * 64 + 64], crow4[:, m * 128:m * 128 + 128], ident[0:64, 0:64])
            ins.then_inc(chidT_ready, 1)
            eng.wait_ge(cact, CGELU)
            chains = []
            for pair in range(2):
                o = SA0[64 * pair:64 * pair + 48, pair, 0:D]
                hz = (chz0, chz1)[pair]
                chain = [(o, clsrow[:, pair, :], a2bs[:])]
                for e in range(2 + pair):
                    a = 3 + e if pair == 0 else e
                    chain += [(o, hz[:, e, m, :], a2s[:, a, m, :]) for m in range(NM)]
                chains.append(chain)
            for k in range(len(chains[1])):
                for chain in chains:
                    if k < len(chain):
                        ins = mm(*chain[k], k == 0, k == len(chain) - 1)
            ins.then_inc(cout_ready, 1)

        @block.scalar
        def _(eng):
            def act(o, i_, f, **kw):
                return eng.activation(o, i_, f, **kw)

            eng.dma_start(ident[:], c_ident).then_inc(att_const, 16)
            eng.dma_start(parity[:], c_parity).then_inc(att_const, 16)
            eng.dma_start(tailsel[:], c_tail).then_inc(att_const, 16)
            eng.dma_start(X[64:96, :, :], c_onehot).then_inc(att_const, 16)
            eng.dma_start(kbd[32:96, :, :], c_kbd).then_inc(att_const, 16)
            eng.dma_start(wproj[:], wprojT.rearrange("(k p) n -> p k n", p=FB)).then_inc(att_const, 16)
            eng.dma_start(wqkv[:], wqkvT.rearrange("(k p) n -> p k n", p=FB)).then_inc(qkv_const, 16)
            eng.dma_start(krep[:].bitcast(U16), c_krep).then_inc(val_const, 16)
            eng.dma_start(vrep[:].bitcast(U16), c_vrep).then_inc(val_const, 16)
            eng.dma_start(bvcol[:], bv96).then_inc(val_const, 16)
            eng.wait_ge(pool_const, 1)
            for half in range(2):
                for par in range(2):
                    eng.dma_start(wbil[:, half, par, HS * par:HS * par + HS], wvT[128 * half:128 * half + 128, :]).then_inc(val_const, 16)
            eng.wait_ge(row_loaded, 16)
            eng.dma_start(w1s[:], w1.rearrange("(k p) n -> p k n", p=FB)).then_inc(ffn_const, 16)
            eng.dma_start(b1s[:], b1c).then_inc(ffn_const, 16)
            eng.dma_start(w2s[:], w2.rearrange("(m p) n -> p m n", p=128)).then_inc(ffn_const, 16)
            eng.dma_start(b2row[:], b2.rearrange("(o d) -> o d", o=1).to_broadcast([TT, D])).then_inc(ffn_const, 16)

            def transposed_copy(bank, dst, kb, g):
                a, z = ((0, 3), (3, 5))[g]
                return act(dst[:, kb, a * TT:z * TT], bank[0:FB, 0:(z - a) * TT], ACT.Copy)

            def exps(b, j):
                eng.wait_ge(centred, upto(b, NT, j + 1))
                act(E[:, j % 4], E[:, j % 4], ACT.Exp, scale=SCALE).then_inc(exp_done, 1)

            def copy_projection(b, k):
                eng.wait_ge(qkv_ready, upto(b, NQ, k + 1))
                if k == 0:
                    eng.wait_ge(kset_step, upto(b - 1, 6))
                    eng.wait_ge(part3_done, upto(b - 1, 2))
                    eng.wait_ge(qk_done, upto(b - 1, 1))
                if k == 4:
                    eng.wait_ge(q_placed, upto(b - 1, 16 * 3))
                dst = kvT[:, k, :] if k < 4 else qT[:, k - 4, :]
                slot = (SA0, SA1, SA0, SA1, SCC)[k]
                act(halves(dst), both(slot, FB), ACT.Copy).then_inc(qkv_copied, 1)

            def part1(b, kv):
                eng.wait_ge(qkv_copied, upto(b, NQ, 2 * kv + 2))
                eng.wait_ge((v_stacked if kv else k_stacked), upto(b - 1, 16 * 3))
                act(parts[:, 0, 2 * kv:2 * kv + 2, :], kvT[:, 2 * kv:2 * kv + 2, :], ACT.Copy).then_inc(part1_done, 1)

            def copy_attT(b, j):
                slot = (SA0, SA1)[j % 2]
                eng.wait_ge(attT_ready, upto(b, NT, j + 1))
                if j == 0:
                    eng.wait_ge(ffn2_ready, upto(b - 1, 2))
                act(
                    ET[:, :, TT * j:TT * j + TT].rearrange("p (k q) t -> p k q t", k=2),
                    slot[:, :, 0:3 * TT].rearrange("p k (q t) -> p k q t", q=3), ACT.Copy).then_inc(attT_copied, 1)

            def apply_norm(which, src, dst, sem, tiles):
                for j in tiles:
                    act(dst[:, j, :], src[:, j, :], ACT.Identity, scale=rstd[:, which, j:j + 1],
                        bias=nmean[:, which, j:j + 1]).then_inc(sem, 1)

            def iteration(i):
                p, l = i + 1, i + 2
                at, nx = exists(i), exists(p)
                if at:
                    copy_attT(i, 0)
                    copy_attT(i, 1)
                if nx:
                    copy_projection(p, 0)
                if at:
                    exps(i, 3)
                if nx:
                    copy_projection(p, 1)
                if at:
                    exps(i, 4)
                if nx:
                    part1(p, 0)
                    copy_projection(p, 2)
                if nx:
                    copy_projection(p, 3)
                    part1(p, 1)
                if at:
                    copy_attT(i, 2)
                    copy_attT(i, 3)
                if nx:
                    copy_projection(p, 4)
                if at:
                    copy_attT(i, 4)
                if is_at(i, NB - 1):
                    eng.wait_ge(contracted, upto(i, NU))
                    eng.dma_start(a1s[:], a1.rearrange("a (k p) n -> p a k n", p=FB)).then_inc(cls_const, 16)
                    eng.dma_start(a1bs[:], a1bc).then_inc(cls_const, 16)
                    eng.dma_start(a2s[:], a2.rearrange("a (m p) n -> p a m n", p=128)).then_inc(cls_const, 16)
                    eng.dma_start(a2bs[:], a2b).then_inc(cls_const, 16)
                    eng.dma_start(gws[:], gw).then_inc(cls_const, 16)
                    eng.dma_start(pick[:], c_pick).then_inc(cls_const, 16)
                    eng.dma_start(clsrow[:], c_cls).then_inc(cls_const, 16)

                def copy_v0(k):
                    pair = k // 3
                    eng.wait_ge(vr_ready, upto(p, NVR, k + 1))
                    if pair < 2:
                        eng.wait_ge(outer_done, upto(p - 1, NKR, 6 * (pair + 7)))
                    else:
                        eng.wait_ge(outer_done, upto(p, NKR, 6 * (pair - 1)))
                    act(vrows[:, pair % 2, k % 3, :], VR, ACT.Copy).then_inc(vr_copied, 1)

                def copy_values(s):
                    c, kb = s // 2, s % 2
                    eng.wait_ge(contracted, upto(p, NU, 4 * s + 4))
                    if s == 0:
                        eng.wait_ge(outT_done, upto(p - 1, 2))
                        eng.wait_ge(tail_done, upto(p - 1, 2))
                        eng.wait_ge(vset_step, upto(p - 1, 6))
                        if is_at(p, 0):
                            eng.wait_ge(val_const, 16 * NVAL)
                    act(vT[:, kb, CH * c:CH * c + CH], ACC[s % 2], ACT.Identity, bias=bvcol[:, 0:1]).then_inc(v_copied, 1)

                def fill(f):
                    if f < NXT:
                        eng.wait_ge(xn2T_ready, upto(i, NXT, f + 1))
                        if f == 0:
                            eng.wait_ge(ffn1_ready, upto(i - 1, NF1))
                            eng.wait_ge(cx_copied, upto(i - 1, 1))
                        transposed_copy(F[f % 2], xn2T, f % 2, f // 2).then_inc(xn2T_copied, 1)
                        if f == NXT - 1:
                            eng.wait_ge(xn2T_copied, upto(i, NXT))
                            act(cx[:, :, :, i], xn2T[:, :, 0:NCLS], ACT.Copy).then_inc(cx_copied, 1)
                    else:
                        c, m = (f - NXT) // NM, (f - NXT) % NM
                        eng.wait_ge(ffn1_ready, upto(i, NF1, f - NXT + 1))
                        if f == NXT:
                            eng.wait_ge(pv_ready, upto(i, 4))
                        act(hid[:, m, CH * c:CH * c + CH], F[f % 2][:, 0:CH], ACT.Gelu,
                            bias=b1s[:, m:m + 1]).then_inc(gelu_done, 1)

                def norm2(tiles):
                    if tiles[0] == 0:
                        eng.wait_ge(nmean2_done, upto(i, 1))
                        eng.wait_ge(xn2T_ready, upto(i - 1, NXT))
                    apply_norm(1, h1, xn2, ln2_applied, tiles)

                def norm1(tiles):
                    if tiles[0] == 0:
                        eng.wait_ge(nmean1_done, upto(l, 1))
                        eng.wait_ge(xn1T_ready, upto(l - 1, NXT))
                    apply_norm(0, hA, xn1, ln1_applied, tiles)

                if nx:
                    def copy_half(c):
                        eng.wait_ge(qkv_ready, upto(p, NQ, 6 + c))
                        act(qT[:, 1, CH * c:CH * c + CH], (SCC, SB)[c][0:FB, c, 0:CH], ACT.Copy).then_inc(qkv_copied, 1)

                    copy_half(0)
                    for k in range(3):
                        copy_v0(k)
                    for u in range(NU):
                        for k in copies_after(u):
                            copy_v0(k)
                        if u == 4:
                            copy_half(1)
                        if exists(l) and u >= NU - NT:
                            norm1((u - (NU - NT),))
                        if u >= 4 and u % 4 == 0:
                            copy_values(u // 4 - 1)
                        if at:
                            if u == 4:
                                norm2((0, 1, 2))
                            if u == 5:
                                norm2((3, 4))
                            for f in fill_after(u):
                                fill(f)
                    copy_values(3)
                elif at:
                    norm2(range(NT))
                if exists(l):
                    if not nx:
                        norm1(range(NT))
                if at:
                    for f in left_fill() if nx else range(NFILL):
                        fill(f)
                if exists(l):
                    for s in range(NXT):
                        eng.wait_ge(xn1T_ready, upto(l, NXT, s + 1))
                        if s == 0:
                            eng.wait_ge(qkv_ready, upto(l - 1, NQ))
                        transposed_copy((SCC, SA1)[s // 2][:, s % 2, :], xn1T, s // 2, s % 2).then_inc(xn1T_copied, 1)
                if nx:
                    exps(p, 0)
                    exps(p, 1)
                    exps(p, 2)
                    eng.wait_ge(vst_ready, upto(p, 1))
                    eng.wait_ge(pv_ready, upto(p - 1, 4))
                    act(vst[:], SA1[:, 1, 0:2 * FB].rearrange("p (k n) -> p k n", k=2), ACT.Copy).then_inc(vst_copied, 1)

            eng.wait_ge(ffn_const, 16 * NFFN)
            run(eng, iteration)

            eng.wait_ge(cdve, 2)
            act(cg[:, 1, :], cg[:, 0, :], ACT.Exp).then_inc(cact, 1)
            eng.wait_ge(chid_ready, 1)
            act(crow[:, 0], SA0[:, 0, 0:HID // 2], ACT.Copy).then_inc(crow_act, 1)
            eng.wait_ge(chid_ready, 3)
            for half in range(2):
                rows = slice(32 * half, 32 * half + 32)
                act(crow4[rows], SA1[rows, half, 0:HID // 2], ACT.Copy).then_inc(crow_act, 1)
            eng.wait_ge(cdve, CHID)
            for par in range(2):
                src = chp[:, 0].rearrange("p m (c b) -> p m c b", b=NB)[:, :, par:NCLS:2, :]
                dst = chz0[:, par].rearrange("p m (c b) -> p m c b", b=NB)[:, :, par:NCLS:2, :]
                act(dst, src, ACT.Gelu).then_inc(cact, 1)
            for e in range(3):
                src = chp[:, 1].rearrange("p m (o c b) -> p m o c b", o=2, b=NB)[:, :, :, e, :]
                dst = chz1[:, e, :, 2 * NB * e:2 * NB * e + 2 * NB].rearrange("p m (o b) -> p m o b", o=2)
                act(dst, src, ACT.Gelu).then_inc(cact, 1)

        @block.vector
        def _(eng):
            tt, ts, stt = eng.tensor_tensor, eng.tensor_scalar, eng.scalar_tensor_tensor
            eng.memset(counts[:], 0.0)
            eng.memset(rank_base[:], 0.0).then_inc(base_done, 1)

            def score(b):
                eng.wait_ge(x_loaded, upto(b, 16))
                if is_at(b, 0):
                    eng.wait_ge(tok_const, 16 * NTOKC)
                for c in range(NSC):
                    ins = eng.tensor_tensor_reduce(score_junk[:, c, :], xs[:, c, :], wtok[:], 1.0, 0.0,
                                                   ALU.mult, ALU.add, score_raw[:, c:c + 1])
                ins.then_inc(score_step, 1)
                eng.wait_ge(score_step, upto(b, 1))
                eng.wait_ge(score_stored, upto(b - 1, 16))
                eng.wait_ge(rank_step, upto(b - 1, NSC + 1))
                ts(score_col[:], score_raw[:], btok[:, 0:1], None, ALU.add).then_inc(score_done, 1)

            def rank_count(b, c):
                if c == 0:
                    eng.wait_ge(row_loaded, upto(b, 16))
                    eng.wait_ge(score_done, upto(b, 1))
                a = SC * c
                s = score_col[:, c:c + 1]
                if c >= 2:
                    eng.wait_ge(rank_step, upto(b, NSC + 1, c - 1))
                if c >= 1:
                    ts(cmp_junk[:, c % 2, 0:a], score_row[:, 0:a], s, None, ALU.is_ge, ALU.add,
                       accum_out=counts[:, 0, c:c + 1])
                ts(cmp_junk[:, c % 2, a:], score_row[:, a:], s, None, ALU.is_gt, ALU.add,
                   accum_out=counts[:, 1, c:c + 1])
                ins = stt(tie_junk[:, c % 2, :], score_row[:, a:a + SC], s, lower[:],
                          ALU.is_equal, ALU.mult, accum_out=counts[:, 2, c:c + 1])
                ins.then_inc(rank_step, 1)

            def rank(b):
                eng.wait_ge(rank_step, upto(b, NSC + 1, NSC))
                eng.tensor_reduce(rank_sum[:], counts[:].rearrange("p k c -> p c k"), AX.X, ALU.add).then_inc(rank_step, 1)
                eng.wait_ge(rank_step, upto(b, NSC + 1))
                eng.wait_ge(scattered, upto(b - 1, 16 * NSC))
                eng.wait_ge(base_done, upto(b, 1, 1))
                ts(rank_idx[:], rank_sum[:], rank_base[:, 0:1], None, ALU.add).then_inc(rank_done, 1)
                eng.wait_ge(rank_done, upto(b, 1))
                ts(rank_base[:], rank_base[:], float(NTOK), None, ALU.add).then_inc(base_done, 1)

            def norm_stats(b, which, src, step, tiles=range(NT)):
                for j in tiles:
                    ins = eng.bn_stats(stats[:, which, j, :], src[:, j, :])
                if tiles[-1] < NT - 1:
                    return
                ins.then_inc(step, 1)
                eng.wait_ge(step, upto(b, 3, 1))
                passed(eng)
                for j in range(NT):
                    ins = eng.bn_aggr(meanvar[:, which, j, :], stats[:, which, j, :])
                ins.then_inc(step, 1)
                eng.wait_ge(step, upto(b, 3, 2))
                eng.wait_ge((ln1_applied, ln2_applied)[which], upto(b - 1, NT))
                ts(vareps[:, which, :], meanvar[:, which, :, 1], EPS, None, ALU.add).then_inc(step, 1)

            def norm_mean(b, which, rstd_done, sem):
                eng.wait_ge(rstd_done, upto(b, 1))
                stt(nmean[:, which, :], meanvar[:, which, :, 0], -1.0, rstd[:, which, :],
                           ALU.mult, ALU.mult).then_inc(sem, 1)

            def centre(b, j):
                slot = (SB, SCC)[j % 2]
                psum = slot[0:TT, :, 0:384].rearrange("p k (h s) -> p k h s", s=64)
                smax_j = smax[:, j % 2, :].rearrange("p (k h) -> p k h", k=2)
                eng.wait_ge(logits_ready, upto(b, NT, j + 1))
                eng.wait_ge(centred, upto(b, NT, j - 1))
                eng.tensor_reduce(smax_j, psum, AX.X, ALU.max).then_inc(max_step, 1)
                eng.wait_ge(max_step, upto(b, NT, j + 1))
                if j >= 4:
                    eng.wait_ge(attT_ready, upto(b, NT, j - 3))
                else:
                    eng.wait_ge(attT_ready, upto(b - 1, NT))
                tt(E[:, j % 4].rearrange("p (k q) (r s) -> p k (q r) s", k=2, r=2), psum,
                   smax_j.unsqueeze(3).to_broadcast([TT, 2, 6, 64]), ALU.subtract).then_inc(centred, 1)

            def normalise(b, j):
                e = E[:, j % 4].rearrange("p q (r s) -> p (q r) s", r=2)
                eng.wait_ge(exp_done, upto(b, NT, j + 1))
                eng.wait_ge(rden_done, upto(b, NT, j - 1))
                eng.tensor_reduce(den[:, j % 2, :], e, AX.X, ALU.add).then_inc(sum_done, 1)
                eng.wait_ge(sum_done, upto(b, NT, j + 1))
                eng.wait_ge(norm_done, upto(b, NT, j - 1))
                eng.reciprocal(rden[:, j % 2, :], den[:, j % 2, :]).then_inc(rden_done, 1)
                eng.wait_ge(rden_done, upto(b, NT, j + 1))
                tt(e, e, rden[:, j % 2, :].unsqueeze(2).to_broadcast([TT, NH, 64]), ALU.mult).then_inc(norm_done, 1)

            def iteration(i):
                n, l, p = i + 3, i + 2, i + 1
                at, nx = exists(i), exists(p)
                if at:
                    normalise(i, 2)
                    centre(i, 3)
                    centre(i, 4)
                    normalise(i, 3)
                    normalise(i, 4)
                if nx:
                    k_, v_ = slice(0, 2), slice(2, 4)
                    eng.wait_ge(rest1_done, upto(p, 1))
                    eng.tensor_copy(parts[:, 1, k_, :], rest[:, k_, :]).then_inc(part2_done, 1)
                    eng.wait_ge(part1_done, upto(p, 2, 2))
                    tt(rest[:, v_, :], kvT[:, v_, :], parts[:, 0, v_, :], ALU.subtract).then_inc(rest2_done, 1)
                    eng.wait_ge(rest2_done, upto(p, 1))
                    eng.tensor_copy(parts[:, 1, v_, :], rest[:, v_, :]).then_inc(part2_done, 1)
                    eng.wait_ge(part2_done, upto(p, 2, 2))
                    tt(parts[:, 2, v_, :], rest[:, v_, :], parts[:, 1, v_, :], ALU.subtract).then_inc(part3_done, 1)
                    tt(parts[:, 2, k_, :], rest[:, k_, :], parts[:, 1, k_, :], ALU.subtract).then_inc(part3_done, 1)
                if at:
                    for n_, kb, num, tail in ((0, 1, SB, SCC), (1, 0, SA0, SA1)):
                        eng.wait_ge(pv_ready, upto(i, 4, 2 * n_ + 1))
                        tt(halves(tailv[:, kb, :]), both(tail, FB), halves(vT[:, kb, :]), ALU.mult).then_inc(tail_done, 1)
                        eng.wait_ge(tail_done, upto(i, 2, n_ + 1))
                        eng.wait_ge(pv_ready, upto(i, 4, 2 * n_ + 2))
                        eng.wait_ge(proj_ready, upto(i - 1, 2))
                        tt(halves(outT[:, kb, :]), both(num, FB), halves(tailv[:, kb, :]), ALU.add).then_inc(outT_done, 1)

                def products(u):
                    eng.wait_ge(kr_ready, upto(p, NKR, 3 * u + 2))
                    eng.wait_ge(vr_copied, upto(p, NVR, 3 * (u // 2) + 2))
                    eng.wait_ge(contracted, upto(p, NU, u - 3) if u >= 4 else upto(p - 1, NU, u + 13))
                    tt(outer[:, u % 4, 0:2, :], SA0[:, :, 0:CH], vrows[:, u // 2 % 2, 0:2, :], ALU.mult).then_inc(outer_done, 2)
                    eng.wait_ge(kr_ready, upto(p, NKR, 3 * u + 3))
                    eng.wait_ge(vr_copied, upto(p, NVR, 3 * (u // 2) + 3))
                    tt(outer[:, u % 4, 2, :], KR[2], vrows[:, u // 2 % 2, 2, :], ALU.mult).then_inc(outer_done, 1)

                if nx:
                    products(0)
                    products(1)
                if at:
                    eng.wait_ge(proj_ready, upto(i, 2, 1))
                    eng.wait_ge(hR_loaded, upto(i, 16))
                    eng.wait_ge(h1b_done, upto(i - 1, 1))
                    eng.wait_ge(ln2_applied, upto(i - 1, NT))
                    eng.wait_ge(cls_stored, upto(i - 1, 16))
                    tt(h1[:, 0:4, :].rearrange("p (k j) d -> p k (j d)", k=2), SB[0:TT, :, 0:2 * D],
                       hR[:, 0:4, :].rearrange("p (k j) d -> p k (j d)", k=2), ALU.add).then_inc(residual_done, 1)
                    eng.wait_ge(proj_ready, upto(i, 2, 2))
                    tt(h1[:, 4, :], SCC[0:TT, 1, 0:D], hR[:, 4, :], ALU.add).then_inc(residual_done, 1)
                if not nx:
                    if at:
                        eng.wait_ge(residual_done, upto(i, 2))
                        norm_stats(i, 1, h1, ln_stats2)
                        norm_mean(i, 1, rstd2_done, nmean2_done)
                    if exists(l):
                        eng.wait_ge(hA_loaded, upto(l, 16))
                        norm_stats(l, 0, hA, ln_stats1)
                        norm_mean(l, 0, rstd1_done, nmean1_done)
                    if exists(n):
                        score(n)
                if nx:
                    for u in range(2, NU):
                        products(u)
                        if at:
                            if u == 2:
                                eng.wait_ge(residual_done, upto(i, 2))
                                norm_stats(i, 1, h1, ln_stats2, (0, 1, 2))
                            if u == 3:
                                norm_stats(i, 1, h1, ln_stats2, (3, 4))
                            if u == 4:
                                norm_mean(i, 1, rstd2_done, nmean2_done)
                        if exists(n) and u == 7:
                            score(n)
                        if exists(l):
                            if u == 9:
                                eng.wait_ge(hA_loaded, upto(l, 16))
                                norm_stats(l, 0, hA, ln_stats1, (0, 1, 2))
                            if u == 10:
                                norm_stats(l, 0, hA, ln_stats1, (3, 4))
                            if u == 11:
                                norm_mean(l, 0, rstd1_done, nmean1_done)
                        if exists(n) and u >= NU - RANKED:
                            rank_count(n, u - (NU - RANKED))
                if nx:
                    eng.wait_ge(kset_step, upto(p, 6))
                    eng.wait_ge(logits_ready, upto(p - 1, NT))
                    if is_at(p, 0):
                        eng.wait_ge(att_const, 16 * NATT)
                    for q in range(3):
                        rows = slice(32 * q, 32 * q + 32)
                        for par in range(2):
                            ins = ts(kbd[0:32, q:q + 4:3, 64 * par:64 * par + NSET], ksets[rows, :, 0:NSET],
                                     parity[rows, par:par + 1], None, ALU.mult)
                    ins.then_inc(kbd_done, 1)
                if exists(n):
                    for c in range(RANKED if nx else 0, RANKED2):
                        rank_count(n, c)
                if nx:
                    centre(p, 0)
                    centre(p, 1)
                if exists(n):
                    for c in range(RANKED2, NSC):
                        rank_count(n, c)
                    rank(n)
                if nx:
                    eng.wait_ge(vset_step, upto(p, 6))
                    eng.wait_ge(vst_ready, upto(p - 1, 1))
                    for par in range(2):
                        ins = ts(vexp[:, :, par, 0:NSET], vsets[:, :, 0:NSET], parity[:, par:par + 1], None, ALU.mult)
                    ins.then_inc(vexp_done, 1)
                    normalise(p, 0)
                    centre(p, 2)
                    normalise(p, 1)
                if at:
                    eng.wait_ge(h1b_done, upto(i, 1))
                    eng.wait_ge(out_stored, upto(i - 1, 16 * 2))
                    eng.wait_ge(ffn2_ready, upto(i, 2, 1))
                    tt(osb[:, 0:4, :].rearrange("p (k j) d -> p k (j d)", k=2), SA0[0:TT, :, 0:2 * D],
                                h1b[:, 0:4, :].rearrange("p (k j) d -> p k (j d)", k=2), ALU.add).then_inc(added, 1)
                    eng.wait_ge(ffn2_ready, upto(i, 2, 2))
                    tt(osb[:, 4, :], SA1[0:TT, 0, 0:D], h1b[:, 4, :], ALU.add).then_inc(added, 1)

            eng.wait_ge(pool_const, NPOOL)
            run(eng, iteration)

            count = [0]

            def step(ins):
                ins.then_inc(cdve, 1)
                count[0] += 1
                eng.wait_ge(cdve, count[0])

            eng.wait_ge(cgate_ready, 1)
            eng.wait_ge(cls_const, 16 * NCC)
            gl = cg[:, 2, :]
            ins = tt(cgs[:], SCC[0:48, 1, 0:2 * NCLS].rearrange("p (c o) -> p c o", o=2), pick[:], ALU.mult)
            ins.then_inc(cgs_done, 1)
            eng.wait_ge(cgs_done, 1)
            eng.tensor_reduce(gl, cgs[:].rearrange("p c o -> p o c"), AX.X, ALU.add).then_inc(cgs_done, 1)
            eng.wait_ge(cgs_done, 2)
            step(eng.tensor_reduce(cg[:, 3, 0:1], gl, AX.X, ALU.max))
            step(ts(cg[:, 0, :], gl, cg[:, 3, 0:1], None, ALU.subtract))
            eng.wait_ge(chid_ready, 2)
            eng.tensor_copy(crow[:, 1], SA0[:, 1, 0:HID // 2]).then_inc(crow_dve, 1)
            for a in range(5):
                pair = 0 if a < 3 else 1
                n_ = 2 * NB if pair == 0 else 3 * NB
                at_ = n_ * (a if pair == 0 else a - 3)
                if a in (0, 4):
                    eng.wait_ge(chidT_ready, 1 if a == 0 else 2)
                if a < 4:
                    hp = SB[:, :, 0:3 * 128].rearrange("p k (m c) -> p k m c", m=3)[:, :, :, 32 * a + COFF[a]:32 * a + COFF[a] + n_]
                else:
                    hp = SCC[:, 0, 0:3 * 64].rearrange("p (m k c) -> p k m c", m=3, k=2)[:, :, :, COFF[a]:COFF[a] + n_]
                step(tt(chp[:, pair, :, at_:at_ + n_].rearrange("p (k m) c -> p k m c", k=2), hp,
                        a1bs[:, a, :].rearrange("p (k m) -> p k m", k=2).unsqueeze(3).to_broadcast([128, 2, 3, n_]), ALU.add))
            assert count[0] == CHID
            eng.wait_ge(cact, 1)
            e = cg[:, 1, :]
            step(eng.tensor_reduce(cg[:, 4, 0:1], e, AX.X, ALU.add))
            step(eng.reciprocal(cg[:, 4, 1:2], cg[:, 4, 0:1]))
            step(ts(cg[:, 5, :], e, cg[:, 4, 1:2], None, ALU.mult))
            step(eng.tensor_reduce(cg[:, 6, 0:1], cg[:, 5, :], AX.X, ALU.min))
            step(stt(cg[:, 7, :], cg[:, 5, :], cg[:, 6, 0:1], cg[:, 5, :], ALU.is_gt, ALU.mult))
            step(eng.tensor_reduce(cg[:, 8, 0:1], cg[:, 7, :], AX.X, ALU.add))
            step(ts(cg[:, 8, 1:2], cg[:, 8, 0:1], 1e-6, None, ALU.max))
            step(eng.reciprocal(cg[:, 9, 0:1], cg[:, 8, 1:2]))
            step(ts(cg[:, 10, :], cg[:, 7, :], cg[:, 9, 0:1], None, ALU.mult))
            eng.wait_ge(cout_ready, 1)
            eng.wait_ge(cls_io, 16)
            step(eng.tensor_copy(c0[:], SA0[64:112, 1, 0:D]))
            step(stt(cres[:], SA0[0:48, 0, 0:D], cg[:, 10, 0:1], cres[:], ALU.mult, ALU.add))
            step(stt(c0[:], c0[:], cg[:, 10, 1:2], cres[:], ALU.mult, ALU.add))
            assert count[0] == CDVE

        @block.gpsimd
        def _(eng):
            eng.memset(wbil[:], 0.0).then_inc(pool_const, 1)
            eng.memset(neghalf[:], -0.5)
            for t_ in (xn1T, xn2T, ET):
                eng.memset(t_[:, :, T:TP], 0.0)
            eng.memset(vexp[:], 0.0)
            eng.memset(kbd[0:32, :, :], 0.0)
            eng.memset(chz0[:], 0.0)
            eng.memset(chz1[:], 0.0).then_inc(pool_const, 1)

            def running_sums(b, buf, step):
                w = 1
                k = 0
                while w < BLK:
                    v = buf.rearrange("p k (n t) -> p (k n) t", t=2 * w)
                    if k:
                        eng.wait_ge(step, upto(b, 4, k))
                    last = v[:, :, w - 1:w].to_broadcast([FB, 2 * TP // (2 * w), w]) if w > 1 else v[:, :, 0:1]
                    eng.tensor_tensor(v[:, :, w:2 * w], v[:, :, w:2 * w], last, ALU.add).then_inc(step, 1)
                    w, k = 2 * w, k + 1

            def set_sums(b, buf, sets, step):
                full = buf.rearrange("p k (n t) -> p k n t", t=BLK)
                passed(eng)
                eng.tensor_copy(sets[:, :, 0:32], full[:, :, 0:32, BLK - 1]).then_inc(step, 1)
                at, n = 0, 32
                for k in range(1, 6):
                    eng.wait_ge(step, upto(b, 6, k))
                    eng.tensor_tensor(sets[:, :, at + n:at + n + n // 2], sets[:, :, at:at + n:2],
                                              sets[:, :, at + 1:at + n:2], ALU.add).then_inc(step, 1)
                    at, n = at + n, n // 2

            def scatter(b):
                eng.wait_ge(rank_done, upto(b, 1))
                passed(eng)
                for c in range(NSC):
                    eng.indirect_dma_start(
                        sorted_dram, bass.IndirectOffsetOnAxis(ap=rank_idx[:, c:c + 1], axis=0),
                        xs[:, c, :], None).then_inc(scattered, 16)

            def inv_root(b, which, stats_done, sem):
                eng.wait_ge(stats_done, upto(b, 3))
                eng.wait_ge((nmean1_done, nmean2_done)[which], upto(b - 1, 1))
                eng.wait_ge((ln1_applied, ln2_applied)[which], upto(b - 1, NT))
                eng.tensor_tensor(rstd[:, which, :], vareps[:, which, :], neghalf[:], ALU.pow).then_inc(sem, 1)

            def iteration(i):
                n, l, p = i + 3, i + 2, i + 1
                at, nx = exists(i), exists(p)
                if nx:
                    eng.wait_ge(part1_done, upto(p, 2, 1))
                    eng.tensor_tensor(rest[:, 0:2, :], kvT[:, 0:2, :], parts[:, 0, 0:2, :], ALU.subtract).then_inc(rest1_done, 1)
                    if is_at(p, 0):
                        scatter(1)
                    eng.wait_ge(rest1_done, upto(p, 1))
                    running_sums(p, kvT[:, 0:2, :], kprefix)
                    eng.wait_ge(kprefix, upto(p, 4))
                    eng.wait_ge(kbd_done, upto(p - 1, 1))
                    set_sums(p, kvT[:, 0:2, :], ksets, kset_step)
                if at:
                    inv_root(i, 1, ln_stats2, rstd2_done)
                    eng.wait_ge(residual_done, upto(i, 2))
                    eng.wait_ge(added, upto(i - 1, 2))
                    eng.tensor_tensor(h1b[:], h1[:], b2row[:].unsqueeze(1).to_broadcast([TT, NT, D]), ALU.add).then_inc(h1b_done, 1)
                if nx:
                    eng.wait_ge(qkv_copied, upto(p, NQ))
                    eng.wait_ge(qk_placed, upto(p - 1, 16 * 3))
                    eng.tensor_tensor(qkT[:], qT[:], kvT[:, 0:2, :], ALU.mult).then_inc(qk_done, 1)
                if exists(l):
                    inv_root(l, 0, ln_stats1, rstd1_done)
                if nx:
                    eng.wait_ge(v_copied, upto(p, 4))
                    running_sums(p, vT[:], vprefix)
                    eng.wait_ge(vprefix, upto(p, 4))
                    eng.wait_ge(vexp_done, upto(p - 1, 1))
                    set_sums(p, vT[:], vsets, vset_step)
                if exists(n) and not is_at(n, 1):
                    scatter(n)

            eng.wait_ge(ffn_const, 16 * NFFN)
            run(eng, iteration)

            eng.wait_ge(cx_copied, upto(NB - 1, 1))
            for par in range(2):
                eng.tensor_copy(cxp[:, :, par], cx[:, :, par:NCLS:2, :]).then_inc(cxp_done, 1)


def constants():
    import numpy as np
    one = 0x3F80
    r = np.arange(128)
    krep = np.zeros((FB, 2, 2, 128), np.uint16)
    vrep = np.zeros((FB, 2, 128), np.uint16)
    for part in range(3):
        for par in range(2):
            for e in range(HS):
                row = 3 * (16 * par + e) + part
                vrep[row, par, r % 16 == e] = one
                for half in range(2):
                    krep[row, par, half, 8 * half + r // 16 == e] = one
    kbd = np.zeros((64, 6, 2, 64), np.float32)
    for par in range(2):
        kbd[16 * par:16 * par + 16, :, par, NSET] = 1
    ends, length = [], 1
    while length <= 32:
        ends += [(k + 1) * length for k in range(32 // length)]
        length *= 2
    assert len(ends) == NSET
    for b in range(32):
        kbd[32 + b, :, :, :NSET] = np.where(np.array(ends) > b, NEG, 0)
    onehot = np.zeros((32, 6, TP), np.float32)
    for t in range(T):
        if (t + 1) // BLK < 32:
            onehot[(t + 1) // BLK, :, t] = 1
    parity = np.zeros((FB, 2), np.float32)
    for row in range(FB):
        parity[row, row // 16 % 2] = 1
    tail = np.zeros((128, 32), np.float32)
    for par in range(2):
        tail[64 * par + NSET, 16 * par:16 * par + 16] = 1
    lower = (np.arange(SC)[None, :] < np.arange(SC)[:, None]).astype(np.uint16) * np.uint16(one)
    pick = np.zeros((48, NCLS, 2), np.float32)
    cls = np.zeros((5, 2, 48), np.float32)
    for row in range(48):
        c = row // NB
        pick[row, c] = 1
        cls[3 + c % 2, 0, row] = 1
        cls[c // 2, 1, row] = 1
    return {"c_ident": np.eye(128, dtype=np.float32), "c_krep": krep, "c_vrep": vrep,
            "c_kbd": kbd.reshape(64, 6, 128), "c_onehot": onehot, "c_parity": parity,
            "c_tail": tail, "c_lower": lower, "c_pick": pick, "c_cls": cls}


def layout(inp):
    import numpy as np
    f = {k: np.asarray(v) for k, v in inp.items()}
    ct = np.ascontiguousarray
    return {
        "x": f["x"], "tok_w": ct(f["L0_tok_w"].reshape(D)), "tok_b": f["L0_tok_b"],
        "wqkvT": ct(f["L0_attn_Wqkv"].T), "wprojT": ct(f["L0_attn_Wproj"].T),
        "wvT": ct(f["L0_attn_Wv"].T), "bv96": ct(np.tile(f["L0_attn_bv"], FB // HS).reshape(FB, 1)),
        "w1": f["L0_ffn_moe0_W1"], "b1c": ct(f["L0_ffn_moe0_b1"].reshape(NM, 128).T),
        "w2": f["L0_ffn_moe0_W2"], "b2": f["L0_ffn_moe0_b2"],
        "a1": f["L0_ffn_A1_W"], "a1bc": ct(f["L0_ffn_A1_b"].reshape(5, NM, 128).transpose(2, 0, 1)),
        "a2": f["L0_ffn_A2_W"], "a2b": f["L0_ffn_A2_b"], "gw": ct(f["L0_ffn_G_W"].reshape(NCLS, 2, FB, 2).transpose(2, 1, 0, 3)),
        **constants(),
    }


def kernel(**inputs):
    import concourse.bacc as bacc
    from concourse.bass_utils import run_bass_kernel_spmd

    nc = bacc.Bacc("TRN2", target_bir_lowering=False, num_devices=1)
    arrays = layout(inputs)
    aps = [nc.dram_tensor(name, list(a.shape), mybir.dt.from_np(a.dtype), kind="ExternalInput").ap()
           for name, a in arrays.items()]
    out = nc.dram_tensor("out", [NB, T, D], F32, kind="ExternalOutput").ap()
    build(nc, *aps, out)
    r = run_bass_kernel_spmd(nc, [arrays], core_ids=[0])
    return r.results[0]["out"]
```
